# Optimizing a Trainium2 kernel written in Bass

```python
import numpy as np
import jax
import jax.numpy as jnp

def _softmax(x, axis=-1):
    return jax.nn.softmax(x, axis=axis)

def _gelu(x):
    return jax.nn.gelu(x, approximate=True)

def _silu(x):
    return jax.nn.silu(x)

def _sigmoid(x):
    return jax.nn.sigmoid(x)

def _layernorm(x, axis=-1, eps=1e-05):
    m = jnp.mean(x, axis=axis, keepdims=True)
    v = jnp.var(x, axis=axis, keepdims=True)
    return (x - m) / jnp.sqrt(v + eps)

def _scatter_add(tgt, idx, src, axis=0):
    return tgt.at[idx].add(src)

def _segment_sum(src, seg, n):
    return jax.ops.segment_sum(src, seg, n)
kernel_name = 'mk_decoder_preln_d1_seqx_r4_b41b0b'

def setup_inputs(seed: int=0):
    np.random.seed(seed)
    _w = jnp.asarray

    def _rec_inputs():
        import jax
        import jax.numpy as jnp
        _rk = jax.random.key(seed)
        x = 7.22e-05 + 1 * jax.random.normal(jax.random.fold_in(_rk, 1), (2, 512, 512), jnp.float32)
        _lenS = 512 - jax.random.randint(jax.random.fold_in(_rk, 7), (2,), 0, max(1, 512 // 4) + 1, jnp.int32)
        _lenS2 = 1024 - jax.random.randint(jax.random.fold_in(_rk, 8), (2,), 0, max(1, 1024 // 4) + 1, jnp.int32)
        _ctx_2048P = jax.random.normal(jax.random.fold_in(_rk, 11), (2, 16, 512), jnp.float32)
        _ctx_2048c = jax.random.dirichlet(jax.random.fold_in(_rk, 511), 0.3 * jnp.ones((16,), jnp.float32), (2, 1024))
        _ctx_2048t = jnp.einsum('bsk,bkd->bsd', _ctx_2048c, _ctx_2048P)
        _ctx_2048t = _ctx_2048t * jax.lax.rsqrt(jnp.mean(jnp.square(_ctx_2048t)) + 1e-12) * 0.953939
        ctx_2048 = -0.000514642 + 1.00011 * (_ctx_2048t + 0.3 * jax.random.normal(jax.random.fold_in(_rk, 611), (2, 1024, 512), jnp.float32))
        return (x, ctx_2048)
    x, ctx_2048 = _rec_inputs()

    def _L0_attn_setup():
        import jax, jax.numpy as jnp
        import numpy as np
        B, T, HID = (1, 512, 512)
        H = 16
        D = HID // H
        EPS = 1e-05

        def _layer_norm(x, eps=1e-05):
            mu = jnp.mean(x, axis=-1, keepdims=True)
            var = jnp.mean((x - mu) ** 2, axis=-1, keepdims=True)
            return (x - mu) * jax.lax.rsqrt(var + eps)

        def _feature_map(x, gamma, beta):
            return _layer_norm(x * gamma + beta)
        key = jax.random.key(seed)
        ks = jax.random.split(key, 8)
        s = HID ** (-0.5)
        return {'hidden_states': jax.random.normal(ks[0], (B, T, HID), jnp.float32), 'Wq': jax.random.normal(ks[1], (HID, HID), jnp.float32) * s, 'Wk': jax.random.normal(ks[2], (HID, HID), jnp.float32) * s, 'Wv': jax.random.normal(ks[3], (HID, HID), jnp.float32) * s, 'Wo': jax.random.normal(ks[4], (HID, HID), jnp.float32) * s, 'gamma': 1.0 + 0.1 * jax.random.normal(ks[5], (D,), jnp.float32), 'beta': 0.1 * jax.random.normal(ks[6], (D,), jnp.float32)}
    _L0_attn_all = _L0_attn_setup()
    _L0_attn_in = {k: v for k, v in _L0_attn_all.items() if k in ('Wq', 'Wk', 'Wv', 'Wo', 'gamma', 'beta')}
    del _L0_attn_all

    def _L0_xattn_setup():
        import jax, jax.numpy as jnp
        import numpy as np
        D_MODEL = 512
        NUM_HEADS = 16
        HEAD_DIM = D_MODEL // NUM_HEADS

        def _fq_sym(x, axis):
            s = jnp.max(jnp.abs(x), axis=axis, keepdims=True) / 127.0
            s = jnp.maximum(s, 1e-08)
            q = jnp.clip(jnp.round(x / s), -127.0, 127.0) * s
            return x + jax.lax.stop_gradient(q - x)

        def _fq_unsigned(x, axis):
            s = jnp.max(x, axis=axis, keepdims=True) / 255.0
            s = jnp.maximum(s, 1e-08)
            q = jnp.clip(jnp.round(x / s), 0.0, 255.0) * s
            return x + jax.lax.stop_gradient(q - x)
        key = jax.random.key(seed)
        ks = jax.random.split(key, 8)
        B, N, M, C = (2, 512, 128, D_MODEL)
        return {'x': jax.random.normal(ks[0], (B, N, C), jnp.float32), 'cond': jax.random.normal(ks[1], (B, M, C), jnp.float32), 'Wq': jax.random.normal(ks[2], (C, C), jnp.float32) * 0.02, 'bq': jnp.zeros((C,), jnp.float32), 'Wkv': jax.random.normal(ks[3], (C, 2 * C), jnp.float32) * 0.02, 'bkv': jnp.zeros((2 * C,), jnp.float32), 'Wp': jax.random.normal(ks[4], (C, C), jnp.float32) * 0.02, 'bp': jnp.zeros((C,), jnp.float32)}
    _L0_xattn_all = _L0_xattn_setup()
    _L0_xattn_in = {k: v for k, v in _L0_xattn_all.items() if k in ('Wq', 'bq', 'Wkv', 'bkv', 'Wp', 'bp')}
    del _L0_xattn_all

    def _L0_ffn_setup():
        import jax, jax.numpy as jnp
        import numpy as np
        E = 8
        K = 2
        C = 512
        I = 352
        IS = I * 2
        B, T = (2, 512)
        key = jax.random.key(seed)
        ks = jax.random.split(key, 9)
        s = 0.02
        return {'x': jax.random.normal(ks[0], (B, T, C), dtype=jnp.float32), 'gate_w': jax.random.normal(ks[1], (E, C), dtype=jnp.float32) * s, 'w1': jax.random.normal(ks[2], (E, I, C), dtype=jnp.float32) * s, 'w2': jax.random.normal(ks[3], (E, I, C), dtype=jnp.float32) * s, 'w3': jax.random.normal(ks[4], (E, C, I), dtype=jnp.float32) * s, 'sw1': jax.random.normal(ks[5], (IS, C), dtype=jnp.float32) * s, 'sw2': jax.random.normal(ks[6], (IS, C), dtype=jnp.float32) * s, 'sw3': jax.random.normal(ks[7], (C, IS), dtype=jnp.float32) * s}
    _L0_ffn_all = _L0_ffn_setup()
    _L0_ffn_in = {k: v for k, v in _L0_ffn_all.items() if k in ('gate_w', 'w1', 'w2', 'w3', 'sw1', 'sw2', 'sw3')}
    del _L0_ffn_all
    return {'x': x, 'ctx_2048': ctx_2048, 'L0_attn_Wq': _L0_attn_in['Wq'], 'L0_attn_Wk': _L0_attn_in['Wk'], 'L0_attn_Wv': _L0_attn_in['Wv'], 'L0_attn_Wo': _L0_attn_in['Wo'], 'L0_attn_gamma': _L0_attn_in['gamma'], 'L0_attn_beta': _L0_attn_in['beta'], 'L0_xattn_Wq': _L0_xattn_in['Wq'], 'L0_xattn_bq': _L0_xattn_in['bq'], 'L0_xattn_Wkv': _L0_xattn_in['Wkv'], 'L0_xattn_bkv': _L0_xattn_in['bkv'], 'L0_xattn_Wp': _L0_xattn_in['Wp'], 'L0_xattn_bp': _L0_xattn_in['bp'], 'L0_ffn_gate_w': _L0_ffn_in['gate_w'], 'L0_ffn_w1': _L0_ffn_in['w1'], 'L0_ffn_w2': _L0_ffn_in['w2'], 'L0_ffn_w3': _L0_ffn_in['w3'], 'L0_ffn_sw1': _L0_ffn_in['sw1'], 'L0_ffn_sw2': _L0_ffn_in['sw2'], 'L0_ffn_sw3': _L0_ffn_in['sw3']}

def reference(x, ctx_2048, L0_attn_Wq, L0_attn_Wk, L0_attn_Wv, L0_attn_Wo, L0_attn_gamma, L0_attn_beta, L0_xattn_Wq, L0_xattn_bq, L0_xattn_Wkv, L0_xattn_bkv, L0_xattn_Wp, L0_xattn_bp, L0_ffn_gate_w, L0_ffn_w1, L0_ffn_w2, L0_ffn_w3, L0_ffn_sw1, L0_ffn_sw2, L0_ffn_sw3):
    import jax
    import jax.numpy as jnp

    def _L0_attn_ref(hidden_states, Wq, Wk, Wv, Wo, gamma, beta):
        import jax, jax.numpy as jnp
        import numpy as np
        B, T, HID = (1, 512, 512)
        H = 16
        D = HID // H
        EPS = 1e-05

        def _layer_norm(x, eps=1e-05):
            mu = jnp.mean(x, axis=-1, keepdims=True)
            var = jnp.mean((x - mu) ** 2, axis=-1, keepdims=True)
            return (x - mu) * jax.lax.rsqrt(var + eps)

        def _feature_map(x, gamma, beta):
            return _layer_norm(x * gamma + beta)
        b, t, _ = hidden_states.shape
        q = (hidden_states @ Wq.T).reshape(b, t, H, D)
        k = (hidden_states @ Wk.T).reshape(b, t, H, D)
        v = (hidden_states @ Wv.T).reshape(b, t, H, D)
        q = _feature_map(q, gamma, beta)
        k = _feature_map(k, gamma, beta)
        q = q * D ** (-0.5)
        attn = jnp.einsum('bqhd,bkhd->bhqk', q, k) ** 2
        mask = jnp.tril(jnp.ones((t, t), dtype=bool))
        attn = jnp.where(mask, attn, 0.0)
        o = jnp.einsum('bhqk,bkhd->bqhd', attn, v)
        z = jnp.sum(attn, axis=-1)
        o = o / (jnp.swapaxes(z, 1, 2)[..., None] + EPS)
        o = o.reshape(b, t, H * D)
        return o @ Wo.T

    def _L0_xattn_ref(x, cond, Wq, bq, Wkv, bkv, Wp, bp):
        import jax, jax.numpy as jnp
        import numpy as np
        D_MODEL = 512
        NUM_HEADS = 16
        HEAD_DIM = D_MODEL // NUM_HEADS

        def _fq_sym(x, axis):
            s = jnp.max(jnp.abs(x), axis=axis, keepdims=True) / 127.0
            s = jnp.maximum(s, 1e-08)
            q = jnp.clip(jnp.round(x / s), -127.0, 127.0) * s
            return x + jax.lax.stop_gradient(q - x)

        def _fq_unsigned(x, axis):
            s = jnp.max(x, axis=axis, keepdims=True) / 255.0
            s = jnp.maximum(s, 1e-08)
            q = jnp.clip(jnp.round(x / s), 0.0, 255.0) * s
            return x + jax.lax.stop_gradient(q - x)
        B, N, C = x.shape
        H, hd = (NUM_HEADS, HEAD_DIM)
        q = (x @ Wq + bq).reshape(1, B * N, H, hd)
        kv = (cond @ Wkv + bkv).reshape(1, -1, 2, H, hd)
        k, v = (kv[:, :, 0], kv[:, :, 1])
        scale = 1.0 / np.sqrt(hd).astype(np.float32)
        q = jnp.transpose(q * scale, (0, 2, 1, 3))
        k = jnp.transpose(k, (0, 2, 1, 3))
        v = jnp.transpose(v, (0, 2, 1, 3))
        q = _fq_sym(q, axis=-1)
        k = _fq_sym(k, axis=-1)
        v = _fq_sym(v, axis=2)
        attn = jnp.einsum('bhqd,bhkd->bhqk', q, k)
        attn = jax.nn.softmax(attn.astype(jnp.float32), axis=-1)
        attn = _fq_unsigned(attn, axis=-1)
        out = jnp.einsum('bhqk,bhkd->bhqd', attn, v)
        out = jnp.transpose(out, (0, 2, 1, 3)).reshape(B, N, C)
        return out @ Wp + bp

    def _L0_ffn_ref(x, gate_w, w1, w2, w3, sw1, sw2, sw3):
        import jax, jax.numpy as jnp
        import numpy as np
        E = 8
        K = 2
        C = 512
        I = 352
        IS = I * 2
        B, T = (2, 512)
        Bq, Tq, Cq = x.shape
        xf = x.reshape(-1, Cq)
        logits = xf @ gate_w.T
        probs = jax.nn.softmax(logits.astype(jnp.float32), axis=-1)
        topk_p, topk_i = jax.lax.top_k(probs, K)
        comb = (jax.nn.one_hot(topk_i, E, dtype=jnp.float32) * topk_p[..., None]).sum(axis=1).astype(x.dtype)
        h1 = jnp.einsum('nc,eic->eni', xf, w1)
        h2 = jnp.einsum('nc,eic->eni', xf, w2)
        h = jax.nn.silu(h1) * h2
        eo = jnp.einsum('eni,eci->enc', h, w3)
        y = jnp.einsum('enc,ne->nc', eo, comb).reshape(Bq, Tq, Cq)
        sh = jax.nn.silu(xf @ sw1.T) * (xf @ sw2.T) @ sw3.T
        return y + sh.reshape(Bq, Tq, Cq)
    x = x + _L0_attn_ref(_layernorm(x, axis=-1), L0_attn_Wq, L0_attn_Wk, L0_attn_Wv, L0_attn_Wo, L0_attn_gamma, L0_attn_beta)
    x = x + _L0_xattn_ref(_layernorm(x, axis=-1), ctx_2048, L0_xattn_Wq, L0_xattn_bq, L0_xattn_Wkv, L0_xattn_bkv, L0_xattn_Wp, L0_xattn_bp)
    x = x + _L0_ffn_ref(_layernorm(x, axis=-1), L0_ffn_gate_w, L0_ffn_w1, L0_ffn_w2, L0_ffn_w3, L0_ffn_sw1, L0_ffn_sw2, L0_ffn_sw3)
    return x

_drawn_inputs = setup_inputs


def setup_inputs(seed=0):
    import zlib

    import numpy as np

    out = dict(_drawn_inputs(seed))
    spreads = {'L0_xattn_bq': (0.0, 0.8), 'L0_xattn_bkv': (0.0, 0.1), 'L0_xattn_bp': (0.0, 0.1)}
    factors = {'L0_xattn_Wq': 7.973,
     'L0_ffn_gate_w': 5.63,
     'L0_ffn_w1': 4.838,
     'L0_ffn_w2': 4.734,
     'L0_ffn_w3': 4.749,
     'L0_ffn_sw1': 4.129,
     'L0_ffn_sw2': 4.053,
     'L0_ffn_sw3': 4.039}
    for name, (base, spread) in spreads.items():
        noise = np.random.default_rng([zlib.crc32(name.encode()), seed]).standard_normal(out[name].shape)
        drawn = base * np.exp(spread * noise) if base else spread * noise
        out[name] = jnp.asarray(drawn.astype(out[name].dtype))
    for name, factor in factors.items():
        out[name] = (out[name] * factor).astype(out[name].dtype)
    return out
```

```python
from contextlib import ExitStack

import concourse.bass as bass
from concourse import mybir

F32 = mybir.dt.float32
F32R = mybir.dt.float32r
F16 = mybir.dt.float16
BF16 = mybir.dt.bfloat16
I16 = mybir.dt.int16
ALU = mybir.AluOpType
ACT = mybir.ActivationFunctionType
AX_X = mybir.AxisListType.X
ABSMAX = bass.bass_isa.ReduceOp.absmax

P = 128
B, S, C = 2, 512, 512
TOKENS = B * S
TT = TOKENS // P
H, D = 16, 32
CK = C // P
HG = C // P
GH = P // D
BT = S // P
KEYS = 2 * 1024
KT = KEYS // P
LN_EPS = 1e-05
ATT_EPS = 1e-05
MAGIC = 12582912.0
QMAX = 127.0
PMAX = 255.0
Q_FLOOR = 1e-08


def row_halves(ap, n):
    return ap.rearrange("p (n w) -> p n w", n=n)
def constants(nc, ctx):
    def sb(name, shape, dt):
        return ctx.enter_context(nc.sbuf_tensor(name, shape, dt))

    x_res = sb("x_res", [P, TT, C], F32)
    ident = sb("ident", [P, P], F32)
    ident16 = sb("ident16", [P, P], F16)
    ident_bf = sb("ident_bf", [P, P], BF16)
    mask = sb("mask", [P, P], F32)
    minus_half = sb("minus_half", [P, 2 * H], F32)
    made = ctx.enter_context(nc.semaphore("const_made"))
    with nc.Block(no_gpsimd_drain=True) as block:
        @block.gpsimd
        def _(pool):
            nc.gpsimd.memset(minus_half[:, :], -0.5)
            nc.gpsimd.memset(ident[:, :], 0.0).then_inc(made, 1)
            nc.gpsimd.memset(mask[:, :], 1.0).then_inc(made, 1)
            pool.wait_ge(made, 2)
            nc.gpsimd.affine_select(out=ident[:, :], in_=ident[:, :], compare_op=ALU.not_equal, fill=1.0, base=0,
                                    pattern=[[-1, P]], channel_multiplier=1).then_inc(made, 1)
            nc.gpsimd.affine_select(out=mask[:, :], in_=mask[:, :], compare_op=ALU.is_ge, fill=0.0, base=0,
                                    pattern=[[1, P]], channel_multiplier=-1).then_inc(made, 1)
            pool.wait_ge(made, 4)
            nc.gpsimd.tensor_copy(ident16[:, :], ident[:, :]).then_inc(made, 1)
            nc.gpsimd.tensor_copy(ident_bf[:, :], ident[:, :]).then_inc(made, 1)
            pool.wait_ge(made, 6)
    return x_res, (ident, mask, minus_half, ident16, ident_bf)
TURNS = [("z", 0), ("z", 1), ("z", 2), ("q", 0), ("k", 0), ("z", 3), ("q", 1), ("k", 1), ("q", 2), ("k", 2), ("q", 3), ("k", 3)]


def turn_bank(what, t):
    return TURNS.index((what, t)) % 2


def self_attention(nc, x_dram, w_dram, gamma_dram, beta_dram, x_res, ident, mask, minus_half):
    with ExitStack() as ctx:
        def sb(name, shape, dt):
            return ctx.enter_context(nc.sbuf_tensor(name, shape, dt))

        def psum(name, shape, dt):
            return ctx.enter_context(nc.psum_tensor(name, shape, dt))

        def sem(name):
            return ctx.enter_context(nc.semaphore("sa_" + name))

        w_hi = sb("sa_w_hi", [P, 4, CK, C], F32R)
        w_lo = sb("sa_w_lo", [P, 4, CK, C], F32R)
        att = sb("sa_att", [P, BT, GH, S], F32)
        w_raw = att[:, :, :, :]
        gam = sb("sa_gam", [P, C], F32)
        bet = sb("sa_bet", [P, C], F32)
        stats = sb("sa_stats", [P, 2, 6], F32)
        mv = sb("sa_mv", [P, TT, 2], F32)
        ve = sb("sa_ve", [P, TT], F32)
        rstd = sb("sa_rstd", [P, TT], F32)
        z = sb("sa_z", [P, 2, C], F32)
        z_hi = sb("sa_z_hi", [P, 2, CK, P], F32R)
        z_lo = sb("sa_z_lo", [P, 2, CK, P], F32R)
        y = sb("sa_y", [P, 2, 2 * H, D], F32)
        sq = sb("sa_sq", [P, 2, 2 * H, D], F32)
        msum = sb("sa_msum", [P, 2, 2 * H], F32)
        vsum = sb("sa_vsum", [P, 2, 2 * H], F32)
        rsq = sb("sa_rsq", [P, 2, 2 * H], F32)
        qT = sb("sa_qT", [P, HG, S], F32)
        kT = sb("sa_kT", [P, HG, S], F32)
        v = sb("sa_v", [P, BT, C], F32)
        ones = sb("sa_ones", [P, D], F32)
        rec = sb("sa_rec", [P, S], F32)
        oT_hi = sb("sa_oT_hi", [P, HG, S], F32R)
        oT_lo = sb("sa_oT_lo", [P, HG, S], F32R)
        o32 = sb("sa_o32", [P, S], F32)

        tb = [psum(f"sa_tb{i}", [P, 512], F32) for i in range(2)]
        pj = [psum(f"sa_pj{i}", [P, 512], F32) for i in range(2)]
        sc = [psum(f"sa_sc{i}", [P, 512], F32) for i in range(GH)]
        nd = [(pj[0], pj[1]), (tb[0], tb[1])]

        x_in = [sem(f"x_in{b}") for b in range(B)]
        gb_in = sem("gb_in")
        w_in = [sem(f"w_in{m}") for m in range(4)]
        w_hi_ok = sem("w_hi_ok")
        w_split = sem("w_split")
        ones_ok = sem("ones_ok")
        dve = sem("dve")
        ve_ok = sem("ve_ok")
        rstd_ok = sem("rstd_ok")
        z_ok = sem("z_ok")
        zT_ok = sem("zT_ok")
        zhi_ok = sem("zhi_ok")
        zlo_ok = sem("zlo_ok")
        qkv_ok = sem("qkv_ok")
        qk_read = sem("qk_read")
        v_read = sem("v_read")
        y_ok = sem("y_ok")
        c_ok = sem("c_ok")
        sq_ok = sem("sq_ok")
        vs_ok = sem("vs_ok")
        rsq_ok = sem("rsq_ok")
        n_ok = sem("n_ok")
        qkT_ok = sem("qkT_ok")
        qkT_read = sem("qkT_read")
        s_ok = sem("s_ok")
        att_ok = sem("att_ok")
        masked = sem("masked")
        av_ok = sem("av_ok")
        o32_ok = sem("o32_ok")
        ohi_ok = sem("ohi_ok")
        olo_ok = sem("olo_ok")
        out_ok = sem("out_ok")
        out_read = sem("out_read")

        block = ctx.enter_context(nc.Block(no_gpsimd_drain=True))
        x_tiles = x_dram.rearrange("(t p) c -> p t c", p=P)

        @block.sync
        def _(sp):
            for b in range(B):
                sp.dma_start(x_res[:, BT * b:BT * (b + 1), :], x_tiles[:, BT * b:BT * (b + 1), :]).then_inc(x_in[b], 16)
            for m in range(4):
                sp.dma_start(w_raw[:, m, :, :], w_dram[m].rearrange("(k p) n -> p k n", p=P)).then_inc(w_in[m], 16)
            sp.dma_start(gam[:, :], gamma_dram.partition_broadcast(P)).then_inc(gb_in, 16)
            sp.dma_start(bet[:, :], beta_dram.partition_broadcast(P)).then_inc(gb_in, 16)

        @block.gpsimd
        def _(pool):
            pool.memset(ones[:, :], 1.0).then_inc(ones_ok, 1)
            pool.wait_ge(ve_ok, 1)
            pool.tensor_tensor(rstd[:, :], ve[:, :], minus_half[:, 0:TT], ALU.pow).then_inc(rstd_ok, 1)
            for m in (2, 3):
                pool.wait_ge(w_hi_ok, m + 1)
                pool.tensor_tensor(w_lo[:, m, :, :], w_raw[:, m, :, :], w_hi[:, m, :, :].bitcast(F32),
                                   ALU.subtract).then_inc(w_split, 1)
            pool.wait_ge(gb_in, 32)
            with pool.Fori(0, B) as b:
                for t in range(BT):
                    n = BT * b + t
                    yt = y[:, t % 2, :, :].rearrange("p (m h) d -> p m (h d)", m=2)
                    pool.wait_ge(qk_read, 2 * n + 2)
                    pool.tensor_tensor(yt, yt, bet[:, :].unsqueeze(1).broadcast_to([P, 2, C]), ALU.add).then_inc(y_ok, 1)
                    pool.wait_ge(vs_ok, n + 1)
                    pool.tensor_tensor(rsq[:, t % 2, :], vsum[:, t % 2, :], minus_half[:, 0:2 * H],
                                       ALU.pow).then_inc(rsq_ok, 1)
                for hg in range(HG):
                    for kt in range(BT):
                        diag = att[:, kt, :, kt * P:(kt + 1) * P]
                        pool.wait_ge(att_ok, (b * HG * BT + hg * BT + kt + 1) * GH)
                        pool.tensor_tensor(diag, diag, mask[:, :].unsqueeze(1).broadcast_to([P, GH, P]),
                                           ALU.mult).then_inc(masked, 1)

        @block.scalar
        def _(act):
            for m in range(4):
                act.wait_ge(w_in[m], 16)
                nc.scalar.copy(w_hi[:, m, :, :], w_raw[:, m, :, :]).then_inc(w_hi_ok, 1)

            def read_z(b, t):
                n = BT * b + t
                act.wait_ge(zT_ok, n + 1)
                nc.scalar.copy(row_halves(z_hi[:, t % 2, :, :].rearrange("p k n -> p (k n)"), CK),
                               row_halves(tb[turn_bank("z", t)][:, :], CK)).then_inc(zhi_ok, 1)

            def read_qkT(b, t):
                n = BT * b + t
                for i, (what, dst) in enumerate((("q", qT), ("k", kT))):
                    act.wait_ge(qkT_ok, 2 * n + i + 1)
                    nc.scalar.copy(dst[:, :, t * P:(t + 1) * P],
                                   row_halves(tb[turn_bank(what, t)][:, :], HG)).then_inc(qkT_read, 1)

            with act.Fori(0, B) as b:
                read_z(b, 0)
                for t in range(BT):
                    n = BT * b + t
                    if t + 1 < BT:
                        read_z(b, t + 1)
                    act.wait_ge(qkv_ok, 3 * n + 3)
                    nc.scalar.copy(v[:, t, :], pj[(3 * t + 2) % 2][:, :]).then_inc(v_read, 1)
                    act.wait_ge(c_ok, n + 1)
                    nc.scalar.activation(sq[:, t % 2, :, :], y[:, t % 2, :, :], ACT.Square).then_inc(sq_ok, 1)
                    if t >= 1:
                        read_qkT(b, t - 1)
                read_qkT(b, BT - 1)
                act.wait_ge(w_split, 4)
                for hg in range(HG):
                    for kt in range(BT):
                        if hg > 0:
                            act.wait_ge(av_ok, (b * HG + hg - 1) * BT + kt + 1)
                        for j in range(GH):
                            act.wait_ge(s_ok, ((b * HG + hg) * BT + kt) * GH + j + 1)
                            nc.scalar.activation(att[:, kt, j, kt * P:S], sc[j][:, kt * P:S],
                                                 ACT.Square).then_inc(att_ok, 1)
                    act.wait_ge(o32_ok, b * HG + hg + 1)
                    nc.scalar.copy(oT_hi[:, hg, :], o32[:, :]).then_inc(ohi_ok, 1)

        @block.vector
        def _(v_):
            links = [0]

            def link(ins, base=0):
                links[0] += 1
                ins.then_inc(dve, 1)
                v_.wait_ge(dve, base + links[0])

            for t in range(TT):
                if t % BT == 0:
                    v_.wait_ge(x_in[t // BT], 16)
                link(nc.vector.bn_stats(stats[:, t % 2, :], x_res[:, t, :]))
                link(nc.vector.bn_aggr(mv[:, t, :], stats[:, t % 2, :]))
            nc.vector.tensor_scalar(ve[:, :], mv[:, :, 1], LN_EPS, None, ALU.add).then_inc(ve_ok, 1)
            for m in (0, 1):
                v_.wait_ge(w_hi_ok, m + 1)
                nc.vector.tensor_tensor(w_lo[:, m, :, :], w_raw[:, m, :, :], w_hi[:, m, :, :].bitcast(F32),
                                        ALU.subtract).then_inc(w_split, 1)
            v_.wait_ge(rstd_ok, 1)
            v_.wait_ge(gb_in, 32)
            head = links[0]
            LINKS = 4 * BT + 2 * HG

            with v_.Fori(0, B) as b:
                links[0] = 0
                base = head + b * LINKS

                def norm(t):
                    n = BT * b + t
                    if t >= 2:
                        v_.wait_ge(zT_ok, n - 1)
                    nc.vector.tensor_scalar(z[:, t % 2, :], x_res[:, n, :], mv[:, n, 0:1], rstd[:, bass.ds(n, 1)],
                                            ALU.subtract, ALU.mult).then_inc(z_ok, 1)

                def low_z(t):
                    n = BT * b + t
                    v_.wait_ge(zhi_ok, n + 1)
                    nc.vector.tensor_tensor(z_lo[:, t % 2, :, :], row_halves(tb[turn_bank("z", t)][:, :], CK),
                                            z_hi[:, t % 2, :, :].bitcast(F32), ALU.subtract).then_inc(zlo_ok, 1)

                def times_gamma(t):
                    n = BT * b + t
                    for i in range(2):
                        v_.wait_ge(qkv_ok, 3 * n + i + 1)
                        nc.vector.tensor_tensor(y[:, t % 2, i * H:(i + 1) * H, :].rearrange("p h d -> p (h d)"),
                                                pj[(3 * t + i) % 2][:, :], gam[:, :], ALU.mult).then_inc(qk_read, 1)

                def variances(t):
                    n = BT * b + t
                    v_.wait_ge(y_ok, n + 1)
                    link(nc.vector.tensor_reduce(msum[:, t % 2, :], y[:, t % 2, :, :], AX_X, ALU.add), base)
                    link(nc.vector.tensor_scalar(msum[:, t % 2, :], msum[:, t % 2, :], 1.0 / D, None, ALU.mult), base)
                    nc.vector.tensor_tensor(y[:, t % 2, :, :], y[:, t % 2, :, :],
                                            msum[:, t % 2, :].unsqueeze(2).broadcast_to([P, 2 * H, D]),
                                            ALU.subtract).then_inc(c_ok, 1)
                    v_.wait_ge(sq_ok, n + 1)
                    link(nc.vector.tensor_reduce(vsum[:, t % 2, :], sq[:, t % 2, :, :], AX_X, ALU.add), base)
                    nc.vector.tensor_scalar(vsum[:, t % 2, :], vsum[:, t % 2, :], 1.0 / D, ATT_EPS,
                                            ALU.mult, ALU.add).then_inc(vs_ok, 1)

                def finish_features(t):
                    n = BT * b + t
                    v_.wait_ge(rsq_ok, n + 1)
                    link(nc.vector.tensor_scalar(rsq[:, t % 2, 0:H], rsq[:, t % 2, 0:H], float(D) ** -0.5, None,
                                                 ALU.mult), base)
                    nc.vector.tensor_tensor(y[:, t % 2, :, :], y[:, t % 2, :, :],
                                            rsq[:, t % 2, :].unsqueeze(2).broadcast_to([P, 2 * H, D]),
                                            ALU.mult).then_inc(n_ok, 1)

                norm(0)
                norm(1)
                low_z(0)
                for t in range(BT):
                    if t + 1 < BT:
                        low_z(t + 1)
                    if t + 2 < BT:
                        norm(t + 2)
                    if t >= 2:
                        v_.wait_ge(qkT_ok, 2 * (BT * b + t - 1))
                    times_gamma(t)
                    if t >= 1:
                        finish_features(t - 1)
                    variances(t)
                finish_features(BT - 1)

                for hg in range(HG):
                    num, den = nd[hg % 2]
                    n = HG * b + hg
                    v_.wait_ge(av_ok, BT * (n + 1))
                    link(nc.vector.tensor_scalar(rec[:, :], den[:, :], ATT_EPS, None, ALU.add), base)
                    link(nc.vector.reciprocal(rec[:, :], rec[:, :]), base)
                    if hg:
                        v_.wait_ge(olo_ok, n)
                    nc.vector.tensor_tensor(o32[:, :], num[:, :], rec[:, :], ALU.mult).then_inc(o32_ok, 1)
                    v_.wait_ge(ohi_ok, n + 1)
                    nc.vector.tensor_tensor(oT_lo[:, hg, :], o32[:, :], oT_hi[:, hg, :].bitcast(F32),
                                            ALU.subtract).then_inc(olo_ok, 1)
                for t in range(BT):
                    n = BT * b + t
                    v_.wait_ge(out_ok, n + 1)
                    nc.vector.tensor_tensor(x_res[:, n, :], x_res[:, n, :], pj[t % 2][:, :],
                                            ALU.add).then_inc(out_read, 1)
                assert links[0] == LINKS

        @block.tensor
        def _(pe):
            def project(out, hi, lo, m, count):
                for k in range(CK):
                    for i, (a, w) in enumerate(((hi, w_hi), (lo, w_hi), (hi, w_lo))):
                        ins = nc.tensor.matmul(out, a(k), w[:, m, k, :], start=(k == 0 and i == 0),
                                               stop=(k == CK - 1 and i == 2))
                ins.then_inc(count, 1)

            def bank_free(b, what, t):
                turn = TURNS.index((what, t))
                if turn >= 2:
                    what, t = TURNS[turn - 2]
                    if what == "z":
                        pe.wait_ge(zlo_ok, BT * b + t + 1)
                    else:
                        pe.wait_ge(qkT_read, 2 * (BT * b + t) + (what == "k") + 1)

            def transpose_z(b, t):
                n = BT * b + t
                pe.wait_ge(z_ok, n + 1)
                bank_free(b, "z", t)
                for k in range(CK):
                    ins = nc.tensor.transpose(tb[turn_bank("z", t)][:, k * P:(k + 1) * P], z[:, t % 2, k * P:(k + 1) * P],
                                              ident[:, :])
                ins.then_inc(zT_ok, 1)

            def transpose_qk(b, t):
                n = BT * b + t
                pe.wait_ge(n_ok, n + 1)
                for i, what in enumerate("qk"):
                    bank_free(b, what, t)
                    for g in range(HG):
                        ins = nc.tensor.transpose(
                            tb[turn_bank(what, t)][:, g * P:(g + 1) * P],
                            y[:, t % 2, i * H + g * GH:i * H + (g + 1) * GH, :].rearrange("p h d -> p (h d)"),
                            ident[:, :])
                    ins.then_inc(qkT_ok, 1)

            pe.wait_ge(ones_ok, 1)
            with pe.Fori(0, B) as b:
                transpose_z(b, 0)
                for t in range(BT):
                    n = BT * b + t
                    if t + 1 < BT:
                        transpose_z(b, t + 1)
                    pe.wait_ge(zlo_ok, n + 1)
                    for m in range(3):
                        if t == 0:
                            pe.wait_ge(w_split, m + 1)
                        if 3 * t + m >= 2:
                            tenant = 3 * t + m - 2
                            if tenant % 3 == 2:
                                pe.wait_ge(v_read, BT * b + tenant // 3 + 1)
                            else:
                                pe.wait_ge(qk_read, 2 * (BT * b + tenant // 3) + tenant % 3 + 1)
                        project(pj[(3 * t + m) % 2][:, :], lambda k: z_hi[:, t % 2, k, :],
                                lambda k: z_lo[:, t % 2, k, :], m, qkv_ok)
                    if t >= 1:
                        transpose_qk(b, t - 1)
                transpose_qk(b, BT - 1)
                pe.wait_ge(qkT_read, 2 * BT * (b + 1))
                pe.wait_ge(v_read, BT * (b + 1))
                for hg in range(HG):
                    for kt in range(BT):
                        for j in range(GH):
                            rows = slice(D * j, D * (j + 1))
                            if hg or kt:
                                pe.wait_ge(att_ok, ((b * HG + hg) * BT + kt - 1) * GH + j + 1)
                            nc.tensor.matmul(sc[j][:, kt * P:S], kT[rows, hg, kt * P:(kt + 1) * P],
                                             qT[rows, hg, kt * P:S], start=True, stop=True).then_inc(s_ok, 1)
                    num, den = nd[hg % 2]
                    if hg >= 2:
                        pe.wait_ge(o32_ok, HG * b + hg - 1)
                    for kt in range(BT):
                        pe.wait_ge(masked, (b * HG + hg) * BT + kt + 1)
                        for j in range(GH):
                            rows = slice(D * j, D * (j + 1))
                            nc.tensor.matmul(num[rows, kt * P:S], v[:, kt, (hg * GH + j) * D:(hg * GH + j + 1) * D],
                                             att[:, kt, j, kt * P:S], start=(kt == 0), stop=(kt == BT - 1))
                        for j in range(GH):
                            rows = slice(D * j, D * (j + 1))
                            ins = nc.tensor.matmul(den[rows, kt * P:S], ones[:, :],
                                                   att[:, kt, j, kt * P:S], start=(kt == 0), stop=(kt == BT - 1))
                            if j == GH - 1:
                                ins.then_inc(av_ok, 1)
                pe.wait_ge(w_split, 4)
                pe.wait_ge(olo_ok, HG * (b + 1))
                for t in range(BT):
                    if t >= 2:
                        pe.wait_ge(out_read, BT * b + t - 1)
                    project(pj[t % 2][:, :], lambda k: oT_hi[:, k, t * P:(t + 1) * P],
                            lambda k: oT_lo[:, k, t * P:(t + 1) * P], 3, out_ok)
                pe.wait_ge(out_read, BT * (b + 1))
BLOCK_TILES = 4
LOOP_TILES = 2 * BLOCK_TILES


def context_keys_values(nc, ctxT_dram, wkv_dram, bkv_dram, k_parts, v_int, v_step, ident_bf):
    with ExitStack() as ctx:
        def sb(name, shape, dt):
            return ctx.enter_context(nc.sbuf_tensor(name, shape, dt))

        def psum(name, shape, dt):
            return ctx.enter_context(nc.psum_tensor(name, shape, dt))

        def sem(name):
            return ctx.enter_context(nc.semaphore("ck_" + name))

        v_raw = sb("ck_v_raw", [P, KT, C], F32)
        w_raw = v_raw[:, 0:2 * CK, :].rearrange("p (k m) c -> p k (m c)", k=CK)
        w_hi = sb("ck_w_hi", [P, CK, 2 * C], F32R)
        w_lo = sb("ck_w_lo", [P, CK, 2 * C], F32R)
        raw = sb("ck_raw", [P, 2, CK, BLOCK_TILES * P], F32)
        c_hi = sb("ck_c_hi", [P, 2, CK, P], F32R)
        c_lo = sb("ck_c_lo", [P, 2, CK, P], F32R)
        bias = sb("ck_bias", [P, 2 * C], F32)
        kf = sb("ck_kf", [P, H, D], F32)
        kq = sb("ck_kq", [P, H, D], F32)
        rest = sb("ck_rest", [P, H, D], F32)
        step = sb("ck_step", [P, H], F32)
        rstep = sb("ck_rstep", [P, H], F32)
        parts = sb("ck_parts", [P, 2, H, 3, D], BF16)
        v_top = sb("ck_v_top", [P, C], F32)
        v_rstep = sb("ck_v_rstep", [P, C], F32)

        kb = [psum(f"ck_kb{i}", [P, C], F32) for i in range(2)]
        vb = [psum(f"ck_vb{i}", [P, C], F32) for i in range(2)]
        tr = [psum(f"ck_tr{i}", [3 * D, H, P], BF16) for i in range(2)]

        w_in = sem("w_in")
        b_in = sem("b_in")
        raw_in = [sem(f"raw_in{i}") for i in range(2)]
        whi_ok = sem("whi_ok")
        wlo_ok = sem("wlo_ok")
        chi_ok = sem("chi_ok")
        clo_ok = sem("clo_ok")
        k_ok = sem("k_ok")
        v_ok = sem("v_ok")
        kf_ok = sem("kf_ok")
        vf_ok = sem("vf_ok")
        kt_ok = sem("kt_ok")
        hi_ok = sem("hi_ok")
        rest_ok = sem("rest_ok")
        mid_ok = sem("mid_ok")
        lo_ok = sem("lo_ok")
        tr_ok = sem("tr_ok")
        tr_read = sem("tr_read")
        top_ok = sem("top_ok")
        all_top = sem("all_top")
        dve = sem("dve")

        block = ctx.enter_context(nc.Block(no_gpsimd_drain=True))
        ctxT = ctxT_dram.rearrange("(k p) n -> p k n", p=P)

        @block.sync
        def _(sp):
            sp.dma_start(w_raw, wkv_dram.rearrange("(k p) n -> p k n", p=P)).then_inc(w_in, 16)
            sp.dma_start(bias[:, :], bkv_dram.partition_broadcast(P)).then_inc(b_in, 16)
            for g in range(KT // BLOCK_TILES):
                if g >= 2:
                    sp.wait_ge(clo_ok, (g - 1) * BLOCK_TILES)
                sp.dma_start(raw[:, g % 2, :, :], ctxT[:, :, g * BLOCK_TILES * P:(g + 1) * BLOCK_TILES * P])\
                  .then_inc(raw_in[g % 2], 16)

        def raw_tile(t):
            return raw[:, t // BLOCK_TILES, :, t % BLOCK_TILES * P:(t % BLOCK_TILES + 1) * P]

        @block.gpsimd
        def _(pool):
            pool.wait_ge(whi_ok, 1)
            nc.gpsimd.tensor_tensor(w_lo[:, :, C:2 * C], w_raw[:, :, C:2 * C], w_hi[:, :, C:2 * C].bitcast(F32),
                                    ALU.subtract).then_inc(wlo_ok, 1)
            with pool.Fori(0, KT // LOOP_TILES) as i:
                for t in range(LOOP_TILES):
                    pool.wait_ge(chi_ok, i * LOOP_TILES + t + 1)
                    nc.gpsimd.tensor_tensor(c_lo[:, t % 2, :, :], raw_tile(t), c_hi[:, t % 2, :, :].bitcast(F32),
                                            ALU.subtract).then_inc(clo_ok, 1)
            pool.wait_ge(top_ok, 1)
            nc.gpsimd.partition_all_reduce(v_step[:, :], v_top[:, :], P, ABSMAX).then_inc(all_top, 1)

        @block.scalar
        def _(act):
            act.wait_ge(w_in, 16)
            nc.scalar.copy(w_hi[:, :, :], w_raw).then_inc(whi_ok, 1)

            def split(i, t):
                n = i * LOOP_TILES + t
                if t % BLOCK_TILES == 0:
                    act.wait_ge(raw_in[t // BLOCK_TILES], 16 * i + 16)
                if t >= 2:
                    act.wait_ge(v_ok, n - 1)
                nc.scalar.copy(c_hi[:, t % 2, :, :], raw_tile(t)).then_inc(chi_ok, 1)

            with act.Fori(0, KT // LOOP_TILES) as i:
                split(i, 0)
                for t in range(LOOP_TILES):
                    n = i * LOOP_TILES + t
                    if t + 1 < LOOP_TILES:
                        split(i, t + 1)
                    act.wait_ge(kt_ok, n + 1)
                    nc.scalar.copy(parts[:, t % 2, :, 0, :], kq[:, :, :]).then_inc(hi_ok, 1)
                    act.wait_ge(rest_ok, n + 1)
                    nc.scalar.copy(parts[:, t % 2, :, 1, :], rest[:, :, :]).then_inc(mid_ok, 1)

        @block.vector
        def _(v_):
            links = [0]

            def link(ins, base=0):
                links[0] += 1
                ins.then_inc(dve, 1)
                v_.wait_ge(dve, base + links[0])

            def per_head(x):
                return x[:, :].unsqueeze(2).broadcast_to([P, H, D])

            def keep_keys(i, t):
                n = i * LOOP_TILES + t
                v_.wait_ge(tr_ok, n + 1)
                nc.vector.tensor_copy(k_parts[0:3 * D, :, bass.ds(n * P, P)], tr[t % 2][:, :, :]).then_inc(tr_read, 1)

            v_.wait_ge(whi_ok, 1)
            nc.vector.tensor_tensor(w_lo[:, :, 0:C], w_raw[:, :, 0:C], w_hi[:, :, 0:C].bitcast(F32),
                                    ALU.subtract).then_inc(wlo_ok, 1)
            v_.wait_ge(b_in, 16)
            LINKS = 5 * LOOP_TILES
            with v_.Fori(0, KT // LOOP_TILES) as i:
                links[0] = 0
                base = i * LINKS
                for t in range(LOOP_TILES):
                    n = i * LOOP_TILES + t
                    v_.wait_ge(k_ok, n + 1)
                    nc.vector.tensor_tensor(kf[:, :, :], kb[t % 2][:, :].rearrange("p (h d) -> p h d", h=H),
                                            bias[:, 0:C].rearrange("p (h d) -> p h d", h=H), ALU.add).then_inc(kf_ok, 1)
                    v_.wait_ge(kf_ok, n + 1)
                    link(nc.vector.tensor_reduce(step[:, :], kf[:, :, :], AX_X, ALU.max, apply_absolute_value=True), base)
                    link(nc.vector.tensor_scalar(step[:, :], step[:, :], 1.0 / QMAX, Q_FLOOR, ALU.mult, ALU.max), base)
                    link(nc.vector.reciprocal(rstep[:, :], step[:, :]), base)
                    link(nc.vector.tensor_tensor(kf[:, :, :], kf[:, :, :], per_head(rstep), ALU.mult), base)
                    link(nc.vector.tensor_scalar(kf[:, :, :], kf[:, :, :], MAGIC, MAGIC, ALU.add, ALU.subtract), base)
                    nc.vector.tensor_tensor(kq[:, :, :], kf[:, :, :], per_head(step), ALU.mult).then_inc(kt_ok, 1)
                    v_.wait_ge(v_ok, n + 1)
                    nc.vector.tensor_tensor(v_raw[:, n, :], vb[t % 2][:, :], bias[:, C:2 * C], ALU.add).then_inc(vf_ok, 1)
                    v_.wait_ge(hi_ok, n + 1)
                    nc.vector.tensor_tensor(rest[:, :, :], kq[:, :, :], parts[:, t % 2, :, 0, :],
                                            ALU.subtract).then_inc(rest_ok, 1)
                    if t >= 1:
                        keep_keys(i, t - 1)
                    v_.wait_ge(mid_ok, n + 1)
                    nc.vector.tensor_tensor(parts[:, t % 2, :, 2, :], rest[:, :, :], parts[:, t % 2, :, 1, :],
                                            ALU.subtract).then_inc(lo_ok, 1)
                keep_keys(i, LOOP_TILES - 1)
                assert links[0] == LINKS
            links[0] = 0
            base = LINKS * (KT // LOOP_TILES)
            v_.wait_ge(vf_ok, KT)
            nc.vector.tensor_reduce(v_top[:, :], v_raw[:, :, :].rearrange("p t c -> p c t"), AX_X,
                                    ALU.max, apply_absolute_value=True).then_inc(top_ok, 1)
            v_.wait_ge(all_top, 1)
            link(nc.vector.tensor_scalar(v_step[:, :], v_step[:, :], 1.0 / QMAX, Q_FLOOR, ALU.mult, ALU.max), base)
            link(nc.vector.reciprocal(v_rstep[:, :], v_step[:, :]), base)
            link(nc.vector.tensor_tensor(v_raw[:, :, :], v_raw[:, :, :],
                                         v_rstep[:, :].unsqueeze(1).broadcast_to([P, KT, C]), ALU.mult), base)
            link(nc.vector.tensor_scalar(v_int[:, :, :], v_raw[:, :, :], MAGIC, MAGIC, ALU.add, ALU.subtract), base)

        @block.tensor
        def _(pe):
            def transpose_keys(i, t):
                n = i * LOOP_TILES + t
                pe.wait_ge(lo_ok, n + 1)
                if t >= 2:
                    pe.wait_ge(tr_read, n - 1)
                for h in range(H):
                    ins = nc.tensor.transpose(tr[t % 2][:, h, :], parts[:, t % 2, h, :, :].rearrange("p a d -> p (a d)"),
                                              ident_bf[:, :])
                ins.then_inc(tr_ok, 1)

            pe.wait_ge(wlo_ok, 2)
            with pe.Fori(0, KT // LOOP_TILES) as i:
                for t in range(LOOP_TILES):
                    n = i * LOOP_TILES + t
                    pe.wait_ge(clo_ok, n + 1)
                    for out, m, read, made in ((kb, 0, kf_ok, k_ok), (vb, 1, vf_ok, v_ok)):
                        if t >= 2:
                            pe.wait_ge(read, n - 1)
                        for k in range(CK):
                            for j, (a, w) in enumerate(((c_hi, w_hi), (c_lo, w_hi), (c_hi, w_lo))):
                                ins = nc.tensor.matmul(out[t % 2][:, :], a[:, t % 2, k, :], w[:, k, m * C:(m + 1) * C],
                                                       start=(k == 0 and j == 0), stop=(k == CK - 1 and j == 2))
                        ins.then_inc(made, 1)
                    if t >= 1:
                        transpose_keys(i, t - 1)
                transpose_keys(i, LOOP_TILES - 1)
                pe.wait_ge(tr_read, (i + 1) * LOOP_TILES)
LN_PMAX = 5.541263545158426
HALF = KEYS // 2
HKT = KT // 2


def normalise_statistics(v_, pool, nc, x_res, stats, mv, ve, rstd, minus_half, chain, ve_ok, rstd_ok):
    for t in range(TT):
        nc.vector.bn_stats(stats[:, t, :], x_res[:, t, :]).then_inc(chain, 1)
    v_.wait_ge(chain, TT)
    for t in range(TT):
        nc.vector.bn_aggr(mv[:, t, :], stats[:, t, :]).then_inc(chain, 1)
    v_.wait_ge(chain, 2 * TT)
    nc.vector.tensor_scalar(ve[:, :], mv[:, :, 1], LN_EPS, None, ALU.add).then_inc(ve_ok, 1)


def cross_queries(nc, wq_dram, bq_dram, x_res, q_int, q_step, q_nstep, ident, minus_half, ident_bf):
    scale = float(D) ** -0.5
    with ExitStack() as ctx:
        def sb(name, shape, dt):
            return ctx.enter_context(nc.sbuf_tensor(name, shape, dt))

        def psum(name, shape, dt):
            return ctx.enter_context(nc.psum_tensor(name, shape, dt))

        def sem(name):
            return ctx.enter_context(nc.semaphore("cq_" + name))

        w_raw = sb("cq_w_raw", [P, CK, C], F32)
        w_hi = sb("cq_w_hi", [P, CK, C], F32R)
        w_lo = sb("cq_w_lo", [P, CK, C], F32R)
        bias = sb("cq_bias", [P, C], F32)
        stats = sb("cq_stats", [P, TT, 6], F32)
        mv = sb("cq_mv", [P, TT, 2], F32)
        ve = sb("cq_ve", [P, TT], F32)
        rstd = sb("cq_rstd", [P, TT], F32)
        z = sb("cq_z", [P, 2, C], F32)
        z_hi = sb("cq_z_hi", [P, 2, CK, P], F32R)
        z_lo = sb("cq_z_lo", [P, 2, CK, P], F32R)
        qf = sb("cq_qf", [P, H, D], F32)
        rstep = sb("cq_rstep", [P, H], F32)
        q3 = sb("cq_q3", [P, 2, H, 3, D], BF16)
        tz = [psum(f"cq_tz{i}", [P, C], F32) for i in range(2)]
        pq = [psum(f"cq_pq{i}", [P, C], F32) for i in range(2)]
        tq = [psum(f"cq_tq{i}", [3 * D, H, P], BF16) for i in range(2)]

        w_in = sem("w_in")
        b_in = sem("b_in")
        whi_ok = sem("whi_ok")
        wlo_ok = sem("wlo_ok")
        chain = sem("chain")
        ve_ok = sem("ve_ok")
        rstd_ok = sem("rstd_ok")
        z_ok = sem("z_ok")
        zT_ok = sem("zT_ok")
        zhi_ok = sem("zhi_ok")
        zlo_ok = sem("zlo_ok")
        q_ok = sem("q_ok")
        q_read = sem("q_read")
        q3_ok = sem("q3_ok")
        tq_ok = sem("tq_ok")
        tq_read = sem("tq_read")
        dve = sem("dve")
        block = ctx.enter_context(nc.Block(no_gpsimd_drain=True))

        @block.sync
        def _(sp):
            sp.dma_start(w_raw[:, :, :], wq_dram.rearrange("(k p) n -> p k n", p=P)).then_inc(w_in, 16)
            sp.dma_start(bias[:, :], bq_dram.partition_broadcast(P)).then_inc(b_in, 16)

        @block.gpsimd
        def _(pool):
            pool.wait_ge(ve_ok, 1)
            nc.gpsimd.tensor_tensor(rstd[:, :], ve[:, :], minus_half[:, 0:TT], ALU.pow).then_inc(rstd_ok, 1)

        @block.scalar
        def _(act):
            act.wait_ge(w_in, 16)
            nc.scalar.copy(w_hi[:, :, :], w_raw[:, :, :]).then_inc(whi_ok, 1)
            with act.Fori(0, TT // 2) as i:
                for t in range(2):
                    act.wait_ge(zT_ok, 2 * i + t + 1)
                    nc.scalar.copy(z_hi[:, t, :, :], row_halves(tz[t][:, :], CK)).then_inc(zhi_ok, 1)

        @block.vector
        def _(v_):
            links = [0]

            def link(ins, base=0):
                links[0] += 1
                ins.then_inc(dve, 1)
                v_.wait_ge(dve, base + links[0])

            def per_head(x):
                return x[:, :].unsqueeze(2).broadcast_to([P, H, D])

            normalise_statistics(v_, None, nc, x_res, stats, mv, ve, rstd, minus_half, chain, ve_ok, rstd_ok)
            v_.wait_ge(whi_ok, 1)
            nc.vector.tensor_tensor(w_lo[:, :, :], w_raw[:, :, :], w_hi[:, :, :].bitcast(F32),
                                    ALU.subtract).then_inc(wlo_ok, 1)
            v_.wait_ge(rstd_ok, 1)
            v_.wait_ge(b_in, 16)
            LINKS = 2 * 6
            with v_.Fori(0, TT // 2) as i:
                links[0] = 0
                base = i * LINKS
                for t in range(2):
                    n = 2 * i + t
                    nc.vector.tensor_scalar(z[:, t, :], x_res[:, n, :], mv[:, n, 0:1], rstd[:, bass.ds(n, 1)],
                                            ALU.subtract, ALU.mult).then_inc(z_ok, 1)
                for t in range(2):
                    n = 2 * i + t
                    v_.wait_ge(zhi_ok, n + 1)
                    nc.vector.tensor_tensor(z_lo[:, t, :, :], row_halves(tz[t][:, :], CK), z_hi[:, t, :, :].bitcast(F32),
                                            ALU.subtract).then_inc(zlo_ok, 1)
                for t in range(2):
                    n = 2 * i + t
                    v_.wait_ge(q_ok, n + 1)
                    link(nc.vector.tensor_tensor(qf[:, :, :], pq[t][:, :].rearrange("p (h d) -> p h d", h=H),
                                                 bias[:, :].rearrange("p (h d) -> p h d", h=H), ALU.add), base)
                    link(nc.vector.tensor_reduce(rstep[:, :], qf[:, :, :], AX_X, ALU.max, apply_absolute_value=True), base)
                    link(nc.vector.tensor_scalar(q_step[:, n, :], rstep[:, :], scale / QMAX, Q_FLOOR, ALU.mult, ALU.max), base)
                    nc.vector.tensor_scalar(q_nstep[:, n, :], q_step[:, n, :], -1.0, None, ALU.mult)
                    link(nc.vector.reciprocal(rstep[:, :], q_step[:, n, :]), base)
                    link(nc.vector.tensor_scalar(rstep[:, :], rstep[:, :], scale, None, ALU.mult), base)
                    link(nc.vector.tensor_tensor(qf[:, :, :], qf[:, :, :], per_head(rstep), ALU.mult), base)
                    nc.vector.tensor_scalar(q3[:, t, :, :, :], qf[:, :, :].unsqueeze(2).broadcast_to([P, H, 3, D]),
                                            MAGIC, MAGIC, ALU.add, ALU.subtract).then_inc(q3_ok, 1)
                    v_.wait_ge(q3_ok, n + 1)
                for t in range(2):
                    n = 2 * i + t
                    v_.wait_ge(tq_ok, n + 1)
                    nc.vector.tensor_copy(q_int[0:3 * D, n, :, :], tq[t][:, :, :]).then_inc(tq_read, 1)
                assert links[0] == LINKS

        @block.tensor
        def _(pe):
            pe.wait_ge(wlo_ok, 1)
            with pe.Fori(0, TT // 2) as i:
                for t in range(2):
                    pe.wait_ge(z_ok, 2 * i + t + 1)
                    for k in range(CK):
                        ins = nc.tensor.transpose(tz[t][:, k * P:(k + 1) * P], z[:, t, k * P:(k + 1) * P], ident[:, :])
                    ins.then_inc(zT_ok, 1)
                for t in range(2):
                    pe.wait_ge(zlo_ok, 2 * i + t + 1)
                    for k in range(CK):
                        for j, (a, w) in enumerate(((z_hi, w_hi), (z_lo, w_hi), (z_hi, w_lo))):
                            ins = nc.tensor.matmul(pq[t][:, :], a[:, t, k, :], w[:, k, :],
                                                   start=(k == 0 and j == 0), stop=(k == CK - 1 and j == 2))
                    ins.then_inc(q_ok, 1)
                for t in range(2):
                    pe.wait_ge(q3_ok, 2 * i + t + 1)
                    for h in range(H):
                        ins = nc.tensor.transpose(tq[t][:, h, :], q3[:, t, h, :, :].rearrange("p a d -> p (a d)"),
                                                  ident_bf[:, :])
                    ins.then_inc(tq_ok, 1)
                pe.wait_ge(tq_read, 2 * i + 2)


def cross_scores(nc, k_parts, v_int, q_int, q_step, q_nstep, o_raw, z_sum, ident16):
    with ExitStack() as ctx:
        def sb(name, shape, dt):
            return ctx.enter_context(nc.sbuf_tensor(name, shape, dt))

        def psum(name, shape, dt):
            return ctx.enter_context(nc.psum_tensor(name, shape, dt))

        def sem(name):
            return ctx.enter_context(nc.semaphore("cs_" + name))

        p_int = sb("cs_p_int", [P, 2, KEYS], I16)
        pT = sb("cs_pT", [P, 2, KT, P], BF16)
        top = sb("cs_top", [P, 2, 2], F32)
        top1 = sb("cs_top1", [P, 2], F32)
        bias = sb("cs_bias", [P, 2], F32)
        s_a = [psum(f"cs_s_a{i}", [P, HALF], F32) for i in range(2)]
        s_b = psum("cs_s_b", [P, HALF], F32)
        tp = psum("cs_tp", [P, HKT, P], F16)
        out = psum("cs_out0", [P, C], F32)

        sa_ok = sem("sa_ok")
        sb_ok = sem("sb_ok")
        bias_ok = sem("bias_ok")
        ea_ok = sem("ea_ok")
        eb_ok = sem("eb_ok")
        ta_ok = sem("ta_ok")
        tb_ok = sem("tb_ok")
        ra_ok = sem("ra_ok")
        rb_ok = sem("rb_ok")
        av_ok = sem("av_ok")
        out_read = sem("out_read")
        dve = sem("dve")
        block = ctx.enter_context(nc.Block(no_gpsimd_drain=True))
        UNITS = TT * H

        def units(engine, step):
            for h in range(H):
                step(0, h, h)
            with engine.Fori(1, TT) as t:
                for h in range(H):
                    step(t, h, t * H + h)
            for n in range(UNITS, UNITS + 3):
                step(None, n - UNITS, n)

        def alive(t, h, lag):
            if t is None:
                return h < lag
            return not (isinstance(t, int) and h < lag)

        @block.scalar
        def _(act):
            def step(t, h, n):
                if t is None:
                    return
                act.wait_ge(bias_ok, n + 1)
                if alive(t, h, 2):
                    act.wait_ge(tb_ok, n - 1)
                nc.scalar.activation(p_int[:, h % 2, HALF:KEYS], s_b[:, :], ACT.Exp, bias=bias[:, h % 2:h % 2 + 1],
                                     scale=q_step[:, t, h:h + 1], accum_out=z_sum[:, t, h, 1:2]).then_inc(eb_ok, 1)
                nc.scalar.activation(p_int[:, h % 2, 0:HALF], s_a[h % 2][:, :], ACT.Exp, bias=bias[:, h % 2:h % 2 + 1],
                                     scale=q_step[:, t, h:h + 1], accum_out=z_sum[:, t, h, 0:1]).then_inc(ea_ok, 1)
            units(act, step)

        @block.vector
        def _(v_):
            def step(t, h, n):
                u = h % 2
                if alive(t, h, 2):
                    v_.wait_ge(ta_ok, n - 1)
                    if t is None or alive(t, h, 4):
                        v_.wait_ge(av_ok, n - 3)
                    nc.vector.tensor_copy(pT[:, u, 0:HKT, :], tp[:, :, :].bitcast(I16)).then_inc(ra_ok, 1)
                if t is not None:
                    v_.wait_ge(sa_ok, n + 1)
                    nc.vector.tensor_reduce(top[:, u, 0:1], s_a[u][:, :], AX_X, ALU.max).then_inc(dve, 1)
                if alive(t, h, 2):
                    v_.wait_ge(tb_ok, n - 1)
                    nc.vector.tensor_copy(pT[:, u, HKT:KT, :], tp[:, :, :].bitcast(I16)).then_inc(rb_ok, 1)
                if t is not None:
                    v_.wait_ge(sb_ok, n + 1)
                    nc.vector.tensor_reduce(top[:, u, 1:2], s_b[:, :], AX_X, ALU.max).then_inc(dve, 1)
                    v_.wait_ge(dve, 3 * n + 2)
                    nc.vector.tensor_reduce(top1[:, u:u + 1], top[:, u, :], AX_X, ALU.max).then_inc(dve, 1)
                    v_.wait_ge(dve, 3 * n + 3)
                    if alive(t, h, 2):
                        v_.wait_ge(ea_ok, n - 1)
                    nc.vector.tensor_scalar(bias[:, u:u + 1], top1[:, u:u + 1], q_nstep[:, t, h:h + 1], LN_PMAX,
                                            ALU.mult, ALU.add).then_inc(bias_ok, 1)

            def read_out(t, h, n):
                v_.wait_ge(av_ok, n)
                nc.vector.tensor_copy(o_raw[:, t, :], out[:, :]).then_inc(out_read, 1)

            for h in range(H):
                step(0, h, h)
            with v_.Fori(1, TT) as t:
                for h in range(H):
                    if h == 3:
                        read_out(t - 1, h, t * H)
                    step(t, h, t * H + h)
            for n in range(UNITS, UNITS + 3):
                step(None, n - UNITS, n)
            read_out(TT - 1, 0, UNITS)

        @block.tensor
        def _(pe):
            def transposes(u, half, count):
                for k in range(HKT):
                    key = (half * HKT + k) * P
                    ins = nc.tensor.transpose(tp[:, k, :], p_int[:, u, key:key + P].bitcast(F16), ident16[:, :])
                ins.then_inc(count, 1)

            def step(t, h, n):
                u = h % 2
                if t is not None:
                    if alive(t, h, 2):
                        pe.wait_ge(ea_ok, n - 1)
                    for c in range(2):
                        ins = nc.tensor.matmul(s_a[u][:, c * 512:(c + 1) * 512], q_int[0:3 * D, t, h, :],
                                               k_parts[0:3 * D, h, c * 512:(c + 1) * 512], start=True, stop=True)
                    ins.then_inc(sa_ok, 1)
                if alive(t, h, 2):
                    pe.wait_ge(ea_ok, n - 1)
                    if alive(t, h, 3):
                        pe.wait_ge(rb_ok, n - 2)
                    transposes(u, 0, ta_ok)
                if t is not None:
                    if alive(t, h, 1):
                        pe.wait_ge(eb_ok, n)
                    for c in range(2, 4):
                        ins = nc.tensor.matmul(s_b[:, (c - 2) * 512:(c - 1) * 512], q_int[0:3 * D, t, h, :],
                                               k_parts[0:3 * D, h, c * 512:(c + 1) * 512], start=True, stop=True)
                    ins.then_inc(sb_ok, 1)
                if alive(t, h, 3):
                    head = (h - 3) % H
                    pe.wait_ge(rb_ok, n - 2)
                    if h == 3 and t is not None and not isinstance(t, int):
                        pe.wait_ge(out_read, t)
                    for k in range(KT):
                        ins = nc.tensor.matmul(out[:, head * D:(head + 1) * D], pT[:, (h - 3) % 2, k, :],
                                               v_int[:, k, head * D:(head + 1) * D], start=(k == 0), stop=(k == KT - 1))
                    ins.then_inc(av_ok, 1)
                if alive(t, h, 2):
                    pe.wait_ge(ra_ok, n - 1)
                    transposes(u, 1, tb_ok)

            units(pe, step)


def cross_output(nc, wp_dram, bp_dram, x_res, o_raw, z_sum, v_step, ident):
    with ExitStack() as ctx:
        def sb(name, shape, dt):
            return ctx.enter_context(nc.sbuf_tensor(name, shape, dt))

        def psum(name, shape, dt):
            return ctx.enter_context(nc.psum_tensor(name, shape, dt))

        def sem(name):
            return ctx.enter_context(nc.semaphore("co_" + name))

        w_raw = sb("co_w_raw", [P, CK, C], F32)
        w_hi = sb("co_w_hi", [P, CK, C], F32R)
        w_lo = sb("co_w_lo", [P, CK, C], F32R)
        bias = sb("co_bias", [P, C], F32)
        p_step = sb("co_p_step", [P, TT, H], F32)
        o = sb("co_o", [P, 2, H, D], F32)
        o_hi = sb("co_o_hi", [P, 2, CK, P], F32R)
        o_lo = sb("co_o_lo", [P, 2, CK, P], F32R)
        to = [psum(f"co_to{i}", [P, C], F32) for i in range(2)]
        po = [psum(f"co_po{i}", [P, C], F32) for i in range(2)]
        w_in = sem("w_in")
        b_in = sem("b_in")
        whi_ok = sem("whi_ok")
        wlo_ok = sem("wlo_ok")
        o_ok = sem("o_ok")
        oT_ok = sem("oT_ok")
        ohi_ok = sem("ohi_ok")
        olo_ok = sem("olo_ok")
        y_ok = sem("y_ok")
        y_read = sem("y_read")
        dve = sem("dve")
        block = ctx.enter_context(nc.Block(no_gpsimd_drain=True))

        @block.sync
        def _(sp):
            sp.dma_start(w_raw[:, :, :], wp_dram.rearrange("(k p) n -> p k n", p=P)).then_inc(w_in, 16)
            sp.dma_start(bias[:, :], bp_dram.partition_broadcast(P)).then_inc(b_in, 16)

        @block.scalar
        def _(act):
            act.wait_ge(w_in, 16)
            nc.scalar.copy(w_hi[:, :, :], w_raw[:, :, :]).then_inc(whi_ok, 1)
            with act.Fori(0, TT // 2) as i:
                for t in range(2):
                    act.wait_ge(oT_ok, 2 * i + t + 1)
                    nc.scalar.copy(o_hi[:, t, :, :], row_halves(to[t][:, :], CK)).then_inc(ohi_ok, 1)

        @block.vector
        def _(v_):
            links = [0]

            def link(ins, base=0):
                links[0] += 1
                ins.then_inc(dve, 1)
                v_.wait_ge(dve, base + links[0])

            link(nc.vector.tensor_reduce(p_step[:, :, :], z_sum[:, :, :, :], AX_X, ALU.add))
            link(nc.vector.reciprocal(p_step[:, :, :], p_step[:, :, :]))
            link(nc.vector.tensor_scalar(p_step[:, :, :], p_step[:, :, :], Q_FLOOR, None, ALU.max))
            v_.wait_ge(whi_ok, 1)
            nc.vector.tensor_tensor(w_lo[:, :, :], w_raw[:, :, :], w_hi[:, :, :].bitcast(F32),
                                    ALU.subtract).then_inc(wlo_ok, 1)
            v_.wait_ge(b_in, 16)
            head = links[0]
            LINKS = 2 * 2
            with v_.Fori(0, TT // 2) as i:
                links[0] = 0
                base = head + i * LINKS
                for t in range(2):
                    n = 2 * i + t
                    link(nc.vector.tensor_tensor(o[:, t, :, :], o_raw[:, n, :].rearrange("p (h d) -> p h d", h=H),
                                                 p_step[:, n, :].unsqueeze(2).broadcast_to([P, H, D]), ALU.mult), base)
                    nc.vector.tensor_tensor(o[:, t, :, :].rearrange("p h d -> p (h d)"),
                                            o[:, t, :, :].rearrange("p h d -> p (h d)"), v_step[:, :],
                                            ALU.mult).then_inc(o_ok, 1)
                for t in range(2):
                    n = 2 * i + t
                    v_.wait_ge(ohi_ok, n + 1)
                    nc.vector.tensor_tensor(o_lo[:, t, :, :], row_halves(to[t][:, :], CK), o_hi[:, t, :, :].bitcast(F32),
                                            ALU.subtract).then_inc(olo_ok, 1)
                for t in range(2):
                    n = 2 * i + t
                    link(nc.vector.tensor_tensor(x_res[:, n, :], x_res[:, n, :], bias[:, :], ALU.add), base)
                    v_.wait_ge(y_ok, n + 1)
                    nc.vector.tensor_tensor(x_res[:, n, :], x_res[:, n, :], po[t][:, :], ALU.add).then_inc(y_read, 1)
                assert links[0] == LINKS

        @block.tensor
        def _(pe):
            pe.wait_ge(wlo_ok, 1)
            with pe.Fori(0, TT // 2) as i:
                for t in range(2):
                    pe.wait_ge(o_ok, 2 * i + t + 1)
                    for k in range(CK):
                        ins = nc.tensor.transpose(to[t][:, k * P:(k + 1) * P],
                                                  o[:, t, k * GH:(k + 1) * GH, :].rearrange("p h d -> p (h d)"), ident[:, :])
                    ins.then_inc(oT_ok, 1)
                for t in range(2):
                    pe.wait_ge(olo_ok, 2 * i + t + 1)
                    for k in range(CK):
                        for j, (a, w) in enumerate(((o_hi, w_hi), (o_lo, w_hi), (o_hi, w_lo))):
                            ins = nc.tensor.matmul(po[t][:, :], a[:, t, k, :], w[:, k, :],
                                                   start=(k == 0 and j == 0), stop=(k == CK - 1 and j == 2))
                    ins.then_inc(y_ok, 1)
                pe.wait_ge(y_read, 2 * i + 2)


def cross_attention(nc, wq, bq, ctxT, wkv, bkv, wp, bp, x_res, ident, minus_half, ident16, ident_bf):
    with ExitStack() as ctx:
        def sb(name, shape, dt):
            return ctx.enter_context(nc.sbuf_tensor(name, shape, dt))

        k_parts = sb("k_parts", [3 * D, H, KEYS], BF16)
        v_int = sb("v_int", [P, KT, C], BF16)
        v_step = sb("v_step", [P, C], F32)
        context_keys_values(nc, ctxT, wkv, bkv, k_parts, v_int, v_step, ident_bf)
        q_int = sb("q_int", [3 * D, TT, H, P], BF16)
        q_step = sb("q_step", [P, TT, H], F32)
        q_nstep = sb("q_nstep", [P, TT, H], F32)
        cross_queries(nc, wq, bq, x_res, q_int, q_step, q_nstep, ident, minus_half, ident_bf)
        o_raw = sb("o_raw", [P, TT, C], F32)
        z_sum = sb("z_sum", [P, TT, H, 2], F32)
        cross_scores(nc, k_parts, v_int, q_int, q_step, q_nstep, o_raw, z_sum, ident16)
        cross_output(nc, wp, bp, x_res, o_raw, z_sum, v_step, ident)
E_N, TOP, I_W = 8, 2, 352
ROUTED = E_N * I_W // P
SHARED_W = 2 * I_W
CHUNKS = (E_N * I_W + SHARED_W + P - 1) // P
GROUP = 2
PAIR = 2 * GROUP
HALF_T = TOKENS // 2
LO_ROW = 32


def ffn_gate(nc, gate_dram, x_res, zT_hi, zT_lo, comb, ident, minus_half, rank_dram):
    with ExitStack() as ctx:
        def sb(name, shape, dt):
            return ctx.enter_context(nc.sbuf_tensor(name, shape, dt))

        def psum(name, shape, dt):
            return ctx.enter_context(nc.psum_tensor(name, shape, dt))

        def sem(name):
            return ctx.enter_context(nc.semaphore("fg_" + name))

        g_raw = sb("fg_g_raw", [P, CK, E_N], F32)
        g_hi = sb("fg_g_hi", [P, CK, E_N], F32R)
        g_lo = sb("fg_g_lo", [P, CK, E_N], F32R)
        rank = sb("fg_rank", [P, TT, E_N], F32)
        stats = sb("fg_stats", [P, TT, 6], F32)
        mv = sb("fg_mv", [P, TT, 2], F32)
        ve = sb("fg_ve", [P, TT], F32)
        rstd = sb("fg_rstd", [P, TT], F32)
        z = sb("fg_z", [P, 2, C], F32)
        lg = sb("fg_lg", [P, TT, E_N], F32)
        prob = sb("fg_prob", [P, TT, E_N], F32)
        left = sb("fg_left", [P, TT, E_N], F32)
        hot = sb("fg_hot", [P, TT, E_N], F32)
        w = sb("fg_w", [P, TT, E_N], F32)
        one = sb("fg_one", [P, TT], F32)
        tz = [psum(f"fg_tz{i}", [P, C], F32) for i in range(2)]
        pl = psum("fg_pl", [P, TT, E_N], F32)
        tc = psum("fg_tc", [E_N, TOKENS], F32)

        g_in = sem("g_in")
        r_in = sem("r_in")
        ghi_ok = sem("ghi_ok")
        glo_ok = sem("glo_ok")
        chain = sem("chain")
        ve_ok = sem("ve_ok")
        rstd_ok = sem("rstd_ok")
        z_ok = sem("z_ok")
        zT_ok = sem("zT_ok")
        zhi_ok = sem("zhi_ok")
        zlo_ok = sem("zlo_ok")
        lg_ok = sem("lg_ok")
        sub_ok = sem("sub_ok")
        exp_ok = sem("exp_ok")
        w_ok = sem("w_ok")
        tc_ok = sem("tc_ok")
        chi_ok = sem("chi_ok")
        zero_ok = sem("zero_ok")
        dve = sem("dve")
        block = ctx.enter_context(nc.Block(no_gpsimd_drain=True))

        @block.sync
        def _(sp):
            sp.dma_start(g_raw[:, :, :], gate_dram.rearrange("(k p) e -> p k e", p=P)).then_inc(g_in, 16)
            sp.dma_start(rank[:, :, :].rearrange("p t e -> p (t e)"), rank_dram.partition_broadcast(P)).then_inc(r_in, 16)

        @block.gpsimd
        def _(pool):
            nc.gpsimd.memset(comb[:, :].bitcast(F32), 0.0).then_inc(zero_ok, 1)
            pool.wait_ge(ve_ok, 1)
            nc.gpsimd.tensor_tensor(rstd[:, :], ve[:, :], minus_half[:, 0:TT], ALU.pow).then_inc(rstd_ok, 1)

        @block.scalar
        def _(act):
            act.wait_ge(g_in, 16)
            nc.scalar.copy(g_hi[:, :, :], g_raw[:, :, :]).then_inc(ghi_ok, 1)
            for t in range(TT):
                act.wait_ge(zT_ok, t + 1)
                nc.scalar.copy(zT_hi[:, :, t * P:(t + 1) * P], row_halves(tz[t % 2][:, :], CK)).then_inc(zhi_ok, 1)
            act.wait_ge(sub_ok, 1)
            nc.scalar.activation(lg[:, :, :], lg[:, :, :], ACT.Exp).then_inc(exp_ok, 1)
            act.wait_ge(tc_ok, 1)
            act.wait_ge(zero_ok, 1)
            nc.scalar.copy(comb[0:E_N, :], tc[:, :]).then_inc(chi_ok, 1)

        @block.vector
        def _(v_):
            links = [0]

            def link(ins):
                links[0] += 1
                ins.then_inc(dve, 1)
                v_.wait_ge(dve, links[0])

            normalise_statistics(v_, None, nc, x_res, stats, mv, ve, rstd, minus_half, chain, ve_ok, rstd_ok)
            v_.wait_ge(ghi_ok, 1)
            nc.vector.tensor_tensor(g_lo[:, :, :], g_raw[:, :, :], g_hi[:, :, :].bitcast(F32), ALU.subtract).then_inc(glo_ok, 1)
            v_.wait_ge(rstd_ok, 1)

            def norm(t):
                if t >= 2:
                    v_.wait_ge(zT_ok, t - 1)
                nc.vector.tensor_scalar(z[:, t % 2, :], x_res[:, t, :], mv[:, t, 0:1], rstd[:, t:t + 1],
                                        ALU.subtract, ALU.mult).then_inc(z_ok, 1)
            norm(0)
            for t in range(TT):
                if t + 1 < TT:
                    norm(t + 1)
                v_.wait_ge(zhi_ok, t + 1)
                nc.vector.tensor_tensor(zT_lo[:, :, t * P:(t + 1) * P], row_halves(tz[t % 2][:, :], CK),
                                        zT_hi[:, :, t * P:(t + 1) * P].bitcast(F32), ALU.subtract).then_inc(zlo_ok, 1)

            def across(x):
                return x[:, :].unsqueeze(2).broadcast_to([P, TT, E_N])

            v_.wait_ge(lg_ok, TT)
            link(nc.vector.tensor_reduce(one[:, :], pl[:, :, :], AX_X, ALU.max))
            nc.vector.tensor_tensor(lg[:, :, :], pl[:, :, :], across(one), ALU.subtract).then_inc(sub_ok, 1)
            v_.wait_ge(exp_ok, 1)
            link(nc.vector.tensor_reduce(one[:, :], lg[:, :, :], AX_X, ALU.add))
            link(nc.vector.reciprocal(one[:, :], one[:, :]))
            link(nc.vector.tensor_tensor(prob[:, :, :], lg[:, :, :], across(one), ALU.mult))
            link(nc.vector.tensor_copy(left[:, :, :], prob[:, :, :]))
            v_.wait_ge(r_in, 16)
            for k in range(TOP):
                link(nc.vector.tensor_reduce(one[:, :], left[:, :, :], AX_X, ALU.max))
                link(nc.vector.tensor_tensor(hot[:, :, :], left[:, :, :], across(one), ALU.is_equal))
                link(nc.vector.tensor_tensor(hot[:, :, :], hot[:, :, :], rank[:, :, :], ALU.mult))
                link(nc.vector.tensor_reduce(one[:, :], hot[:, :, :], AX_X, ALU.max))
                link(nc.vector.tensor_tensor(hot[:, :, :], hot[:, :, :], across(one), ALU.is_equal))
                link(nc.vector.scalar_tensor_tensor(out=left[:, :, :], in0=hot[:, :, :], scalar=-2.0,
                                                    in1=left[:, :, :], op0=ALU.mult, op1=ALU.add))
            link(nc.vector.tensor_scalar(hot[:, :, :], left[:, :, :], -0.5, None, ALU.is_lt))
            nc.vector.tensor_tensor(w[:, :, :], hot[:, :, :], prob[:, :, :], ALU.mult).then_inc(w_ok, 1)
            v_.wait_ge(chi_ok, 1)
            link(nc.vector.tensor_tensor(comb[LO_ROW:LO_ROW + E_N, :], tc[:, :], comb[0:E_N, :].bitcast(F32), ALU.subtract))

        @block.tensor
        def _(pe):
            pe.wait_ge(glo_ok, 1)

            def gate(t):
                pe.wait_ge(zlo_ok, t + 1)
                for k in range(CK):
                    for j, (a, g) in enumerate(((zT_hi, g_hi), (zT_lo, g_hi), (zT_hi, g_lo))):
                        ins = nc.tensor.matmul(pl[:, t, :], a[:, k, t * P:(t + 1) * P], g[:, k, :],
                                               start=(k == 0 and j == 0), stop=(k == CK - 1 and j == 2))
                ins.then_inc(lg_ok, 1)

            for t in range(TT):
                pe.wait_ge(z_ok, t + 1)
                if t >= 2:
                    pe.wait_ge(zlo_ok, t - 1)
                for k in range(CK):
                    ins = nc.tensor.transpose(tz[t % 2][:, k * P:(k + 1) * P], z[:, t % 2, k * P:(k + 1) * P], ident[:, :])
                ins.then_inc(zT_ok, 1)
                if t >= 1:
                    gate(t - 1)
            gate(TT - 1)
            pe.wait_ge(w_ok, 1)
            for t in range(TT):
                ins = nc.tensor.transpose(tc[:, t * P:(t + 1) * P], w[:, t, :], ident[:, :])
            ins.then_inc(tc_ok, 1)


def ffn_hidden(nc, w_dram, sel_dram, out_dram, x_res, zT_hi, zT_lo, comb):
    with ExitStack() as ctx:
        def sb(name, shape, dt):
            return ctx.enter_context(nc.sbuf_tensor(name, shape, dt))

        def psum(name, shape, dt):
            return ctx.enter_context(nc.psum_tensor(name, shape, dt))

        def sem(name):
            return ctx.enter_context(nc.semaphore("fh_" + name))

        raw = sb("fh_raw", [P, PAIR, 3 * C], F32)
        up_hi = sb("fh_up_hi", [P, 2, 2, CK, P], F32R)
        up_lo = sb("fh_up_lo", [P, 2, 2, CK, P], F32R)
        dn_hi = sb("fh_dn_hi", [P, PAIR, C], F32R)
        dn_lo = sb("fh_dn_lo", [P, PAIR, C], F32R)
        h_hi = sb("fh_h_hi", [P, PAIR, TOKENS], F32R)
        h_lo = sb("fh_h_lo", [P, PAIR, TOKENS], F32R)
        act_s = sb("fh_s", [P, 2, HALF_T], F32)
        g = sb("fh_g", [P, 2, HALF_T], F32)
        sel_raw = sb("fh_sel_raw", [2 * LO_ROW, ROUTED * P], F32)
        sel = sb("fh_sel", [2 * LO_ROW, 2, P], F32R)
        h1 = [psum(f"fh_h1{i}", [P, HALF_T], F32) for i in range(2)]
        h2 = [psum(f"fh_h2{i}", [P, HALF_T], F32) for i in range(2)]
        pc = [psum(f"fh_pc{i}", [P, HALF_T], F32) for i in range(2)]
        py = [psum(f"fh_py{i}", [P, C], F32) for i in range(2)]

        sel_in = sem("sel_in")
        w_in = [sem(f"w_in{i}") for i in range(PAIR)]
        uhi_ok = sem("uhi_ok")
        ulo_ok = sem("ulo_ok")
        dhi_ok = sem("dhi_ok")
        dlo_ok = sem("dlo_ok")
        h1_ok = sem("h1_ok")
        h2_ok = sem("h2_ok")
        s_ok = sem("s_ok")
        g1_ok = sem("g1_ok")
        g_ok = sem("g_ok")
        hhi_ok = sem("hhi_ok")
        hlo_ok = sem("hlo_ok")
        y_ok = sem("y_ok")
        y_read = sem("y_read")
        stored = sem("stored")
        block = ctx.enter_context(nc.Block(no_gpsimd_drain=True))
        PAIRS = CHUNKS // PAIR
        ROUTED_PAIRS = ROUTED // PAIR
        assert CHUNKS % PAIR == 0

        def turns(engine, turn):
            turn(0, PAIR)
            with engine.Fori(1, ROUTED_PAIRS) as p:
                turn(p, PAIR)
            for p in range(ROUTED_PAIRS, PAIRS):
                turn(p, max(0, ROUTED - PAIR * p))

        def before(p, j, n):
            return not (isinstance(p, int) and PAIR * p + j < n)

        def last(p, j):
            return isinstance(p, int) and PAIR * p + j == CHUNKS - 1

        @block.sync
        def _(sp):
            sp.dma_start(sel_raw[:, :], sel_dram).then_inc(sel_in, 16)

            def turn(p, routed):
                for j in range(PAIR):
                    if before(p, j, PAIR):
                        sp.wait_ge(dlo_ok, PAIR * p + j + 1 - PAIR)
                    sp.dma_start(raw[:, j, :], w_dram[bass.ds(PAIR * p + j, 1), :, :].rearrange("a p n -> p (a n)"))\
                      .then_inc(w_in[j], 16)
            turns(sp, turn)
            sp.wait_ge(y_read, TT * PAIRS * 2)
            sp.dma_start(out_dram.rearrange("(t p) c -> p t c", p=P), x_res[:, :, :]).then_inc(stored, 16)
            sp.wait_ge(stored, 16)

        @block.scalar
        def _(act):
            def split_up(p, j, routed):
                act.wait_ge(w_in[j], 16 * (p + 1))
                if before(p, j, 2):
                    act.wait_ge(h2_ok, 2 * (PAIR * p + j) - 2)
                if routed:
                    nc.scalar.copy(sel[:, j % 2, :], sel_raw[:, bass.ds((PAIR * p + j) * P, P)])
                nc.scalar.copy(up_hi[:, j % 2, :, :, :].rearrange("p a k n -> p (a k n)"),
                               raw[:, j, 0:2 * C]).then_inc(uhi_ok, 1)

            def turn(p, routed):
                for j in range(PAIR):
                    c = PAIR * p + j
                    if j + 1 < PAIR:
                        split_up(p, j + 1, j + 1 < routed)
                    elif not last(p, j):
                        split_up(p + 1, 0, not (isinstance(p, int) and PAIR * (p + 1) >= ROUTED))
                    for b in range(2):
                        act.wait_ge(h1_ok, 2 * c + b + 1)
                        nc.scalar.activation(act_s[:, b, :], h1[b][:, :], ACT.Silu).then_inc(s_ok, 1)
                        act.wait_ge(g_ok, 2 * c + b + 1)
                        if before(p, j, PAIR) and b == 0 and j % GROUP == 0:
                            act.wait_ge(y_ok, TT * (2 * p + j // GROUP - 1))
                        nc.scalar.copy(h_hi[:, j, b * HALF_T:(b + 1) * HALF_T], g[:, b, :]).then_inc(hhi_ok, 1)
                    nc.scalar.copy(dn_hi[:, j, :], raw[:, j, 2 * C:3 * C]).then_inc(dhi_ok, 1)

            act.wait_ge(sel_in, 16)
            split_up(0, 0, True)
            turns(act, turn)

        @block.gpsimd
        def _(pool):
            def split_up(p, j):
                pool.wait_ge(uhi_ok, PAIR * p + j + 1)
                nc.gpsimd.tensor_tensor(up_lo[:, j % 2, :, :, :].rearrange("p a k n -> p (a k n)"), raw[:, j, 0:2 * C],
                                        up_hi[:, j % 2, :, :, :].rearrange("p a k n -> p (a k n)").bitcast(F32),
                                        ALU.subtract).then_inc(ulo_ok, 1)

            def turn(p, routed):
                for j in range(PAIR):
                    c = PAIR * p + j
                    if j + 1 < PAIR:
                        split_up(p, j + 1)
                    elif not last(p, j):
                        split_up(p + 1, 0)
                    for b in range(2):
                        pool.wait_ge(hhi_ok, 2 * c + b + 1)
                        nc.gpsimd.tensor_tensor(h_lo[:, j, b * HALF_T:(b + 1) * HALF_T], g[:, b, :],
                                                h_hi[:, j, b * HALF_T:(b + 1) * HALF_T].bitcast(F32),
                                                ALU.subtract).then_inc(hlo_ok, 1)
                    pool.wait_ge(dhi_ok, c + 1)
                    nc.gpsimd.tensor_tensor(dn_lo[:, j, :], raw[:, j, 2 * C:3 * C], dn_hi[:, j, :].bitcast(F32),
                                            ALU.subtract).then_inc(dlo_ok, 1)

            split_up(0, 0)
            turns(pool, turn)

        @block.vector
        def _(v_):
            def add_y(group):
                for t in range(TT):
                    v_.wait_ge(y_ok, TT * group + t + 1)
                    nc.vector.tensor_tensor(x_res[:, t, :], x_res[:, t, :], py[t % 2][:, :], ALU.add).then_inc(y_read, 1)

            def turn(p, routed):
                for j in range(PAIR):
                    c = PAIR * p + j
                    for b in range(2):
                        v_.wait_ge(s_ok, 2 * c + b + 1)
                        v_.wait_ge(h2_ok, 2 * c + b + 1)
                        if before(p, j, 1):
                            v_.wait_ge(hlo_ok, 2 * c + b - 1)
                        ins = nc.vector.tensor_tensor(g[:, b, :], act_s[:, b, :], h2[b][:, :], ALU.mult)
                        if j < routed:
                            ins.then_inc(g1_ok, 1)
                            v_.wait_ge(g1_ok, 2 * c + b + 1)
                            ins = nc.vector.tensor_tensor(g[:, b, :], g[:, b, :], pc[b][:, :], ALU.mult)
                        ins.then_inc(g_ok, 1)
                    if j == GROUP - 1 and before(p, j, PAIR):
                        add_y(2 * p - 1)
                    if j == PAIR - 1:
                        add_y(2 * p)
            turns(v_, turn)
            add_y(2 * PAIRS - 1)

        @block.tensor
        def _(pe):
            def hidden(p, j, routed):
                c = PAIR * p + j
                pe.wait_ge(ulo_ok, c + 1)
                for b in range(2):
                    if before(p, j, 1):
                        pe.wait_ge(g_ok, 2 * c + b - 1)
                    cols = slice(b * HALF_T, (b + 1) * HALF_T)
                    for m, (out, made) in enumerate(((h1, h1_ok), (h2, h2_ok))):
                        if m and routed:
                            nc.tensor.matmul(pc[b][:, :], sel[:, j % 2, :], comb[:, cols], start=True, stop=True)
                        for k in range(CK):
                            for i, (w, zz) in enumerate(((up_hi, zT_hi), (up_lo, zT_hi), (up_hi, zT_lo))):
                                ins = nc.tensor.matmul(out[b][:, :], w[:, j % 2, m, k, :], zz[:, k, cols],
                                                       start=(k == 0 and i == 0), stop=(k == CK - 1 and i == 2))
                        ins.then_inc(made, 1)

            def down(group, u):
                pe.wait_ge(hlo_ok, 2 * GROUP * (group + 1))
                pe.wait_ge(dlo_ok, GROUP * (group + 1))
                for t in range(TT):
                    if not (isinstance(group, int) and group == 0 and t < 2):
                        pe.wait_ge(y_read, TT * group + t - 1)
                    for q in range(GROUP):
                        j = u * GROUP + q
                        tile = slice(t * P, (t + 1) * P)
                        for i, (hh, w) in enumerate(((h_hi, dn_hi), (h_lo, dn_hi), (h_hi, dn_lo))):
                            ins = nc.tensor.matmul(py[t % 2][:, :], hh[:, j, tile], w[:, j, :],
                                                   start=(q == 0 and i == 0), stop=(q == GROUP - 1 and i == 2))
                    ins.then_inc(y_ok, 1)

            def turn(p, routed):
                for j in range(PAIR):
                    hidden(p, j, j < routed)
                    if j == GROUP - 1 and before(p, j, PAIR):
                        down(2 * p - 1, 1)
                    if j == PAIR - 1:
                        down(2 * p, 0)
            turns(pe, turn)
            down(2 * PAIRS - 1, 1)


def feed_forward(nc, gate, rank, weights, sel, out, x_res, ident, minus_half):
    with ExitStack() as ctx:
        def sb(name, shape, dt):
            return ctx.enter_context(nc.sbuf_tensor(name, shape, dt))

        zT_hi = sb("zT_hi", [P, CK, TOKENS], F32R)
        zT_lo = sb("zT_lo", [P, CK, TOKENS], F32R)
        comb = sb("comb", [2 * LO_ROW, TOKENS], F32R)
        ffn_gate(nc, gate, x_res, zT_hi, zT_lo, comb, ident, minus_half, rank)
        ffn_hidden(nc, weights, sel, out, x_res, zT_hi, zT_lo, comb)
def decoder_layer(nc, x, ctxT, wq, wk, wv, wo, gamma, beta, cwq, cbq, cwkv, cbkv, cwp, cbp, gate, rank, weights, sel, out):
    with ExitStack() as ctx:
        x_res, (ident, mask, minus_half, ident16, ident_bf) = constants(nc, ctx)
        self_attention(nc, x, (wq, wk, wv, wo), gamma, beta, x_res, ident, mask, minus_half)
        cross_attention(nc, cwq, cbq, ctxT, cwkv, cbkv, cwp, cbp, x_res, ident, minus_half, ident16, ident_bf)
        feed_forward(nc, gate, rank, weights, sel, out, x_res, ident, minus_half)


def _arrays(inputs):
    import numpy as np

    def f(name):
        return np.asarray(inputs[name])

    a = {
        "x": f("x").reshape(TOKENS, C),
        "ctxT": f("ctx_2048").reshape(KEYS, C).T,
        "wq": f("L0_attn_Wq").T, "wk": f("L0_attn_Wk").T, "wv": f("L0_attn_Wv").T, "wo": f("L0_attn_Wo").T,
        "gamma": np.tile(f("L0_attn_gamma"), H)[None], "beta": np.tile(f("L0_attn_beta"), H)[None],
        "cwq": f("L0_xattn_Wq"), "cbq": f("L0_xattn_bq")[None],
        "cwkv": f("L0_xattn_Wkv"), "cbkv": f("L0_xattn_bkv")[None],
        "cwp": f("L0_xattn_Wp"), "cbp": f("L0_xattn_bp")[None],
        "gate": f("L0_ffn_gate_w").T,
        "rank": np.tile(np.arange(E_N, 0, -1, dtype=np.float32), TT)[None],
    }
    pad = CHUNKS * P - E_N * I_W - SHARED_W

    def rows(routed, shared):
        return np.concatenate([routed, shared, np.zeros((pad, C), np.float32)]).reshape(CHUNKS, P, C)

    up = [rows(f(f"L0_ffn_{r}").reshape(-1, C), f(f"L0_ffn_{s}")).reshape(CHUNKS, P, CK, P).transpose(0, 3, 2, 1)
          .reshape(CHUNKS, P, C) for r, s in (("w1", "sw1"), ("w2", "sw2"))]
    down = rows(f("L0_ffn_w3").transpose(0, 2, 1).reshape(-1, C), f("L0_ffn_sw3").T)
    a["weights"] = np.concatenate([*up, down], axis=2)
    one_hot = (np.arange(ROUTED * P)[None] // I_W == np.arange(E_N)[:, None]).astype(np.float32)
    a["sel"] = np.zeros((2 * LO_ROW, ROUTED * P), np.float32)
    a["sel"][0:E_N] = one_hot
    a["sel"][LO_ROW:LO_ROW + E_N] = one_hot
    return {n: np.ascontiguousarray(v) for n, v in a.items()}


def kernel(**inputs):
    import numpy as _np
    import concourse.bacc as _bacc
    from concourse.bass_utils import run_bass_kernel_spmd as _run

    nc = _bacc.Bacc("TRN2", target_bir_lowering=False, num_devices=1)
    arrays, args = {}, []
    for name, a in _arrays(inputs).items():
        arrays[f"in_{name}_dram"] = a
        args.append(nc.dram_tensor(f"in_{name}_dram", a.shape, mybir.dt.from_np(a.dtype), kind="ExternalInput").ap())
    args.append(nc.dram_tensor("out_dram", (TOKENS, C), F32, kind="ExternalOutput").ap())
    decoder_layer(nc, *args)
    r = _run(nc, [arrays], core_ids=[0])
    return r.results[0]["out_dram"].reshape(B, S, C)
```

```python
from contextlib import ExitStack

import concourse.bass as bass
from concourse import mybir

F32 = mybir.dt.float32
F32R = mybir.dt.float32r
F16 = mybir.dt.float16
BF16 = mybir.dt.bfloat16
I16 = mybir.dt.int16
ALU = mybir.AluOpType
ACT = mybir.ActivationFunctionType
AX_X = mybir.AxisListType.X
ABSMAX = bass.bass_isa.ReduceOp.absmax

P = 128
B, S, C = 2, 512, 512
TOKENS = B * S
TT = TOKENS // P
H, D = 16, 32
CK = C // P
HG = C // P
GH = P // D
BT = S // P
KEYS = 2 * 1024
KT = KEYS // P
LN_EPS = 1e-05
ATT_EPS = 1e-05
MAGIC = 12582912.0
QMAX = 127.0
PMAX = 255.0
Q_FLOOR = 1e-08


def row_halves(ap, n):
    return ap.rearrange("p (n w) -> p n w", n=n)
def constants(nc, ctx):
    def sb(name, shape, dt):
        return ctx.enter_context(nc.sbuf_tensor(name, shape, dt))

    x_res = sb("x_res", [P, TT, C], F32)
    ident = sb("ident", [P, P], F32)
    ident16 = sb("ident16", [P, P], F16)
    ident_bf = sb("ident_bf", [P, P], BF16)
    mask = sb("mask", [P, P], F32)
    minus_half = sb("minus_half", [P, 2 * H], F32)
    made = ctx.enter_context(nc.semaphore("const_made"))
    with nc.Block(no_gpsimd_drain=True) as block:
        @block.gpsimd
        def _(pool):
            nc.gpsimd.memset(minus_half[:, :], -0.5)
            nc.gpsimd.memset(ident[:, :], 0.0).then_inc(made, 1)
            nc.gpsimd.memset(mask[:, :], 1.0).then_inc(made, 1)
            pool.wait_ge(made, 2)
            nc.gpsimd.affine_select(out=ident[:, :], in_=ident[:, :], compare_op=ALU.not_equal, fill=1.0, base=0,
                                    pattern=[[-1, P]], channel_multiplier=1).then_inc(made, 1)
            nc.gpsimd.affine_select(out=mask[:, :], in_=mask[:, :], compare_op=ALU.is_ge, fill=0.0, base=0,
                                    pattern=[[1, P]], channel_multiplier=-1).then_inc(made, 1)
            pool.wait_ge(made, 4)
            nc.gpsimd.tensor_copy(ident16[:, :], ident[:, :]).then_inc(made, 1)
            nc.gpsimd.tensor_copy(ident_bf[:, :], ident[:, :]).then_inc(made, 1)
            pool.wait_ge(made, 6)
    return x_res, (ident, mask, minus_half, ident16, ident_bf)
TURNS = [("z", 0), ("z", 1), ("z", 2), ("q", 0), ("k", 0), ("z", 3), ("q", 1), ("k", 1), ("q", 2), ("k", 2), ("q", 3), ("k", 3)]


def turn_bank(what, t):
    return TURNS.index((what, t)) % 2


def self_attention(nc, x_dram, w_dram, gamma_dram, beta_dram, x_res, ident, mask, minus_half):
    with ExitStack() as ctx:
        def sb(name, shape, dt):
            return ctx.enter_context(nc.sbuf_tensor(name, shape, dt))

        def psum(name, shape, dt):
            return ctx.enter_context(nc.psum_tensor(name, shape, dt))

        def sem(name):
            return ctx.enter_context(nc.semaphore("sa_" + name))

        w_hi = sb("sa_w_hi", [P, 4, CK, C], F32R)
        w_lo = sb("sa_w_lo", [P, 4, CK, C], F32R)
        att = sb("sa_att", [P, BT, GH, S], F32)
        w_raw = att[:, :, :, :]
        gam = sb("sa_gam", [P, C], F32)
        bet = sb("sa_bet", [P, C], F32)
        stats = sb("sa_stats", [P, 2, 6], F32)
        mv = sb("sa_mv", [P, TT, 2], F32)
        ve = sb("sa_ve", [P, TT], F32)
        rstd = sb("sa_rstd", [P, TT], F32)
        z = sb("sa_z", [P, 2, C], F32)
        z_hi = sb("sa_z_hi", [P, 2, CK, P], F32R)
        z_lo = sb("sa_z_lo", [P, 2, CK, P], F32R)
        y = sb("sa_y", [P, 2, 2 * H, D], F32)
        sq = sb("sa_sq", [P, 2, 2 * H, D], F32)
        msum = sb("sa_msum", [P, 2, 2 * H], F32)
        vsum = sb("sa_vsum", [P, 2, 2 * H], F32)
        root = sb("sa_root", [P, 2, 2 * H], F32)
        rsq = sb("sa_rsq", [P, 2, 2 * H], F32)
        qT = sb("sa_qT", [P, HG, S], F32)
        kT = sb("sa_kT", [P, HG, S], F32)
        kz = sb("sa_kz", [P, 2, GH, S], F32)
        v = sb("sa_v", [P, BT, C], F32)
        ones = sb("sa_ones", [P, D], F32)
        eps = sb("sa_eps", [P, 2], F32)
        rec = sb("sa_rec", [P, S], F32)
        oT_hi = sb("sa_oT_hi", [P, HG, S], F32R)
        oT_lo = sb("sa_oT_lo", [P, HG, S], F32R)
        o32 = sb("sa_o32", [P, S], F32)

        tb = [psum(f"sa_tb{i}", [P, 512], F32) for i in range(2)]
        pj = [psum(f"sa_pj{i}", [P, 512], F32) for i in range(2)]
        sc = [psum(f"sa_sc{i}", [P, 512], F32) for i in range(GH)]
        nd = [(pj[0], pj[1]), (tb[0], tb[1])]

        x_in = [sem(f"x_in{b}") for b in range(B)]
        gb_in = sem("gb_in")
        w_in = [sem(f"w_in{m}") for m in range(4)]
        gamma_q_ok = sem("gamma_q_ok")
        gamma_k_ok = sem("gamma_k_ok")
        lo_q_ok = sem("lo_q_ok")
        wo_hi_ok = sem("wo_hi_ok")
        w_hi_ok = sem("w_hi_ok")
        w_split = sem("w_split")
        ones_ok = sem("ones_ok")
        dve = sem("dve")
        ve_ok = sem("ve_ok")
        rstd_ok = sem("rstd_ok")
        z_ok = sem("z_ok")
        zT_ok = sem("zT_ok")
        zhi_ok = sem("zhi_ok")
        zlo_ok = sem("zlo_ok")
        qkv_ok = sem("qkv_ok")
        qk_read = sem("qk_read")
        v_read = sem("v_read")
        c_ok = sem("c_ok")
        sq_ok = sem("sq_ok")
        vs_ok = sem("vs_ok")
        root_ok = sem("root_ok")
        n_ok = sem("n_ok")
        qkT_ok = sem("qkT_ok")
        qkT_read = sem("qkT_read")
        zeros_ok = sem("zeros_ok")
        kz_ok = sem("kz_ok")
        s_ok = sem("s_ok")
        att_ok = sem("att_ok")
        masked = sem("masked")
        av_ok = sem("av_ok")
        o32_ok = sem("o32_ok")
        ohi_ok = sem("ohi_ok")
        olo_ok = sem("olo_ok")
        out_ok = sem("out_ok")
        out_read = sem("out_read")

        block = ctx.enter_context(nc.Block(no_gpsimd_drain=True))
        x_tiles = x_dram.rearrange("(t p) c -> p t c", p=P)

        @block.sync
        def _(sp):
            def load_x(b):
                sp.dma_start(x_res[:, BT * b:BT * (b + 1), :], x_tiles[:, BT * b:BT * (b + 1), :]).then_inc(x_in[b], 16)

            def load_w(m):
                sp.dma_start(w_raw[:, m, :, :], w_dram[m].rearrange("(k p) n -> p k n", p=P)).then_inc(w_in[m], 16)
            load_x(0)
            sp.dma_start(gam[:, :], gamma_dram.partition_broadcast(P)).then_inc(gb_in, 16)
            sp.dma_start(bet[:, :], beta_dram.partition_broadcast(P)).then_inc(gb_in, 16)
            load_w(0)
            load_x(1)
            load_w(1)
            load_w(2)
            load_w(3)

        @block.gpsimd
        def _(pool):
            pool.memset(ones[:, :], 1.0).then_inc(ones_ok, 1)
            pool.memset(eps[:, 0:1], ATT_EPS * D).then_inc(zeros_ok, 1)
            pool.memset(eps[:, 1:2], ATT_EPS).then_inc(zeros_ok, 1)
            pool.memset(kz[:, :, :, :], 0.0).then_inc(zeros_ok, 1)
            def power(b):
                pool.wait_ge(ve_ok, b + 1)
                tiles = slice(BT * b, BT * (b + 1))
                pool.tensor_tensor(rstd[:, tiles], ve[:, tiles], minus_half[:, 0:BT], ALU.pow).then_inc(rstd_ok, 1)
            power(0)
            pool.wait_ge(gb_in, 32)
            pool.wait_ge(w_in[1], 16)
            pool.tensor_tensor(w_raw[:, 1, :, :], w_raw[:, 1, :, :], gam[:, :].unsqueeze(1).broadcast_to([P, CK, C]),
                               ALU.mult).then_inc(gamma_k_ok, 1)
            for m in (1, 2, 3):
                if m < 3:
                    pool.wait_ge(w_hi_ok, m + 1)
                else:
                    power(1)
                    pool.wait_ge(w_in[m], 16)
                    pool.tensor_copy(w_hi[:, m, :, :], w_raw[:, m, :, :]).then_inc(wo_hi_ok, 1)
                    pool.wait_ge(wo_hi_ok, 1)
                pool.tensor_tensor(w_lo[:, m, :, :], w_raw[:, m, :, :], w_hi[:, m, :, :].bitcast(F32),
                                   ALU.subtract).then_inc(w_split, 1)
            with pool.Fori(0, B) as b:
                for hg in range(HG):
                    for kt in range(BT):
                        diag = att[:, kt, :, kt * P:(kt + 1) * P]
                        pool.wait_ge(att_ok, (b * HG * BT + hg * BT + kt + 1) * GH)
                        pool.tensor_tensor(diag, diag, mask[:, :].unsqueeze(1).broadcast_to([P, GH, P]),
                                           ALU.mult).then_inc(masked, 1)

        @block.scalar
        def _(act):
            act.wait_ge(zeros_ok, 3)
            for m in range(3):
                act.wait_ge(*((gamma_q_ok, 1), (gamma_k_ok, 1), (w_in[2], 16))[m])
                nc.scalar.copy(w_hi[:, m, :, :], w_raw[:, m, :, :]).then_inc(w_hi_ok, 1)

            def read_z(b, t):
                n = BT * b + t
                act.wait_ge(zT_ok, n + 1)
                nc.scalar.copy(row_halves(z_hi[:, t % 2, :, :].rearrange("p k n -> p (k n)"), CK),
                               row_halves(tb[turn_bank("z", t)][:, :], CK)).then_inc(zhi_ok, 1)

            def read_qkT(b, t):
                n = BT * b + t
                for i, (what, dst) in enumerate((("q", qT), ("k", kT))):
                    act.wait_ge(qkT_ok, 2 * n + i + 1)
                    nc.scalar.copy(dst[:, :, t * P:(t + 1) * P],
                                   row_halves(tb[turn_bank(what, t)][:, :], HG)).then_inc(qkT_read, 1)

            with act.Fori(0, B) as b:
                read_z(b, 0)
                for t in range(BT):
                    n = BT * b + t
                    if t + 1 < BT:
                        read_z(b, t + 1)
                    act.wait_ge(qkv_ok, 3 * n + 3)
                    nc.scalar.copy(v[:, t, :], pj[(3 * t + 2) % 2][:, :]).then_inc(v_read, 1)
                    act.wait_ge(c_ok, n + 1)
                    nc.scalar.activation(sq[:, t % 2, :, :], y[:, t % 2, :, :], ACT.Square).then_inc(sq_ok, 1)
                    act.wait_ge(vs_ok, n + 1)
                    nc.scalar.activation(root[:, t % 2, 0:H], vsum[:, t % 2, 0:H], ACT.Sqrt, bias=eps[:, 0:1])
                    nc.scalar.activation(root[:, t % 2, H:2 * H], vsum[:, t % 2, H:2 * H], ACT.Sqrt, bias=eps[:, 1:2],
                                         scale=1.0 / D).then_inc(root_ok, 1)
                    if t >= 1:
                        read_qkT(b, t - 1)
                read_qkT(b, BT - 1)
                act.wait_ge(w_split, 3)
                def high_out(hg):
                    act.wait_ge(o32_ok, b * HG + hg + 1)
                    nc.scalar.copy(oT_hi[:, hg, :], o32[:, :]).then_inc(ohi_ok, 1)

                for hg in range(HG):
                    for kt in range(BT):
                        if hg > 0:
                            act.wait_ge(av_ok, (b * HG + hg - 1) * BT + kt + 1)
                        for j in range(GH):
                            act.wait_ge(s_ok, ((b * HG + hg) * BT + kt) * GH + j + 1)
                            nc.scalar.activation(att[:, kt, j, kt * P:S], sc[j][:, kt * P:S],
                                                 ACT.Square).then_inc(att_ok, 1)
                    if hg > 0:
                        high_out(hg - 1)
                high_out(HG - 1)

        @block.vector
        def _(v_):
            links = [0]

            def link(ins, base=0):
                links[0] += 1
                ins.then_inc(dve, 1)
                v_.wait_ge(dve, base + links[0])

            def statistics(b):
                v_.wait_ge(x_in[b], 16)
                for t in range(BT * b, BT * (b + 1)):
                    link(nc.vector.bn_stats(stats[:, t % 2, :], x_res[:, t, :]))
                    link(nc.vector.bn_aggr(mv[:, t, :], stats[:, t % 2, :]))
                tiles = slice(BT * b, BT * (b + 1))
                nc.vector.tensor_scalar(ve[:, tiles], mv[:, tiles, 1], LN_EPS, None, ALU.add).then_inc(ve_ok, 1)

            statistics(0)
            v_.wait_ge(gb_in, 32)
            v_.wait_ge(w_in[0], 16)
            nc.vector.tensor_tensor(w_raw[:, 0, :, :], w_raw[:, 0, :, :],
                                    gam[:, :].unsqueeze(1).broadcast_to([P, CK, C]), ALU.mult).then_inc(gamma_q_ok, 1)
            statistics(1)
            v_.wait_ge(w_hi_ok, 1)
            nc.vector.tensor_tensor(w_lo[:, 0, :, :], w_raw[:, 0, :, :], w_hi[:, 0, :, :].bitcast(F32),
                                    ALU.subtract).then_inc(lo_q_ok, 1)
            v_.wait_ge(zeros_ok, 3)
            head = links[0]
            LINKS = 2 * BT + 2 * HG

            with v_.Fori(0, B) as b:
                links[0] = 0
                base = head + b * LINKS

                def norm(t):
                    n = BT * b + t
                    if t >= 2:
                        v_.wait_ge(zT_ok, n - 1)
                    nc.vector.tensor_scalar(z[:, t % 2, :], x_res[:, n, :], mv[:, n, 0:1], rstd[:, bass.ds(n, 1)],
                                            ALU.subtract, ALU.mult).then_inc(z_ok, 1)

                def low_z(t):
                    n = BT * b + t
                    v_.wait_ge(zhi_ok, n + 1)
                    nc.vector.tensor_tensor(z_lo[:, t % 2, :, :], row_halves(tb[turn_bank("z", t)][:, :], CK),
                                            z_hi[:, t % 2, :, :].bitcast(F32), ALU.subtract).then_inc(zlo_ok, 1)

                def add_beta(t):
                    n = BT * b + t
                    for i in range(2):
                        v_.wait_ge(qkv_ok, 3 * n + i + 1)
                        nc.vector.tensor_tensor(y[:, t % 2, i * H:(i + 1) * H, :].rearrange("p h d -> p (h d)"),
                                                pj[(3 * t + i) % 2][:, :], bet[:, :], ALU.add).then_inc(qk_read, 1)

                def variances(t):
                    n = BT * b + t
                    v_.wait_ge(qk_read, 2 * n + 2)
                    link(nc.vector.tensor_reduce(msum[:, t % 2, :], y[:, t % 2, :, :], AX_X, ALU.add), base)
                    nc.vector.scalar_tensor_tensor(out=y[:, t % 2, :, :],
                                                   in0=msum[:, t % 2, :].unsqueeze(2).broadcast_to([P, 2 * H, D]),
                                                   scalar=-1.0 / D, in1=y[:, t % 2, :, :],
                                                   op0=ALU.mult, op1=ALU.add).then_inc(c_ok, 1)
                    v_.wait_ge(sq_ok, n + 1)
                    nc.vector.tensor_reduce(vsum[:, t % 2, :], sq[:, t % 2, :, :], AX_X, ALU.add).then_inc(vs_ok, 1)

                def finish_features(t):
                    n = BT * b + t
                    v_.wait_ge(root_ok, n + 1)
                    link(nc.vector.reciprocal(rsq[:, t % 2, :], root[:, t % 2, :]), base)
                    nc.vector.tensor_tensor(y[:, t % 2, :, :], y[:, t % 2, :, :],
                                            rsq[:, t % 2, :].unsqueeze(2).broadcast_to([P, 2 * H, D]),
                                            ALU.mult).then_inc(n_ok, 1)

                v_.wait_ge(rstd_ok, b + 1)
                norm(0)
                norm(1)
                low_z(0)
                for t in range(BT):
                    if t + 1 < BT:
                        low_z(t + 1)
                    if t + 2 < BT:
                        norm(t + 2)
                    if t >= 2:
                        v_.wait_ge(qkT_ok, 2 * (BT * b + t - 1))
                    add_beta(t)
                    if t >= 1:
                        finish_features(t - 1)
                    variances(t)
                finish_features(BT - 1)

                def spread_k(hg):
                    for j in range(GH):
                        rows = slice(D * j, D * (j + 1))
                        nc.vector.tensor_copy(kz[rows, hg % 2, j, :], kT[rows, hg, :]).then_inc(kz_ok, 1)

                v_.wait_ge(qkT_read, 2 * BT * (b + 1))
                spread_k(0)
                spread_k(1)
                for hg in range(HG):
                    num, den = nd[hg % 2]
                    n = HG * b + hg
                    v_.wait_ge(av_ok, BT * (n + 1))
                    if hg + 2 < HG:
                        spread_k(hg + 2)
                    link(nc.vector.tensor_scalar(rec[:, :], den[:, :], ATT_EPS, None, ALU.add), base)
                    link(nc.vector.reciprocal(rec[:, :], rec[:, :]), base)
                    if hg:
                        v_.wait_ge(olo_ok, n)
                    nc.vector.tensor_tensor(o32[:, :], num[:, :], rec[:, :], ALU.mult).then_inc(o32_ok, 1)
                    v_.wait_ge(ohi_ok, n + 1)
                    nc.vector.tensor_tensor(oT_lo[:, hg, :], o32[:, :], oT_hi[:, hg, :].bitcast(F32),
                                            ALU.subtract).then_inc(olo_ok, 1)
                for t in range(BT):
                    n = BT * b + t
                    v_.wait_ge(out_ok, n + 1)
                    nc.vector.tensor_tensor(x_res[:, n, :], x_res[:, n, :], pj[t % 2][:, :],
                                            ALU.add).then_inc(out_read, 1)
                assert links[0] == LINKS

        @block.tensor
        def _(pe):
            def project(out, hi, lo, m, count):
                for k in range(CK):
                    for i, (a, w) in enumerate(((hi, w_hi), (lo, w_hi), (hi, w_lo))):
                        ins = nc.tensor.matmul(out, a(k), w[:, m, k, :], start=(k == 0 and i == 0),
                                               stop=(k == CK - 1 and i == 2))
                ins.then_inc(count, 1)

            def bank_free(b, what, t):
                turn = TURNS.index((what, t))
                if turn >= 2:
                    what, t = TURNS[turn - 2]
                    if what == "z":
                        pe.wait_ge(zlo_ok, BT * b + t + 1)
                    else:
                        pe.wait_ge(qkT_read, 2 * (BT * b + t) + (what == "k") + 1)

            def transpose_z(b, t):
                n = BT * b + t
                pe.wait_ge(z_ok, n + 1)
                bank_free(b, "z", t)
                for k in range(CK):
                    ins = nc.tensor.transpose(tb[turn_bank("z", t)][:, k * P:(k + 1) * P], z[:, t % 2, k * P:(k + 1) * P],
                                              ident[:, :])
                ins.then_inc(zT_ok, 1)

            def transpose_qk(b, t):
                n = BT * b + t
                pe.wait_ge(n_ok, n + 1)
                for i, what in enumerate("qk"):
                    bank_free(b, what, t)
                    for g in range(HG):
                        ins = nc.tensor.transpose(
                            tb[turn_bank(what, t)][:, g * P:(g + 1) * P],
                            y[:, t % 2, i * H + g * GH:i * H + (g + 1) * GH, :].rearrange("p h d -> p (h d)"),
                            ident[:, :])
                    ins.then_inc(qkT_ok, 1)

            pe.wait_ge(ones_ok, 1)
            with pe.Fori(0, B) as b:
                transpose_z(b, 0)
                for t in range(BT):
                    n = BT * b + t
                    if t + 1 < BT:
                        transpose_z(b, t + 1)
                    pe.wait_ge(zlo_ok, n + 1)
                    for m in range(3):
                        if t == 0:
                            pe.wait_ge(*((lo_q_ok, 1), (w_split, 1), (w_split, 2))[m])
                        if 3 * t + m >= 2:
                            tenant = 3 * t + m - 2
                            if tenant % 3 == 2:
                                pe.wait_ge(v_read, BT * b + tenant // 3 + 1)
                            else:
                                pe.wait_ge(qk_read, 2 * (BT * b + tenant // 3) + tenant % 3 + 1)
                        project(pj[(3 * t + m) % 2][:, :], lambda k: z_hi[:, t % 2, k, :],
                                lambda k: z_lo[:, t % 2, k, :], m, qkv_ok)
                    if t >= 1:
                        transpose_qk(b, t - 1)
                transpose_qk(b, BT - 1)
                pe.wait_ge(qkT_read, 2 * BT * (b + 1))
                pe.wait_ge(v_read, BT * (b + 1))
                for hg in range(HG):
                    for kt in range(BT):
                        for j in range(GH):
                            if kt == 0:
                                pe.wait_ge(kz_ok, (b * HG + hg) * GH + j + 1)
                            if hg or kt:
                                pe.wait_ge(att_ok, ((b * HG + hg) * BT + kt - 1) * GH + j + 1)
                            nc.tensor.matmul(sc[j][:, kt * P:S], kz[:, hg % 2, j, kt * P:(kt + 1) * P],
                                             qT[:, hg, kt * P:S], start=True, stop=True).then_inc(s_ok, 1)
                    num, den = nd[hg % 2]
                    if hg >= 2:
                        pe.wait_ge(o32_ok, HG * b + hg - 1)
                    for kt in range(BT):
                        pe.wait_ge(masked, (b * HG + hg) * BT + kt + 1)
                        for j in range(GH):
                            rows = slice(D * j, D * (j + 1))
                            nc.tensor.matmul(num[rows, kt * P:S], v[:, kt, (hg * GH + j) * D:(hg * GH + j + 1) * D],
                                             att[:, kt, j, kt * P:S], start=(kt == 0), stop=(kt == BT - 1))
                        for j in range(GH):
                            rows = slice(D * j, D * (j + 1))
                            ins = nc.tensor.matmul(den[rows, kt * P:S], ones[:, :],
                                                   att[:, kt, j, kt * P:S], start=(kt == 0), stop=(kt == BT - 1))
                            if j == GH - 1:
                                ins.then_inc(av_ok, 1)
                pe.wait_ge(w_split, 3)
                pe.wait_ge(olo_ok, HG * (b + 1))
                for t in range(BT):
                    if t >= 2:
                        pe.wait_ge(out_read, BT * b + t - 1)
                    project(pj[t % 2][:, :], lambda k: oT_hi[:, k, t * P:(t + 1) * P],
                            lambda k: oT_lo[:, k, t * P:(t + 1) * P], 3, out_ok)
                pe.wait_ge(out_read, BT * (b + 1))
BLOCK_TILES = 4
LOOP_TILES = 2 * BLOCK_TILES


def context_keys_values(nc, ctxT_dram, wkv_dram, bkv_dram, k_parts, v_int, v_step, ident_bf):
    with ExitStack() as ctx:
        def sb(name, shape, dt):
            return ctx.enter_context(nc.sbuf_tensor(name, shape, dt))

        def psum(name, shape, dt):
            return ctx.enter_context(nc.psum_tensor(name, shape, dt))

        def sem(name):
            return ctx.enter_context(nc.semaphore("ck_" + name))

        v_raw = sb("ck_v_raw", [P, KT, C], F32)
        w_raw = v_raw[:, 0:2 * CK, :].rearrange("p (k m) c -> p k (m c)", k=CK)
        w_hi = sb("ck_w_hi", [P, CK, 2 * C], F32R)
        w_lo = sb("ck_w_lo", [P, CK, 2 * C], F32R)
        raw = sb("ck_raw", [P, 2, CK, BLOCK_TILES * P], F32)
        c_hi = sb("ck_c_hi", [P, 2, CK, P], F32R)
        c_lo = sb("ck_c_lo", [P, 2, CK, P], F32R)
        bias = sb("ck_bias", [P, 2 * C], F32)
        kf = sb("ck_kf", [P, H, D], F32)
        kq = sb("ck_kq", [P, H, D], F32)
        rest = sb("ck_rest", [P, H, D], F32)
        step = sb("ck_step", [P, H], F32)
        rstep = sb("ck_rstep", [P, H], F32)
        parts = sb("ck_parts", [P, 2, H, 3, D], BF16)
        v_top = sb("ck_v_top", [P, C], F32)
        v_rstep = sb("ck_v_rstep", [P, C], F32)

        kb = [psum(f"ck_kb{i}", [P, C], F32) for i in range(2)]
        vb = [psum(f"ck_vb{i}", [P, C], F32) for i in range(2)]
        tr = [psum(f"ck_tr{i}", [3 * D, H, P], BF16) for i in range(2)]

        w_in = sem("w_in")
        b_in = sem("b_in")
        raw_in = [sem(f"raw_in{i}") for i in range(2)]
        whi_ok = sem("whi_ok")
        wlo_ok = sem("wlo_ok")
        chi_ok = sem("chi_ok")
        clo_ok = sem("clo_ok")
        k_ok = sem("k_ok")
        v_ok = sem("v_ok")
        kf_ok = sem("kf_ok")
        vf_ok = sem("vf_ok")
        kt_ok = sem("kt_ok")
        hi_ok = sem("hi_ok")
        rest_ok = sem("rest_ok")
        mid_ok = sem("mid_ok")
        lo_ok = sem("lo_ok")
        tr_ok = sem("tr_ok")
        tr_read = sem("tr_read")
        top_ok = sem("top_ok")
        all_top = sem("all_top")
        dve = sem("dve")

        block = ctx.enter_context(nc.Block(no_gpsimd_drain=True))
        ctxT = ctxT_dram.rearrange("(k p) n -> p k n", p=P)

        @block.sync
        def _(sp):
            sp.dma_start(w_raw, wkv_dram.rearrange("(k p) n -> p k n", p=P)).then_inc(w_in, 16)
            sp.dma_start(bias[:, :], bkv_dram.partition_broadcast(P)).then_inc(b_in, 16)
            for g in range(KT // BLOCK_TILES):
                if g >= 2:
                    sp.wait_ge(clo_ok, (g - 1) * BLOCK_TILES)
                sp.dma_start(raw[:, g % 2, :, :], ctxT[:, :, g * BLOCK_TILES * P:(g + 1) * BLOCK_TILES * P])\
                  .then_inc(raw_in[g % 2], 16)

        def raw_tile(t):
            return raw[:, t // BLOCK_TILES, :, t % BLOCK_TILES * P:(t % BLOCK_TILES + 1) * P]

        @block.gpsimd
        def _(pool):
            pool.wait_ge(whi_ok, 1)
            nc.gpsimd.tensor_tensor(w_lo[:, :, C:2 * C], w_raw[:, :, C:2 * C], w_hi[:, :, C:2 * C].bitcast(F32),
                                    ALU.subtract).then_inc(wlo_ok, 1)
            with pool.Fori(0, KT // LOOP_TILES) as i:
                for t in range(LOOP_TILES):
                    pool.wait_ge(chi_ok, i * LOOP_TILES + t + 1)
                    nc.gpsimd.tensor_tensor(c_lo[:, t % 2, :, :], raw_tile(t), c_hi[:, t % 2, :, :].bitcast(F32),
                                            ALU.subtract).then_inc(clo_ok, 1)
            pool.wait_ge(top_ok, 1)
            nc.gpsimd.partition_all_reduce(v_step[:, :], v_top[:, :], P, ABSMAX).then_inc(all_top, 1)

        @block.scalar
        def _(act):
            act.wait_ge(w_in, 16)
            nc.scalar.copy(w_hi[:, :, :], w_raw).then_inc(whi_ok, 1)

            def split(i, t):
                n = i * LOOP_TILES + t
                if t % BLOCK_TILES == 0:
                    act.wait_ge(raw_in[t // BLOCK_TILES], 16 * i + 16)
                if t >= 2:
                    act.wait_ge(v_ok, n - 1)
                nc.scalar.copy(c_hi[:, t % 2, :, :], raw_tile(t)).then_inc(chi_ok, 1)

            with act.Fori(0, KT // LOOP_TILES) as i:
                split(i, 0)
                for t in range(LOOP_TILES):
                    n = i * LOOP_TILES + t
                    if t + 1 < LOOP_TILES:
                        split(i, t + 1)
                    act.wait_ge(kt_ok, n + 1)
                    nc.scalar.copy(parts[:, t % 2, :, 0, :], kq[:, :, :]).then_inc(hi_ok, 1)
                    act.wait_ge(rest_ok, n + 1)
                    nc.scalar.copy(parts[:, t % 2, :, 1, :], rest[:, :, :]).then_inc(mid_ok, 1)

        @block.vector
        def _(v_):
            links = [0]

            def link(ins, base=0):
                links[0] += 1
                ins.then_inc(dve, 1)
                v_.wait_ge(dve, base + links[0])

            def per_head(x):
                return x[:, :].unsqueeze(2).broadcast_to([P, H, D])

            def keep_keys(i, t):
                n = i * LOOP_TILES + t
                v_.wait_ge(tr_ok, n + 1)
                nc.vector.tensor_copy(k_parts[0:3 * D, :, bass.ds(n * P, P)], tr[t % 2][:, :, :]).then_inc(tr_read, 1)

            v_.wait_ge(whi_ok, 1)
            nc.vector.tensor_tensor(w_lo[:, :, 0:C], w_raw[:, :, 0:C], w_hi[:, :, 0:C].bitcast(F32),
                                    ALU.subtract).then_inc(wlo_ok, 1)
            v_.wait_ge(b_in, 16)
            LINKS = 5 * LOOP_TILES
            with v_.Fori(0, KT // LOOP_TILES) as i:
                links[0] = 0
                base = i * LINKS
                for t in range(LOOP_TILES):
                    n = i * LOOP_TILES + t
                    v_.wait_ge(k_ok, n + 1)
                    nc.vector.tensor_tensor(kf[:, :, :], kb[t % 2][:, :].rearrange("p (h d) -> p h d", h=H),
                                            bias[:, 0:C].rearrange("p (h d) -> p h d", h=H), ALU.add).then_inc(kf_ok, 1)
                    v_.wait_ge(kf_ok, n + 1)
                    link(nc.vector.tensor_reduce(step[:, :], kf[:, :, :], AX_X, ALU.max, apply_absolute_value=True), base)
                    link(nc.vector.tensor_scalar(step[:, :], step[:, :], 1.0 / QMAX, Q_FLOOR, ALU.mult, ALU.max), base)
                    link(nc.vector.reciprocal(rstep[:, :], step[:, :]), base)
                    link(nc.vector.tensor_tensor(kf[:, :, :], kf[:, :, :], per_head(rstep), ALU.mult), base)
                    link(nc.vector.tensor_scalar(kf[:, :, :], kf[:, :, :], MAGIC, MAGIC, ALU.add, ALU.subtract), base)
                    nc.vector.tensor_tensor(kq[:, :, :], kf[:, :, :], per_head(step), ALU.mult).then_inc(kt_ok, 1)
                    v_.wait_ge(v_ok, n + 1)
                    nc.vector.tensor_tensor(v_raw[:, n, :], vb[t % 2][:, :], bias[:, C:2 * C], ALU.add).then_inc(vf_ok, 1)
                    v_.wait_ge(hi_ok, n + 1)
                    nc.vector.tensor_tensor(rest[:, :, :], kq[:, :, :], parts[:, t % 2, :, 0, :],
                                            ALU.subtract).then_inc(rest_ok, 1)
                    if t >= 1:
                        keep_keys(i, t - 1)
                    v_.wait_ge(mid_ok, n + 1)
                    nc.vector.tensor_tensor(parts[:, t % 2, :, 2, :], rest[:, :, :], parts[:, t % 2, :, 1, :],
                                            ALU.subtract).then_inc(lo_ok, 1)
                keep_keys(i, LOOP_TILES - 1)
                assert links[0] == LINKS
            links[0] = 0
            base = LINKS * (KT // LOOP_TILES)
            v_.wait_ge(vf_ok, KT)
            nc.vector.tensor_reduce(v_top[:, :], v_raw[:, :, :].rearrange("p t c -> p c t"), AX_X,
                                    ALU.max, apply_absolute_value=True).then_inc(top_ok, 1)
            v_.wait_ge(all_top, 1)
            link(nc.vector.tensor_scalar(v_step[:, :], v_step[:, :], 1.0 / QMAX, Q_FLOOR, ALU.mult, ALU.max), base)
            link(nc.vector.reciprocal(v_rstep[:, :], v_step[:, :]), base)
            link(nc.vector.tensor_tensor(v_raw[:, :, :], v_raw[:, :, :],
                                         v_rstep[:, :].unsqueeze(1).broadcast_to([P, KT, C]), ALU.mult), base)
            link(nc.vector.tensor_scalar(v_int[:, :, :], v_raw[:, :, :], MAGIC, MAGIC, ALU.add, ALU.subtract), base)

        @block.tensor
        def _(pe):
            def transpose_keys(i, t):
                n = i * LOOP_TILES + t
                pe.wait_ge(lo_ok, n + 1)
                if t >= 2:
                    pe.wait_ge(tr_read, n - 1)
                for h in range(H):
                    ins = nc.tensor.transpose(tr[t % 2][:, h, :], parts[:, t % 2, h, :, :].rearrange("p a d -> p (a d)"),
                                              ident_bf[:, :])
                ins.then_inc(tr_ok, 1)

            pe.wait_ge(wlo_ok, 2)
            with pe.Fori(0, KT // LOOP_TILES) as i:
                for t in range(LOOP_TILES):
                    n = i * LOOP_TILES + t
                    pe.wait_ge(clo_ok, n + 1)
                    for out, m, read, made in ((kb, 0, kf_ok, k_ok), (vb, 1, vf_ok, v_ok)):
                        if t >= 2:
                            pe.wait_ge(read, n - 1)
                        for k in range(CK):
                            for j, (a, w) in enumerate(((c_hi, w_hi), (c_lo, w_hi), (c_hi, w_lo))):
                                ins = nc.tensor.matmul(out[t % 2][:, :], a[:, t % 2, k, :], w[:, k, m * C:(m + 1) * C],
                                                       start=(k == 0 and j == 0), stop=(k == CK - 1 and j == 2))
                        ins.then_inc(made, 1)
                    if t >= 1:
                        transpose_keys(i, t - 1)
                transpose_keys(i, LOOP_TILES - 1)
                pe.wait_ge(tr_read, (i + 1) * LOOP_TILES)
LN_PMAX = 5.541263545158426
HALF = KEYS // 2
HKT = KT // 2


def normalise_statistics(v_, pool, nc, x_res, stats, mv, ve, rstd, minus_half, chain, ve_ok, rstd_ok):
    for t in range(TT):
        nc.vector.bn_stats(stats[:, t, :], x_res[:, t, :]).then_inc(chain, 1)
    v_.wait_ge(chain, TT)
    for t in range(TT):
        nc.vector.bn_aggr(mv[:, t, :], stats[:, t, :]).then_inc(chain, 1)
    v_.wait_ge(chain, 2 * TT)
    nc.vector.tensor_scalar(ve[:, :], mv[:, :, 1], LN_EPS, None, ALU.add).then_inc(ve_ok, 1)


def cross_queries(nc, wq_dram, bq_dram, x_res, q_int, q_step, q_nstep, ident, minus_half, ident_bf):
    scale = float(D) ** -0.5
    with ExitStack() as ctx:
        def sb(name, shape, dt):
            return ctx.enter_context(nc.sbuf_tensor(name, shape, dt))

        def psum(name, shape, dt):
            return ctx.enter_context(nc.psum_tensor(name, shape, dt))

        def sem(name):
            return ctx.enter_context(nc.semaphore("cq_" + name))

        w_raw = sb("cq_w_raw", [P, CK, C], F32)
        w_hi = sb("cq_w_hi", [P, CK, C], F32R)
        w_lo = sb("cq_w_lo", [P, CK, C], F32R)
        bias = sb("cq_bias", [P, C], F32)
        stats = sb("cq_stats", [P, TT, 6], F32)
        mv = sb("cq_mv", [P, TT, 2], F32)
        ve = sb("cq_ve", [P, TT], F32)
        rstd = sb("cq_rstd", [P, TT], F32)
        z = sb("cq_z", [P, 2, C], F32)
        z_hi = sb("cq_z_hi", [P, 2, CK, P], F32R)
        z_lo = sb("cq_z_lo", [P, 2, CK, P], F32R)
        qf = sb("cq_qf", [P, H, D], F32)
        rstep = sb("cq_rstep", [P, H], F32)
        q3 = sb("cq_q3", [P, 2, H, 3, D], BF16)
        tz = [psum(f"cq_tz{i}", [P, C], F32) for i in range(2)]
        pq = [psum(f"cq_pq{i}", [P, C], F32) for i in range(2)]
        tq = [psum(f"cq_tq{i}", [3 * D, H, P], BF16) for i in range(2)]

        w_in = sem("w_in")
        b_in = sem("b_in")
        whi_ok = sem("whi_ok")
        wlo_ok = sem("wlo_ok")
        chain = sem("chain")
        ve_ok = sem("ve_ok")
        rstd_ok = sem("rstd_ok")
        z_ok = sem("z_ok")
        zT_ok = sem("zT_ok")
        zhi_ok = sem("zhi_ok")
        zlo_ok = sem("zlo_ok")
        q_ok = sem("q_ok")
        q_read = sem("q_read")
        q3_ok = sem("q3_ok")
        tq_ok = sem("tq_ok")
        tq_read = sem("tq_read")
        dve = sem("dve")
        block = ctx.enter_context(nc.Block(no_gpsimd_drain=True))

        @block.sync
        def _(sp):
            sp.dma_start(w_raw[:, :, :], wq_dram.rearrange("(k p) n -> p k n", p=P)).then_inc(w_in, 16)
            sp.dma_start(bias[:, :], bq_dram.partition_broadcast(P)).then_inc(b_in, 16)

        @block.gpsimd
        def _(pool):
            pool.wait_ge(ve_ok, 1)
            nc.gpsimd.tensor_tensor(rstd[:, :], ve[:, :], minus_half[:, 0:TT], ALU.pow).then_inc(rstd_ok, 1)

        @block.scalar
        def _(act):
            act.wait_ge(w_in, 16)
            nc.scalar.copy(w_hi[:, :, :], w_raw[:, :, :]).then_inc(whi_ok, 1)
            with act.Fori(0, TT // 2) as i:
                for t in range(2):
                    act.wait_ge(zT_ok, 2 * i + t + 1)
                    nc.scalar.copy(z_hi[:, t, :, :], row_halves(tz[t][:, :], CK)).then_inc(zhi_ok, 1)

        @block.vector
        def _(v_):
            links = [0]

            def link(ins, base=0):
                links[0] += 1
                ins.then_inc(dve, 1)
                v_.wait_ge(dve, base + links[0])

            def per_head(x):
                return x[:, :].unsqueeze(2).broadcast_to([P, H, D])

            normalise_statistics(v_, None, nc, x_res, stats, mv, ve, rstd, minus_half, chain, ve_ok, rstd_ok)
            v_.wait_ge(whi_ok, 1)
            nc.vector.tensor_tensor(w_lo[:, :, :], w_raw[:, :, :], w_hi[:, :, :].bitcast(F32),
                                    ALU.subtract).then_inc(wlo_ok, 1)
            v_.wait_ge(rstd_ok, 1)
            v_.wait_ge(b_in, 16)
            LINKS = 2 * 6
            with v_.Fori(0, TT // 2) as i:
                links[0] = 0
                base = i * LINKS
                for t in range(2):
                    n = 2 * i + t
                    nc.vector.tensor_scalar(z[:, t, :], x_res[:, n, :], mv[:, n, 0:1], rstd[:, bass.ds(n, 1)],
                                            ALU.subtract, ALU.mult).then_inc(z_ok, 1)
                for t in range(2):
                    n = 2 * i + t
                    v_.wait_ge(zhi_ok, n + 1)
                    nc.vector.tensor_tensor(z_lo[:, t, :, :], row_halves(tz[t][:, :], CK), z_hi[:, t, :, :].bitcast(F32),
                                            ALU.subtract).then_inc(zlo_ok, 1)
                for t in range(2):
                    n = 2 * i + t
                    v_.wait_ge(q_ok, n + 1)
                    link(nc.vector.tensor_tensor(qf[:, :, :], pq[t][:, :].rearrange("p (h d) -> p h d", h=H),
                                                 bias[:, :].rearrange("p (h d) -> p h d", h=H), ALU.add), base)
                    link(nc.vector.tensor_reduce(rstep[:, :], qf[:, :, :], AX_X, ALU.max, apply_absolute_value=True), base)
                    link(nc.vector.tensor_scalar(q_step[:, n, :], rstep[:, :], scale / QMAX, Q_FLOOR, ALU.mult, ALU.max), base)
                    nc.vector.tensor_scalar(q_nstep[:, n, :], q_step[:, n, :], -1.0, None, ALU.mult)
                    link(nc.vector.reciprocal(rstep[:, :], q_step[:, n, :]), base)
                    link(nc.vector.tensor_scalar(rstep[:, :], rstep[:, :], scale, None, ALU.mult), base)
                    link(nc.vector.tensor_tensor(qf[:, :, :], qf[:, :, :], per_head(rstep), ALU.mult), base)
                    nc.vector.tensor_scalar(q3[:, t, :, :, :], qf[:, :, :].unsqueeze(2).broadcast_to([P, H, 3, D]),
                                            MAGIC, MAGIC, ALU.add, ALU.subtract).then_inc(q3_ok, 1)
                    v_.wait_ge(q3_ok, n + 1)
                for t in range(2):
                    n = 2 * i + t
                    v_.wait_ge(tq_ok, n + 1)
                    nc.vector.tensor_copy(q_int[0:3 * D, n, :, :], tq[t][:, :, :]).then_inc(tq_read, 1)
                assert links[0] == LINKS

        @block.tensor
        def _(pe):
            pe.wait_ge(wlo_ok, 1)
            with pe.Fori(0, TT // 2) as i:
                for t in range(2):
                    pe.wait_ge(z_ok, 2 * i + t + 1)
                    for k in range(CK):
                        ins = nc.tensor.transpose(tz[t][:, k * P:(k + 1) * P], z[:, t, k * P:(k + 1) * P], ident[:, :])
                    ins.then_inc(zT_ok, 1)
                for t in range(2):
                    pe.wait_ge(zlo_ok, 2 * i + t + 1)
                    for k in range(CK):
                        for j, (a, w) in enumerate(((z_hi, w_hi), (z_lo, w_hi), (z_hi, w_lo))):
                            ins = nc.tensor.matmul(pq[t][:, :], a[:, t, k, :], w[:, k, :],
                                                   start=(k == 0 and j == 0), stop=(k == CK - 1 and j == 2))
                    ins.then_inc(q_ok, 1)
                for t in range(2):
                    pe.wait_ge(q3_ok, 2 * i + t + 1)
                    for h in range(H):
                        ins = nc.tensor.transpose(tq[t][:, h, :], q3[:, t, h, :, :].rearrange("p a d -> p (a d)"),
                                                  ident_bf[:, :])
                    ins.then_inc(tq_ok, 1)
                pe.wait_ge(tq_read, 2 * i + 2)


def cross_scores(nc, k_parts, v_int, q_int, q_step, q_nstep, o_raw, z_sum, ident16):
    with ExitStack() as ctx:
        def sb(name, shape, dt):
            return ctx.enter_context(nc.sbuf_tensor(name, shape, dt))

        def psum(name, shape, dt):
            return ctx.enter_context(nc.psum_tensor(name, shape, dt))

        def sem(name):
            return ctx.enter_context(nc.semaphore("cs_" + name))

        p_int = sb("cs_p_int", [P, 2, KEYS], I16)
        pT = sb("cs_pT", [P, 2, KT, P], BF16)
        top = sb("cs_top", [P, 2, 2], F32)
        top1 = sb("cs_top1", [P, 2], F32)
        bias = sb("cs_bias", [P, 2], F32)
        s_a = [psum(f"cs_s_a{i}", [P, HALF], F32) for i in range(2)]
        s_b = psum("cs_s_b", [P, HALF], F32)
        tp = psum("cs_tp", [P, HKT, P], F16)
        out = psum("cs_out0", [P, C], F32)

        sa_ok = sem("sa_ok")
        sb_ok = sem("sb_ok")
        bias_ok = sem("bias_ok")
        ea_ok = sem("ea_ok")
        eb_ok = sem("eb_ok")
        ta_ok = sem("ta_ok")
        tb_ok = sem("tb_ok")
        ra_ok = sem("ra_ok")
        rb_ok = sem("rb_ok")
        av_ok = sem("av_ok")
        out_read = sem("out_read")
        max_ok = sem("max_ok")
        top_ok = sem("top_ok")
        block = ctx.enter_context(nc.Block(no_gpsimd_drain=True))
        UNITS = TT * H

        def units(engine, step):
            for h in range(H - 1):
                step(0, h, h)
            with engine.Fori(0, TT - 1) as t:
                step(t, H - 1, t * H + H - 1)
                for h in range(H - 1):
                    step(t + 1, h, t * H + H + h)
            step(TT - 1, H - 1, UNITS - 1)
            for n in range(UNITS, UNITS + 2):
                step(TT, n - UNITS, n)

        def exists(n):
            return not isinstance(n, int) or 0 <= n < UNITS

        def is_later(n, first):
            return not isinstance(n, int) or n >= first

        @block.scalar
        def _(act):
            def step(t, h, n):
                if not exists(n):
                    return
                u = h % 2
                for half, s, made, used in ((1, s_b, eb_ok, tb_ok), (0, s_a[u], ea_ok, ta_ok)):
                    if half:
                        act.wait_ge(bias_ok, n + 1)
                    if is_later(n, 2):
                        act.wait_ge(used, n - 1)
                    nc.scalar.activation(p_int[:, u, half * HALF:(half + 1) * HALF], s[:, :], ACT.Exp,
                                         bias=bias[:, u:u + 1], scale=q_step[:, t, h:h + 1],
                                         accum_out=z_sum[:, t, h, half:half + 1]).then_inc(made, 1)
                act.wait_ge(tb_ok, n + 1)
                if is_later(n, 2):
                    act.wait_ge(av_ok, n - 1)
                nc.scalar.copy(pT[:, u, HKT:KT, :], tp[:, :, :].bitcast(I16)).then_inc(rb_ok, 1)
            units(act, step)

        @block.vector
        def _(v_):
            def max_a(u, n):
                v_.wait_ge(sa_ok, n + 1)
                nc.vector.tensor_reduce(top[:, u, 0:1], s_a[u][:, :], AX_X, ALU.max).then_inc(max_ok, 1)

            def step(t, h, n):
                u = h % 2
                if exists(n):
                    v_.wait_ge(sb_ok, n + 1)
                    nc.vector.tensor_reduce(top[:, u, 1:2], s_b[:, :], AX_X, ALU.max).then_inc(max_ok, 1)
                    v_.wait_ge(max_ok, 2 * n + 2)
                    nc.vector.tensor_reduce(top1[:, u:u + 1], top[:, u, :], AX_X, ALU.max).then_inc(top_ok, 1)
                    v_.wait_ge(top_ok, n + 1)
                    if is_later(n, 2):
                        v_.wait_ge(ea_ok, n - 1)
                    nc.vector.tensor_scalar(bias[:, u:u + 1], top1[:, u:u + 1], q_nstep[:, t, h:h + 1], LN_PMAX,
                                            ALU.mult, ALU.add).then_inc(bias_ok, 1)
                if exists(n + 1):
                    max_a(1 - u, n + 1)
                if is_later(n, 1) and exists(n - 1):
                    v_.wait_ge(ta_ok, n)
                    if is_later(n, 3):
                        v_.wait_ge(av_ok, n - 2)
                    nc.vector.tensor_copy(pT[:, 1 - u, 0:HKT, :], tp[:, :, :].bitcast(I16)).then_inc(ra_ok, 1)
                if h == 1 and is_later(n, H):
                    v_.wait_ge(av_ok, n - 1)
                    nc.vector.tensor_copy(o_raw[:, t - 1, :], out[:, :]).then_inc(out_read, 1)

            max_a(0, 0)
            units(v_, step)

        @block.tensor
        def _(pe):
            def scores(t, h, s, half, made):
                for c in range(2):
                    keys = half * HALF + c * 512
                    ins = nc.tensor.matmul(s[:, c * 512:(c + 1) * 512], q_int[0:3 * D, t, h, :],
                                           k_parts[0:3 * D, h, keys:keys + 512], start=True, stop=True)
                ins.then_inc(made, 1)

            def transposes(u, half, made):
                for k in range(HKT):
                    key = (half * HKT + k) * P
                    ins = nc.tensor.transpose(tp[:, k, :], p_int[:, u, key:key + P].bitcast(F16), ident16[:, :])
                ins.then_inc(made, 1)

            def step(t, h, n):
                u = h % 2
                before = is_later(n, 1) and exists(n - 1)
                if exists(n):
                    if is_later(n, 1):
                        pe.wait_ge(eb_ok, n)
                    scores(t, h, s_b, 1, sb_ok)
                if before:
                    pe.wait_ge(eb_ok, n)
                    if is_later(n, 2):
                        pe.wait_ge(ra_ok, n - 1)
                    transposes(1 - u, 1, tb_ok)
                if exists(n + 1):
                    if is_later(n, 1):
                        pe.wait_ge(ea_ok, n)
                    scores(t + (h + 1) // H, (h + 1) % H, s_a[1 - u], 0, sa_ok)
                if is_later(n, 2):
                    head = (h - 2) % H
                    pe.wait_ge(ra_ok, n - 1)
                    pe.wait_ge(rb_ok, n - 1)
                    if head == 0 and is_later(n, H):
                        pe.wait_ge(out_read, t)
                    for k in range(KT):
                        ins = nc.tensor.matmul(out[:, head * D:(head + 1) * D], pT[:, u, k, :],
                                               v_int[:, k, head * D:(head + 1) * D], start=(k == 0), stop=(k == KT - 1))
                    ins.then_inc(av_ok, 1)
                if before:
                    pe.wait_ge(ea_ok, n)
                    pe.wait_ge(rb_ok, n)
                    transposes(1 - u, 0, ta_ok)

            scores(0, 0, s_a[0], 0, sa_ok)
            units(pe, step)


def cross_output(nc, wp_dram, bp_dram, x_res, o_raw, z_sum, v_step, ident):
    with ExitStack() as ctx:
        def sb(name, shape, dt):
            return ctx.enter_context(nc.sbuf_tensor(name, shape, dt))

        def psum(name, shape, dt):
            return ctx.enter_context(nc.psum_tensor(name, shape, dt))

        def sem(name):
            return ctx.enter_context(nc.semaphore("co_" + name))

        w_raw = sb("co_w_raw", [P, CK, C], F32)
        w_hi = sb("co_w_hi", [P, CK, C], F32R)
        w_lo = sb("co_w_lo", [P, CK, C], F32R)
        bias = sb("co_bias", [P, C], F32)
        p_step = sb("co_p_step", [P, TT, H], F32)
        o = sb("co_o", [P, 2, H, D], F32)
        o_hi = sb("co_o_hi", [P, 2, CK, P], F32R)
        o_lo = sb("co_o_lo", [P, 2, CK, P], F32R)
        to = [psum(f"co_to{i}", [P, C], F32) for i in range(2)]
        po = [psum(f"co_po{i}", [P, C], F32) for i in range(2)]
        w_in = sem("w_in")
        b_in = sem("b_in")
        whi_ok = sem("whi_ok")
        wlo_ok = sem("wlo_ok")
        o_ok = sem("o_ok")
        oT_ok = sem("oT_ok")
        ohi_ok = sem("ohi_ok")
        olo_ok = sem("olo_ok")
        y_ok = sem("y_ok")
        y_read = sem("y_read")
        dve = sem("dve")
        block = ctx.enter_context(nc.Block(no_gpsimd_drain=True))

        @block.sync
        def _(sp):
            sp.dma_start(w_raw[:, :, :], wp_dram.rearrange("(k p) n -> p k n", p=P)).then_inc(w_in, 16)
            sp.dma_start(bias[:, :], bp_dram.partition_broadcast(P)).then_inc(b_in, 16)

        @block.scalar
        def _(act):
            act.wait_ge(w_in, 16)
            nc.scalar.copy(w_hi[:, :, :], w_raw[:, :, :]).then_inc(whi_ok, 1)
            with act.Fori(0, TT // 2) as i:
                for t in range(2):
                    act.wait_ge(oT_ok, 2 * i + t + 1)
                    nc.scalar.copy(o_hi[:, t, :, :], row_halves(to[t][:, :], CK)).then_inc(ohi_ok, 1)

        @block.vector
        def _(v_):
            links = [0]

            def link(ins, base=0):
                links[0] += 1
                ins.then_inc(dve, 1)
                v_.wait_ge(dve, base + links[0])

            link(nc.vector.tensor_reduce(p_step[:, :, :], z_sum[:, :, :, :], AX_X, ALU.add))
            link(nc.vector.reciprocal(p_step[:, :, :], p_step[:, :, :]))
            link(nc.vector.tensor_scalar(p_step[:, :, :], p_step[:, :, :], Q_FLOOR, None, ALU.max))
            v_.wait_ge(whi_ok, 1)
            nc.vector.tensor_tensor(w_lo[:, :, :], w_raw[:, :, :], w_hi[:, :, :].bitcast(F32),
                                    ALU.subtract).then_inc(wlo_ok, 1)
            v_.wait_ge(b_in, 16)
            head = links[0]
            LINKS = 2 * 2
            with v_.Fori(0, TT // 2) as i:
                links[0] = 0
                base = head + i * LINKS
                for t in range(2):
                    n = 2 * i + t
                    link(nc.vector.tensor_tensor(o[:, t, :, :], o_raw[:, n, :].rearrange("p (h d) -> p h d", h=H),
                                                 p_step[:, n, :].unsqueeze(2).broadcast_to([P, H, D]), ALU.mult), base)
                    nc.vector.tensor_tensor(o[:, t, :, :].rearrange("p h d -> p (h d)"),
                                            o[:, t, :, :].rearrange("p h d -> p (h d)"), v_step[:, :],
                                            ALU.mult).then_inc(o_ok, 1)
                for t in range(2):
                    n = 2 * i + t
                    v_.wait_ge(ohi_ok, n + 1)
                    nc.vector.tensor_tensor(o_lo[:, t, :, :], row_halves(to[t][:, :], CK), o_hi[:, t, :, :].bitcast(F32),
                                            ALU.subtract).then_inc(olo_ok, 1)
                for t in range(2):
                    n = 2 * i + t
                    link(nc.vector.tensor_tensor(x_res[:, n, :], x_res[:, n, :], bias[:, :], ALU.add), base)
                    v_.wait_ge(y_ok, n + 1)
                    nc.vector.tensor_tensor(x_res[:, n, :], x_res[:, n, :], po[t][:, :], ALU.add).then_inc(y_read, 1)
                assert links[0] == LINKS

        @block.tensor
        def _(pe):
            pe.wait_ge(wlo_ok, 1)
            with pe.Fori(0, TT // 2) as i:
                for t in range(2):
                    pe.wait_ge(o_ok, 2 * i + t + 1)
                    for k in range(CK):
                        ins = nc.tensor.transpose(to[t][:, k * P:(k + 1) * P],
                                                  o[:, t, k * GH:(k + 1) * GH, :].rearrange("p h d -> p (h d)"), ident[:, :])
                    ins.then_inc(oT_ok, 1)
                for t in range(2):
                    pe.wait_ge(olo_ok, 2 * i + t + 1)
                    for k in range(CK):
                        for j, (a, w) in enumerate(((o_hi, w_hi), (o_lo, w_hi), (o_hi, w_lo))):
                            ins = nc.tensor.matmul(po[t][:, :], a[:, t, k, :], w[:, k, :],
                                                   start=(k == 0 and j == 0), stop=(k == CK - 1 and j == 2))
                    ins.then_inc(y_ok, 1)
                pe.wait_ge(y_read, 2 * i + 2)


def cross_attention(nc, wq, bq, ctxT, wkv, bkv, wp, bp, x_res, ident, minus_half, ident16, ident_bf):
    with ExitStack() as ctx:
        def sb(name, shape, dt):
            return ctx.enter_context(nc.sbuf_tensor(name, shape, dt))

        k_parts = sb("k_parts", [3 * D, H, KEYS], BF16)
        v_int = sb("v_int", [P, KT, C], BF16)
        v_step = sb("v_step", [P, C], F32)
        context_keys_values(nc, ctxT, wkv, bkv, k_parts, v_int, v_step, ident_bf)
        q_int = sb("q_int", [3 * D, TT, H, P], BF16)
        q_step = sb("q_step", [P, TT, H], F32)
        q_nstep = sb("q_nstep", [P, TT, H], F32)
        cross_queries(nc, wq, bq, x_res, q_int, q_step, q_nstep, ident, minus_half, ident_bf)
        o_raw = sb("o_raw", [P, TT, C], F32)
        z_sum = sb("z_sum", [P, TT, H, 2], F32)
        cross_scores(nc, k_parts, v_int, q_int, q_step, q_nstep, o_raw, z_sum, ident16)
        cross_output(nc, wp, bp, x_res, o_raw, z_sum, v_step, ident)
E_N, TOP, I_W = 8, 2, 352
ROUTED = E_N * I_W // P
SHARED_W = 2 * I_W
SHARED = -(-SHARED_W // P)
CHUNKS = SHARED + ROUTED
GROUP = 2
PAIR = 2 * GROUP
TURNS_F = CHUNKS // PAIR
HALF_T = TOKENS // 2
LO_ROW = 32


def feed_forward(nc, gate_dram, rank_dram, w_dram, sel_dram, out_dram, x_res, ident, minus_half):
    with ExitStack() as ctx:
        def sb(name, shape, dt):
            return ctx.enter_context(nc.sbuf_tensor(name, shape, dt))

        def psum(name, shape, dt):
            return ctx.enter_context(nc.psum_tensor(name, shape, dt))

        def sem(name):
            return ctx.enter_context(nc.semaphore("ff_" + name))

        zT_hi = sb("zT_hi", [P, CK, TOKENS], F32R)
        zT_lo = sb("zT_lo", [P, CK, TOKENS], F32R)
        comb = sb("comb", [2 * LO_ROW, TOKENS], F32R)
        g_raw = sb("fg_g_raw", [P, CK, E_N], F32)
        g_hi = sb("fg_g_hi", [P, CK, E_N], F32R)
        g_lo = sb("fg_g_lo", [P, CK, E_N], F32R)
        rank = sb("fg_rank", [P, TT, E_N], F32)
        stats = sb("fg_stats", [P, TT, 6], F32)
        mv = sb("fg_mv", [P, TT, 2], F32)
        ve = sb("fg_ve", [P, TT], F32)
        rstd = sb("fg_rstd", [P, TT], F32)
        z = sb("fg_z", [P, 2, C], F32)
        lg = sb("fg_lg", [P, TT, E_N], F32)
        prob = sb("fg_prob", [P, TT, E_N], F32)
        left = sb("fg_left", [P, TT, E_N], F32)
        hot = sb("fg_hot", [P, TT, E_N], F32)
        w = sb("fg_w", [P, TT, E_N], F32)
        one = sb("fg_one", [P, TT], F32)
        raw = sb("fh_raw", [P, PAIR, 3 * C], F32)
        up_hi = sb("fh_up_hi", [P, 2, 2, CK, P], F32R)
        up_lo = sb("fh_up_lo", [P, 2, 2, CK, P], F32R)
        dn_hi = sb("fh_dn_hi", [P, PAIR, C], F32R)
        dn_lo = sb("fh_dn_lo", [P, PAIR, C], F32R)
        h_hi = sb("fh_h_hi", [P, PAIR, TOKENS], F32R)
        h_lo = sb("fh_h_lo", [P, PAIR, TOKENS], F32R)
        act_s = sb("fh_s", [P, 2, HALF_T], F32)
        g = sb("fh_g", [P, 2, HALF_T], F32)
        sel_raw = sb("fh_sel_raw", [2 * LO_ROW, ROUTED * P], F32)
        sel = sb("fh_sel", [2 * LO_ROW, 2, P], F32R)
        h1 = [psum(f"fh_h1{i}", [P, HALF_T], F32) for i in range(2)]
        h2 = [psum(f"fh_h2{i}", [P, HALF_T], F32) for i in range(2)]
        pc = [psum(f"fh_pc{i}", [P, HALF_T], F32) for i in range(2)]
        py = [psum(f"fh_py{i}", [P, C], F32) for i in range(2)]

        tz = py
        pl = pc[0][:, 0:TT * E_N].rearrange("p (t e) -> p t e", t=TT)

        g_in = sem("g_in")
        r_in = sem("r_in")
        ghi_ok = sem("ghi_ok")
        glo_ok = sem("glo_ok")
        chain = sem("chain")
        ve_ok = sem("ve_ok")
        rstd_ok = sem("rstd_ok")
        z_ok = sem("z_ok")
        zT_ok = sem("zT_ok")
        zhi_ok = sem("zhi_ok")
        zlo_ok = sem("zlo_ok")
        lg_ok = sem("lg_ok")
        sub_ok = sem("sub_ok")
        exp_ok = sem("exp_ok")
        w_ok = sem("w_ok")
        tc_ok = sem("tc_ok")
        chi_ok = sem("chi_ok")
        zero_ok = sem("zero_ok")
        clo_ok = sem("clo_ok")
        dve = sem("dve")
        sel_in = sem("sel_in")
        w_in = [sem(f"w_in{i}") for i in range(PAIR)]
        uhi_ok = sem("uhi_ok")
        ulo_ok = sem("ulo_ok")
        dhi_ok = sem("dhi_ok")
        dlo_ok = sem("dlo_ok")
        h1_ok = sem("h1_ok")
        h2_ok = sem("h2_ok")
        s_ok = sem("s_ok")
        g1_ok = sem("g1_ok")
        g_ok = sem("g_ok")
        hhi_ok = sem("hhi_ok")
        hlo_ok = sem("hlo_ok")
        y_ok = sem("y_ok")
        y_read = sem("y_read")
        stored = sem("stored")
        block = ctx.enter_context(nc.Block(no_gpsimd_drain=True))
        assert CHUNKS % PAIR == 0 and PAIR < SHARED <= 2 * PAIR

        def turns(engine, turn):
            turn(0, PAIR)
            turn(1, SHARED - PAIR)
            with engine.Fori(2, TURNS_F - 1) as p:
                turn(p, 0)
            turn(TURNS_F - 1, 0)

        def before(p, j, n):
            return not (isinstance(p, int) and PAIR * p + j < n)

        def last(p, j):
            return isinstance(p, int) and PAIR * p + j == CHUNKS - 1

        def has_weights(p, j):
            return not (isinstance(p, int) and PAIR * p + j < SHARED)

        @block.sync
        def _(sp):
            sp.dma_start(g_raw[:, :, :], gate_dram.rearrange("(k p) e -> p k e", p=P)).then_inc(g_in, 16)

            def turn(p, routed):
                for j in range(PAIR):
                    if before(p, j, PAIR):
                        sp.wait_ge(dlo_ok, PAIR * p + j + 1 - PAIR)
                    sp.dma_start(raw[:, j, :], w_dram[bass.ds(PAIR * p + j, 1), :, :].rearrange("a p n -> p (a n)"))\
                      .then_inc(w_in[j], 16)
                if isinstance(p, int) and p == 0:
                    sp.dma_start(rank[:, :, :].rearrange("p t e -> p (t e)"),
                                 rank_dram.partition_broadcast(P)).then_inc(r_in, 16)
                    sp.dma_start(sel_raw[:, :], sel_dram).then_inc(sel_in, 16)
            turns(sp, turn)
            sp.wait_ge(y_read, TT * TURNS_F * 2)
            sp.dma_start(out_dram.rearrange("(t p) c -> p t c", p=P), x_res[:, :, :]).then_inc(stored, 16)
            sp.wait_ge(stored, 16)

        @block.scalar
        def _(act):
            def split_up(p, j):
                act.wait_ge(w_in[j], 16 * (p + 1))
                if before(p, j, 2):
                    act.wait_ge(h2_ok, 2 * (PAIR * p + j) - 2)
                if has_weights(p, j):
                    nc.scalar.copy(sel[:, j % 2, :], sel_raw[:, bass.ds((PAIR * p + j - SHARED) * P, P)])
                nc.scalar.copy(up_hi[:, j % 2, :, :, :].rearrange("p a k n -> p (a k n)"),
                               raw[:, j, 0:2 * C]).then_inc(uhi_ok, 1)

            def turn(p, routed):
                for j in range(PAIR):
                    c = PAIR * p + j
                    if isinstance(p, int) and c == 1:
                        act.wait_ge(sub_ok, 1)
                        nc.scalar.activation(lg[:, :, :], lg[:, :, :], ACT.Exp).then_inc(exp_ok, 1)
                    if isinstance(p, int) and c == PAIR:
                        act.wait_ge(tc_ok, 1)
                        for b in range(2):
                            nc.scalar.copy(comb[0:E_N, b * HALF_T:(b + 1) * HALF_T], pc[b][0:E_N, :]).then_inc(chi_ok, 1)
                    if isinstance(p, int) and c == SHARED - 1:
                        act.wait_ge(sel_in, 16)
                    if j + 1 < PAIR:
                        split_up(p, j + 1)
                    elif not last(p, j):
                        split_up(p + 1, 0)
                    for b in range(2):
                        act.wait_ge(h1_ok, 2 * c + b + 1)
                        nc.scalar.activation(act_s[:, b, :], h1[b][:, :], ACT.Silu).then_inc(s_ok, 1)
                        act.wait_ge(g_ok, 2 * c + b + 1)
                        if before(p, j, PAIR) and b == 0 and j % GROUP == 0:
                            act.wait_ge(y_ok, TT * (2 * p + j // GROUP - 1))
                        nc.scalar.copy(h_hi[:, j, b * HALF_T:(b + 1) * HALF_T], g[:, b, :]).then_inc(hhi_ok, 1)
                    nc.scalar.copy(dn_hi[:, j, :], raw[:, j, 2 * C:3 * C]).then_inc(dhi_ok, 1)

            act.wait_ge(g_in, 16)
            nc.scalar.copy(g_hi[:, :, :], g_raw[:, :, :]).then_inc(ghi_ok, 1)
            for t in range(TT):
                act.wait_ge(zT_ok, t + 1)
                nc.scalar.copy(zT_hi[:, :, t * P:(t + 1) * P], row_halves(tz[t % 2][:, :], CK)).then_inc(zhi_ok, 1)
                if t == 0:
                    split_up(0, 0)
            turns(act, turn)

        @block.gpsimd
        def _(pool):
            def split_up(p, j):
                pool.wait_ge(uhi_ok, PAIR * p + j + 1)
                nc.gpsimd.tensor_tensor(up_lo[:, j % 2, :, :, :].rearrange("p a k n -> p (a k n)"), raw[:, j, 0:2 * C],
                                        up_hi[:, j % 2, :, :, :].rearrange("p a k n -> p (a k n)").bitcast(F32),
                                        ALU.subtract).then_inc(ulo_ok, 1)

            def turn(p, routed):
                for j in range(PAIR):
                    c = PAIR * p + j
                    if j + 1 < PAIR:
                        split_up(p, j + 1)
                    elif not last(p, j):
                        split_up(p + 1, 0)
                    for b in range(2):
                        pool.wait_ge(hhi_ok, 2 * c + b + 1)
                        nc.gpsimd.tensor_tensor(h_lo[:, j, b * HALF_T:(b + 1) * HALF_T], g[:, b, :],
                                                h_hi[:, j, b * HALF_T:(b + 1) * HALF_T].bitcast(F32),
                                                ALU.subtract).then_inc(hlo_ok, 1)
                    pool.wait_ge(dhi_ok, c + 1)
                    nc.gpsimd.tensor_tensor(dn_lo[:, j, :], raw[:, j, 2 * C:3 * C], dn_hi[:, j, :].bitcast(F32),
                                            ALU.subtract).then_inc(dlo_ok, 1)

            nc.gpsimd.memset(comb[:, :].bitcast(F32), 0.0).then_inc(zero_ok, 1)
            pool.wait_ge(ve_ok, 1)
            nc.gpsimd.tensor_tensor(rstd[:, :], ve[:, :], minus_half[:, 0:TT], ALU.pow).then_inc(rstd_ok, 1)
            split_up(0, 0)
            turns(pool, turn)

        @block.vector
        def _(v_):
            links = [0]

            def link(ins):
                links[0] += 1
                ins.then_inc(dve, 1)
                v_.wait_ge(dve, links[0])

            normalise_statistics(v_, None, nc, x_res, stats, mv, ve, rstd, minus_half, chain, ve_ok, rstd_ok)
            v_.wait_ge(ghi_ok, 1)
            nc.vector.tensor_tensor(g_lo[:, :, :], g_raw[:, :, :], g_hi[:, :, :].bitcast(F32), ALU.subtract).then_inc(glo_ok, 1)
            v_.wait_ge(rstd_ok, 1)

            def norm(t):
                if t >= 2:
                    v_.wait_ge(zT_ok, t - 1)
                nc.vector.tensor_scalar(z[:, t % 2, :], x_res[:, t, :], mv[:, t, 0:1], rstd[:, t:t + 1],
                                        ALU.subtract, ALU.mult).then_inc(z_ok, 1)
            norm(0)
            for t in range(TT):
                if t + 1 < TT:
                    norm(t + 1)
                v_.wait_ge(zhi_ok, t + 1)
                nc.vector.tensor_tensor(zT_lo[:, :, t * P:(t + 1) * P], row_halves(tz[t % 2][:, :], CK),
                                        zT_hi[:, :, t * P:(t + 1) * P].bitcast(F32), ALU.subtract).then_inc(zlo_ok, 1)

            def across(x):
                return x[:, :].unsqueeze(2).broadcast_to([P, TT, E_N])

            def route(stage):
                if stage == 0:
                    v_.wait_ge(lg_ok, TT)
                    link(nc.vector.tensor_reduce(one[:, :], pl[:, :, :], AX_X, ALU.max))
                    nc.vector.tensor_tensor(lg[:, :, :], pl[:, :, :], across(one), ALU.subtract).then_inc(sub_ok, 1)
                if stage == 1:
                    v_.wait_ge(exp_ok, 1)
                    link(nc.vector.tensor_reduce(one[:, :], lg[:, :, :], AX_X, ALU.add))
                    link(nc.vector.reciprocal(one[:, :], one[:, :]))
                    link(nc.vector.tensor_tensor(prob[:, :, :], lg[:, :, :], across(one), ALU.mult))
                    link(nc.vector.tensor_copy(left[:, :, :], prob[:, :, :]))
                    v_.wait_ge(r_in, 16)
                if stage in (2, 3):
                    link(nc.vector.tensor_reduce(one[:, :], left[:, :, :], AX_X, ALU.max))
                    link(nc.vector.tensor_tensor(hot[:, :, :], left[:, :, :], across(one), ALU.is_equal))
                    link(nc.vector.tensor_tensor(hot[:, :, :], hot[:, :, :], rank[:, :, :], ALU.mult))
                    link(nc.vector.tensor_reduce(one[:, :], hot[:, :, :], AX_X, ALU.max))
                    link(nc.vector.tensor_tensor(hot[:, :, :], hot[:, :, :], across(one), ALU.is_equal))
                    link(nc.vector.scalar_tensor_tensor(out=left[:, :, :], in0=hot[:, :, :], scalar=-2.0,
                                                        in1=left[:, :, :], op0=ALU.mult, op1=ALU.add))
                if stage == 3:
                    link(nc.vector.tensor_scalar(hot[:, :, :], left[:, :, :], -0.5, None, ALU.is_lt))
                    nc.vector.tensor_tensor(w[:, :, :], hot[:, :, :], prob[:, :, :], ALU.mult).then_inc(w_ok, 1)

            def low_weights():
                v_.wait_ge(chi_ok, 2)
                for b in range(2):
                    cols = slice(b * HALF_T, (b + 1) * HALF_T)
                    nc.vector.tensor_tensor(comb[LO_ROW:LO_ROW + E_N, cols], pc[b][0:E_N, :],
                                            comb[0:E_N, cols].bitcast(F32), ALU.subtract).then_inc(clo_ok, 1)

            def add_y(group):
                for t in range(TT):
                    v_.wait_ge(y_ok, TT * group + t + 1)
                    nc.vector.tensor_tensor(x_res[:, t, :], x_res[:, t, :], py[t % 2][:, :], ALU.add).then_inc(y_read, 1)

            def turn(p, routed):
                for j in range(PAIR):
                    c = PAIR * p + j
                    for b in range(2):
                        v_.wait_ge(s_ok, 2 * c + b + 1)
                        v_.wait_ge(h2_ok, 2 * c + b + 1)
                        if before(p, j, 1):
                            v_.wait_ge(hlo_ok, 2 * c + b - 1)
                        ins = nc.vector.tensor_tensor(g[:, b, :], act_s[:, b, :], h2[b][:, :], ALU.mult)
                        if j >= routed:
                            ins.then_inc(g1_ok, 1)
                            v_.wait_ge(g1_ok, 2 * (c - SHARED) + b + 1)
                            ins = nc.vector.tensor_tensor(g[:, b, :], g[:, b, :], pc[b][:, :], ALU.mult)
                        ins.then_inc(g_ok, 1)
                    if isinstance(p, int) and p == 0:
                        route(j)
                    if isinstance(p, int) and c == PAIR:
                        low_weights()
                    if j == GROUP - 1 and before(p, j, PAIR):
                        add_y(2 * p - 1)
                    if j == PAIR - 1:
                        add_y(2 * p)
            turns(v_, turn)
            add_y(2 * TURNS_F - 1)

        @block.tensor
        def _(pe):
            pe.wait_ge(glo_ok, 1)

            def gate(t):
                pe.wait_ge(zlo_ok, t + 1)
                for k in range(CK):
                    for j, (a, g) in enumerate(((zT_hi, g_hi), (zT_lo, g_hi), (zT_hi, g_lo))):
                        ins = nc.tensor.matmul(pl[:, t, :], a[:, k, t * P:(t + 1) * P], g[:, k, :],
                                               start=(k == 0 and j == 0), stop=(k == CK - 1 and j == 2))
                ins.then_inc(lg_ok, 1)

            for t in range(TT):
                pe.wait_ge(z_ok, t + 1)
                if t >= 2:
                    pe.wait_ge(zlo_ok, t - 1)
                for k in range(CK):
                    ins = nc.tensor.transpose(tz[t % 2][:, k * P:(k + 1) * P], z[:, t % 2, k * P:(k + 1) * P], ident[:, :])
                ins.then_inc(zT_ok, 1)
                if t >= 1:
                    gate(t - 1)
            gate(TT - 1)

            def hidden(p, j, routed):
                c = PAIR * p + j
                pe.wait_ge(ulo_ok, c + 1)
                for b in range(2):
                    if before(p, j, 1):
                        pe.wait_ge(g_ok, 2 * c + b - 1)
                    cols = slice(b * HALF_T, (b + 1) * HALF_T)
                    for m, (out, made) in enumerate(((h1, h1_ok), (h2, h2_ok))):
                        if m and routed:
                            nc.tensor.matmul(pc[b][:, :], sel[:, j % 2, :], comb[:, cols], start=True, stop=True)
                        for k in range(CK):
                            for i, (w, zz) in enumerate(((up_hi, zT_hi), (up_lo, zT_hi), (up_hi, zT_lo))):
                                ins = nc.tensor.matmul(out[b][:, :], w[:, j % 2, m, k, :], zz[:, k, cols],
                                                       start=(k == 0 and i == 0), stop=(k == CK - 1 and i == 2))
                        ins.then_inc(made, 1)

            def down(group, u):
                pe.wait_ge(hlo_ok, 2 * GROUP * (group + 1))
                pe.wait_ge(dlo_ok, GROUP * (group + 1))
                for t in range(TT):
                    if not (isinstance(group, int) and group == 0 and t < 2):
                        pe.wait_ge(y_read, TT * group + t - 1)
                    for q in range(GROUP):
                        j = u * GROUP + q
                        tile = slice(t * P, (t + 1) * P)
                        for i, (hh, w) in enumerate(((h_hi, dn_hi), (h_lo, dn_hi), (h_hi, dn_lo))):
                            ins = nc.tensor.matmul(py[t % 2][:, :], hh[:, j, tile], w[:, j, :],
                                                   start=(q == 0 and i == 0), stop=(q == GROUP - 1 and i == 2))
                    ins.then_inc(y_ok, 1)

            def turn_weights():
                pe.wait_ge(w_ok, 1)
                for t in range(TT):
                    ins = nc.tensor.transpose(pc[t // (TT // 2)][0:E_N, t % (TT // 2) * P:(t % (TT // 2) + 1) * P],
                                              w[:, t, :], ident[:, :])
                ins.then_inc(tc_ok, 1)

            def turn(p, routed):
                for j in range(PAIR):
                    if isinstance(p, int) and PAIR * p + j == SHARED:
                        pe.wait_ge(clo_ok, 2)
                        pe.wait_ge(zero_ok, 1)
                    hidden(p, j, j >= routed)
                    if isinstance(p, int) and PAIR * p + j == PAIR - 1:
                        turn_weights()
                    if j == GROUP - 1 and before(p, j, PAIR):
                        down(2 * p - 1, 1)
                    if j == PAIR - 1:
                        down(2 * p, 0)
            turns(pe, turn)
            down(2 * TURNS_F - 1, 1)


def decoder_layer(nc, x, ctxT, wq, wk, wv, wo, gamma, beta, cwq, cbq, cwkv, cbkv, cwp, cbp, gate, rank, weights, sel, out):
    with ExitStack() as ctx:
        x_res, (ident, mask, minus_half, ident16, ident_bf) = constants(nc, ctx)
        self_attention(nc, x, (wq, wk, wv, wo), gamma, beta, x_res, ident, mask, minus_half)
        cross_attention(nc, cwq, cbq, ctxT, cwkv, cbkv, cwp, cbp, x_res, ident, minus_half, ident16, ident_bf)
        feed_forward(nc, gate, rank, weights, sel, out, x_res, ident, minus_half)


def _arrays(inputs):
    import numpy as np

    def f(name):
        return np.asarray(inputs[name])

    a = {
        "x": f("x").reshape(TOKENS, C),
        "ctxT": f("ctx_2048").reshape(KEYS, C).T,
        "wq": f("L0_attn_Wq").T, "wk": f("L0_attn_Wk").T, "wv": f("L0_attn_Wv").T, "wo": f("L0_attn_Wo").T,
        "gamma": np.tile(f("L0_attn_gamma"), H)[None], "beta": np.tile(f("L0_attn_beta"), H)[None],
        "cwq": f("L0_xattn_Wq"), "cbq": f("L0_xattn_bq")[None],
        "cwkv": f("L0_xattn_Wkv"), "cbkv": f("L0_xattn_bkv")[None],
        "cwp": f("L0_xattn_Wp"), "cbp": f("L0_xattn_bp")[None],
        "gate": f("L0_ffn_gate_w").T,
        "rank": np.tile(np.arange(E_N, 0, -1, dtype=np.float32), TT)[None],
    }
    pad = np.zeros((SHARED * P - SHARED_W, C), np.float32)

    def rows(routed, shared):
        return np.concatenate([shared, pad, routed]).reshape(CHUNKS, P, C)

    up = [rows(f(f"L0_ffn_{r}").reshape(-1, C), f(f"L0_ffn_{s}")).reshape(CHUNKS, P, CK, P).transpose(0, 3, 2, 1)
          .reshape(CHUNKS, P, C) for r, s in (("w1", "sw1"), ("w2", "sw2"))]
    down = rows(f("L0_ffn_w3").transpose(0, 2, 1).reshape(-1, C), f("L0_ffn_sw3").T)
    a["weights"] = np.concatenate([*up, down], axis=2)
    one_hot = (np.arange(ROUTED * P)[None] // I_W == np.arange(E_N)[:, None]).astype(np.float32)
    a["sel"] = np.zeros((2 * LO_ROW, ROUTED * P), np.float32)
    a["sel"][0:E_N] = one_hot
    a["sel"][LO_ROW:LO_ROW + E_N] = one_hot
    return {n: np.ascontiguousarray(v) for n, v in a.items()}


def kernel(**inputs):
    import numpy as _np
    import concourse.bacc as _bacc
    from concourse.bass_utils import run_bass_kernel_spmd as _run

    nc = _bacc.Bacc("TRN2", target_bir_lowering=False, num_devices=1)
    arrays, args = {}, []
    for name, a in _arrays(inputs).items():
        arrays[f"in_{name}_dram"] = a
        args.append(nc.dram_tensor(f"in_{name}_dram", a.shape, mybir.dt.from_np(a.dtype), kind="ExternalInput").ap())
    args.append(nc.dram_tensor("out_dram", (TOKENS, C), F32, kind="ExternalOutput").ap())
    decoder_layer(nc, *args)
    r = _run(nc, [arrays], core_ids=[0])
    return r.results[0]["out_dram"].reshape(B, S, C)
```

```python
from contextlib import ExitStack
from math import log

import concourse.bass as bass
from concourse import mybir

F32 = mybir.dt.float32
F32R = mybir.dt.float32r
F16 = mybir.dt.float16
BF16 = mybir.dt.bfloat16
I16 = mybir.dt.int16
ALU = mybir.AluOpType
ACT = mybir.ActivationFunctionType
AX_X = mybir.AxisListType.X
ABSMAX = bass.bass_isa.ReduceOp.absmax

P = 128
B, S, C = 2, 512, 512
TOKENS = B * S
TT = TOKENS // P
H, D = 16, 32
CK = C // P
HG = C // P
GH = P // D
BT = S // P
KEYS = 2 * 1024
KT = KEYS // P
LN_EPS = 1e-05
ATT_EPS = 1e-05
MAGIC = 12582912.0
QMAX = 127.0
PMAX = 255.0
LN_PMAX = log(PMAX)
Q_FLOOR = 1e-08


def row_halves(ap, n):
    return ap.rearrange("p (n w) -> p n w", n=n)
def constants(nc, ctx):
    def sb(name, shape, dt):
        return ctx.enter_context(nc.sbuf_tensor(name, shape, dt))

    x_res = sb("x_res", [P, TT, C], F32)
    ident = sb("ident", [P, P], F32)
    ident16 = sb("ident16", [P, P], F16)
    ident_bf = sb("ident_bf", [P, P], BF16)
    mask = sb("mask", [P, P], F32)
    minus_half = sb("minus_half", [P, 2 * H], F32)
    made = ctx.enter_context(nc.semaphore("const_made"))
    with nc.Block(no_gpsimd_drain=True) as block:
        @block.gpsimd
        def _(pool):
            nc.gpsimd.memset(minus_half[:, :], -0.5)
            nc.gpsimd.memset(ident[:, :], 0.0).then_inc(made, 1)
            nc.gpsimd.memset(mask[:, :], 1.0).then_inc(made, 1)
            pool.wait_ge(made, 2)
            nc.gpsimd.affine_select(out=ident[:, :], in_=ident[:, :], compare_op=ALU.not_equal, fill=1.0, base=0,
                                    pattern=[[-1, P]], channel_multiplier=1).then_inc(made, 1)
            nc.gpsimd.affine_select(out=mask[:, :], in_=mask[:, :], compare_op=ALU.is_ge, fill=0.0, base=0,
                                    pattern=[[1, P]], channel_multiplier=-1).then_inc(made, 1)
            pool.wait_ge(made, 4)
            nc.gpsimd.tensor_copy(ident16[:, :], ident[:, :]).then_inc(made, 1)
            nc.gpsimd.tensor_copy(ident_bf[:, :], ident[:, :]).then_inc(made, 1)
            pool.wait_ge(made, 6)
    return x_res, (ident, mask, minus_half, ident16, ident_bf)
PE_TURNS = [("z", 0), ("z", 1), ("z", 2), ("q", 0), ("k", 0), ("z", 3),
         ("q", 1), ("k", 1), ("q", 2), ("k", 2), ("q", 3), ("k", 3)]


def turn_bank(what, t):
    return PE_TURNS.index((what, t)) % 2


def self_attention(nc, x_dram, w_dram, gamma_dram, beta_dram, wkv_dram, wkv_in, stage, x_res, ident, mask, minus_half):
    with ExitStack() as ctx:
        def sb(name, shape, dt):
            return ctx.enter_context(nc.sbuf_tensor(name, shape, dt))

        def psum(name, shape, dt):
            return ctx.enter_context(nc.psum_tensor(name, shape, dt))

        def sem(name):
            return ctx.enter_context(nc.semaphore("sa_" + name))

        w_hi = sb("sa_w_hi", [P, 4, CK, C], F32R)
        w_lo = sb("sa_w_lo", [P, 4, CK, C], F32R)
        att = stage[:, :, :].rearrange("p (k h) n -> p k h n", k=BT)
        w_raw = att[:, :, :, :]
        gam = sb("sa_gam", [P, C], F32)
        bet = sb("sa_bet", [P, C], F32)
        stats = sb("sa_stats", [P, 2, 6], F32)
        mv = sb("sa_mv", [P, TT, 2], F32)
        ve = sb("sa_ve", [P, TT], F32)
        rstd = sb("sa_rstd", [P, TT], F32)
        z = sb("sa_z", [P, 2, C], F32)
        z_hi = sb("sa_z_hi", [P, 2, CK, P], F32R)
        z_lo = sb("sa_z_lo", [P, 2, CK, P], F32R)
        y = sb("sa_y", [P, 2, 2 * H, D], F32)
        sq = sb("sa_sq", [P, 2, 2 * H, D], F32)
        msum = sb("sa_msum", [P, 2, 2 * H], F32)
        vsum = sb("sa_vsum", [P, 2, 2 * H], F32)
        root = sb("sa_root", [P, 2, 2 * H], F32)
        rsq = sb("sa_rsq", [P, 2, 2 * H], F32)
        qT = sb("sa_qT", [P, HG, S], F32)
        kT = sb("sa_kT", [P, HG, S], F32)
        kz = sb("sa_kz", [P, 2, GH, S], F32)
        v = sb("sa_v", [P, BT, C], F32)
        ones = sb("sa_ones", [P, D], F32)
        eps = sb("sa_eps", [P, 2], F32)
        rec = sb("sa_rec", [P, S], F32)
        oT_hi = sb("sa_oT_hi", [P, HG, S], F32R)
        oT_lo = sb("sa_oT_lo", [P, HG, S], F32R)
        o32 = sb("sa_o32", [P, S], F32)

        tb = [psum(f"sa_tb{i}", [P, 512], F32) for i in range(2)]
        pj = [psum(f"sa_pj{i}", [P, 512], F32) for i in range(2)]
        sc = [psum(f"sa_sc{i}", [P, 512], F32) for i in range(GH)]
        nd = [(pj[0], pj[1]), (tb[0], tb[1])]

        x_in = [sem(f"x_in{b}") for b in range(B)]
        gb_in = sem("gb_in")
        w_in = [sem(f"w_in{m}") for m in range(4)]
        gamma_q_ok = sem("gamma_q_ok")
        gamma_k_ok = sem("gamma_k_ok")
        lo_q_ok = sem("lo_q_ok")
        wo_hi_ok = sem("wo_hi_ok")
        w_hi_ok = sem("w_hi_ok")
        w_split = sem("w_split")
        dve = sem("dve")
        ve_ok = sem("ve_ok")
        rstd_ok = sem("rstd_ok")
        z_ok = sem("z_ok")
        zT_ok = sem("zT_ok")
        zhi_ok = sem("zhi_ok")
        zlo_ok = sem("zlo_ok")
        qkv_ok = sem("qkv_ok")
        qk_read = sem("qk_read")
        v_read = sem("v_read")
        c_ok = sem("c_ok")
        sq_ok = sem("sq_ok")
        vs_ok = sem("vs_ok")
        root_ok = sem("root_ok")
        n_ok = sem("n_ok")
        qkT_ok = sem("qkT_ok")
        qkT_read = sem("qkT_read")
        made_ok = sem("made_ok")
        kz_ok = sem("kz_ok")
        s_ok = sem("s_ok")
        att_ok = sem("att_ok")
        masked = sem("masked")
        av_ok = sem("av_ok")
        o32_ok = sem("o32_ok")
        ohi_ok = sem("ohi_ok")
        olo_ok = sem("olo_ok")
        out_ok = sem("out_ok")
        out_read = sem("out_read")

        block = ctx.enter_context(nc.Block(no_gpsimd_drain=True))
        x_tiles = x_dram.rearrange("(t p) c -> p t c", p=P)

        @block.sync
        def _(sp):
            def load_x(b):
                sp.dma_start(x_res[:, BT * b:BT * (b + 1), :], x_tiles[:, BT * b:BT * (b + 1), :]).then_inc(x_in[b], 16)

            def load_w(m):
                sp.dma_start(w_raw[:, m, :, :], w_dram[m].rearrange("(k p) n -> p k n", p=P)).then_inc(w_in[m], 16)
            load_x(0)
            sp.dma_start(gam[:, :], gamma_dram.partition_broadcast(P)).then_inc(gb_in, 16)
            sp.dma_start(bet[:, :], beta_dram.partition_broadcast(P)).then_inc(gb_in, 16)
            load_w(0)
            load_x(1)
            load_w(1)
            load_w(2)
            load_w(3)
            sp.wait_ge(av_ok, B * HG * BT)
            wkv = wkv_dram.rearrange("(k p) n -> p k n", p=P)
            for m in range(2):
                sp.dma_start(wkv_place(stage)[:, :, m * C:(m + 1) * C], wkv[:, :, m * C:(m + 1) * C]).then_inc(wkv_in[m], 16)

        @block.gpsimd
        def _(pool):
            pool.memset(ones[:, :], 1.0).then_inc(made_ok, 1)
            pool.memset(eps[:, 0:1], ATT_EPS * D).then_inc(made_ok, 1)
            pool.memset(eps[:, 1:2], ATT_EPS).then_inc(made_ok, 1)
            pool.memset(kz[:, :, :, :], 0.0).then_inc(made_ok, 1)
            def power(b):
                pool.wait_ge(ve_ok, b + 1)
                tiles = slice(BT * b, BT * (b + 1))
                pool.tensor_tensor(rstd[:, tiles], ve[:, tiles], minus_half[:, 0:BT], ALU.pow).then_inc(rstd_ok, 1)
            power(0)
            pool.wait_ge(gb_in, 32)
            pool.wait_ge(w_in[1], 16)
            pool.tensor_tensor(w_raw[:, 1, :, :], w_raw[:, 1, :, :], gam[:, :].unsqueeze(1).broadcast_to([P, CK, C]),
                               ALU.mult).then_inc(gamma_k_ok, 1)
            for m in (1, 2, 3):
                if m < 3:
                    pool.wait_ge(w_hi_ok, m + 1)
                else:
                    power(1)
                    pool.wait_ge(w_in[m], 16)
                    pool.tensor_copy(w_hi[:, m, :, :], w_raw[:, m, :, :]).then_inc(wo_hi_ok, 1)
                    pool.wait_ge(wo_hi_ok, 1)
                pool.tensor_tensor(w_lo[:, m, :, :], w_raw[:, m, :, :], w_hi[:, m, :, :].bitcast(F32),
                                   ALU.subtract).then_inc(w_split, 1)
            with pool.Fori(0, B) as b:
                for hg in range(HG):
                    for kt in range(BT):
                        diag = att[:, kt, :, kt * P:(kt + 1) * P]
                        pool.wait_ge(att_ok, (b * HG * BT + hg * BT + kt + 1) * GH)
                        pool.tensor_tensor(diag, diag, mask[:, :].unsqueeze(1).broadcast_to([P, GH, P]),
                                           ALU.mult).then_inc(masked, 1)

        @block.scalar
        def _(act):
            act.wait_ge(made_ok, 4)
            for m in range(3):
                act.wait_ge(*((gamma_q_ok, 1), (gamma_k_ok, 1), (w_in[2], 16))[m])
                nc.scalar.copy(w_hi[:, m, :, :], w_raw[:, m, :, :]).then_inc(w_hi_ok, 1)

            def read_z(b, t):
                n = BT * b + t
                act.wait_ge(zT_ok, n + 1)
                nc.scalar.copy(row_halves(z_hi[:, t % 2, :, :].rearrange("p k n -> p (k n)"), CK),
                               row_halves(tb[turn_bank("z", t)][:, :], CK)).then_inc(zhi_ok, 1)

            def read_qkT(b, t):
                n = BT * b + t
                for i, (what, dst) in enumerate((("q", qT), ("k", kT))):
                    act.wait_ge(qkT_ok, 2 * n + i + 1)
                    nc.scalar.copy(dst[:, :, t * P:(t + 1) * P],
                                   row_halves(tb[turn_bank(what, t)][:, :], HG)).then_inc(qkT_read, 1)

            with act.Fori(0, B) as b:
                read_z(b, 0)
                for t in range(BT):
                    n = BT * b + t
                    if t + 1 < BT:
                        read_z(b, t + 1)
                    act.wait_ge(qkv_ok, 3 * n + 3)
                    nc.scalar.copy(v[:, t, :], pj[(3 * t + 2) % 2][:, :]).then_inc(v_read, 1)
                    if t >= 1:
                        read_qkT(b, t - 1)
                    act.wait_ge(c_ok, n + 1)
                    nc.scalar.activation(sq[:, t % 2, :, :], y[:, t % 2, :, :], ACT.Square).then_inc(sq_ok, 1)
                    act.wait_ge(vs_ok, n + 1)
                    nc.scalar.activation(root[:, t % 2, 0:H], vsum[:, t % 2, 0:H], ACT.Sqrt, bias=eps[:, 0:1])
                    nc.scalar.activation(root[:, t % 2, H:2 * H], vsum[:, t % 2, H:2 * H], ACT.Sqrt, bias=eps[:, 1:2],
                                         scale=1.0 / D).then_inc(root_ok, 1)
                read_qkT(b, BT - 1)
                act.wait_ge(w_split, 3)
                def high_out(hg):
                    act.wait_ge(o32_ok, b * HG + hg + 1)
                    nc.scalar.copy(oT_hi[:, hg, :], o32[:, :]).then_inc(ohi_ok, 1)

                for hg in range(HG):
                    for kt in range(BT):
                        if hg > 0:
                            act.wait_ge(av_ok, (b * HG + hg - 1) * BT + kt + 1)
                        for j in range(GH):
                            act.wait_ge(s_ok, ((b * HG + hg) * BT + kt) * GH + j + 1)
                            nc.scalar.activation(att[:, kt, j, kt * P:S], sc[j][:, kt * P:S],
                                                 ACT.Square).then_inc(att_ok, 1)
                    if hg > 0:
                        high_out(hg - 1)
                high_out(HG - 1)

        @block.vector
        def _(v_):
            links = [0]

            def link(ins, base=0):
                links[0] += 1
                ins.then_inc(dve, 1)
                v_.wait_ge(dve, base + links[0])

            def statistics(b):
                v_.wait_ge(x_in[b], 16)
                for t in range(BT * b, BT * (b + 1)):
                    link(nc.vector.bn_stats(stats[:, t % 2, :], x_res[:, t, :]))
                    link(nc.vector.bn_aggr(mv[:, t, :], stats[:, t % 2, :]))
                tiles = slice(BT * b, BT * (b + 1))
                nc.vector.tensor_scalar(ve[:, tiles], mv[:, tiles, 1], LN_EPS, None, ALU.add).then_inc(ve_ok, 1)

            statistics(0)
            v_.wait_ge(gb_in, 32)
            v_.wait_ge(w_in[0], 16)
            nc.vector.tensor_tensor(w_raw[:, 0, :, :], w_raw[:, 0, :, :],
                                    gam[:, :].unsqueeze(1).broadcast_to([P, CK, C]), ALU.mult).then_inc(gamma_q_ok, 1)
            statistics(1)
            v_.wait_ge(w_hi_ok, 1)
            nc.vector.tensor_tensor(w_lo[:, 0, :, :], w_raw[:, 0, :, :], w_hi[:, 0, :, :].bitcast(F32),
                                    ALU.subtract).then_inc(lo_q_ok, 1)
            v_.wait_ge(made_ok, 4)
            head = links[0]
            LINKS = 2 * BT + 2 * HG

            with v_.Fori(0, B) as b:
                links[0] = 0
                base = head + b * LINKS

                def norm(t):
                    n = BT * b + t
                    if t >= 2:
                        v_.wait_ge(zT_ok, n - 1)
                    nc.vector.tensor_scalar(z[:, t % 2, :], x_res[:, n, :], mv[:, n, 0:1], rstd[:, bass.ds(n, 1)],
                                            ALU.subtract, ALU.mult).then_inc(z_ok, 1)

                def low_z(t):
                    n = BT * b + t
                    v_.wait_ge(zhi_ok, n + 1)
                    nc.vector.tensor_tensor(z_lo[:, t % 2, :, :], row_halves(tb[turn_bank("z", t)][:, :], CK),
                                            z_hi[:, t % 2, :, :].bitcast(F32), ALU.subtract).then_inc(zlo_ok, 1)

                def add_beta(t):
                    n = BT * b + t
                    for i in range(2):
                        v_.wait_ge(qkv_ok, 3 * n + i + 1)
                        nc.vector.tensor_tensor(y[:, t % 2, i * H:(i + 1) * H, :].rearrange("p h d -> p (h d)"),
                                                pj[(3 * t + i) % 2][:, :], bet[:, :], ALU.add).then_inc(qk_read, 1)

                def variances(t):
                    n = BT * b + t
                    v_.wait_ge(qk_read, 2 * n + 2)
                    link(nc.vector.tensor_reduce(msum[:, t % 2, :], y[:, t % 2, :, :], AX_X, ALU.add), base)
                    nc.vector.scalar_tensor_tensor(out=y[:, t % 2, :, :],
                                                   in0=msum[:, t % 2, :].unsqueeze(2).broadcast_to([P, 2 * H, D]),
                                                   scalar=-1.0 / D, in1=y[:, t % 2, :, :],
                                                   op0=ALU.mult, op1=ALU.add).then_inc(c_ok, 1)
                    v_.wait_ge(sq_ok, n + 1)
                    nc.vector.tensor_reduce(vsum[:, t % 2, :], sq[:, t % 2, :, :], AX_X, ALU.add).then_inc(vs_ok, 1)

                def finish_features(t):
                    n = BT * b + t
                    v_.wait_ge(root_ok, n + 1)
                    link(nc.vector.reciprocal(rsq[:, t % 2, :], root[:, t % 2, :]), base)
                    nc.vector.tensor_tensor(y[:, t % 2, :, :], y[:, t % 2, :, :],
                                            rsq[:, t % 2, :].unsqueeze(2).broadcast_to([P, 2 * H, D]),
                                            ALU.mult).then_inc(n_ok, 1)

                v_.wait_ge(rstd_ok, b + 1)
                norm(0)
                norm(1)
                low_z(0)
                for t in range(BT):
                    if t + 1 < BT:
                        low_z(t + 1)
                    if t + 2 < BT:
                        norm(t + 2)
                    if t >= 2:
                        v_.wait_ge(qkT_ok, 2 * (BT * b + t - 1))
                    add_beta(t)
                    if t >= 1:
                        finish_features(t - 1)
                    variances(t)
                finish_features(BT - 1)

                def spread_k(hg):
                    for j in range(GH):
                        rows = slice(D * j, D * (j + 1))
                        nc.vector.tensor_copy(kz[rows, hg % 2, j, :], kT[rows, hg, :]).then_inc(kz_ok, 1)

                v_.wait_ge(qkT_read, 2 * BT * (b + 1))
                spread_k(0)
                spread_k(1)
                for hg in range(HG):
                    num, den = nd[hg % 2]
                    n = HG * b + hg
                    v_.wait_ge(av_ok, BT * (n + 1))
                    if hg + 2 < HG:
                        spread_k(hg + 2)
                    link(nc.vector.tensor_scalar(rec[:, :], den[:, :], ATT_EPS, None, ALU.add), base)
                    link(nc.vector.reciprocal(rec[:, :], rec[:, :]), base)
                    if hg:
                        v_.wait_ge(olo_ok, n)
                    nc.vector.tensor_tensor(o32[:, :], num[:, :], rec[:, :], ALU.mult).then_inc(o32_ok, 1)
                    v_.wait_ge(ohi_ok, n + 1)
                    nc.vector.tensor_tensor(oT_lo[:, hg, :], o32[:, :], oT_hi[:, hg, :].bitcast(F32),
                                            ALU.subtract).then_inc(olo_ok, 1)
                for t in range(BT):
                    n = BT * b + t
                    v_.wait_ge(out_ok, n + 1)
                    nc.vector.tensor_tensor(x_res[:, n, :], x_res[:, n, :], pj[t % 2][:, :],
                                            ALU.add).then_inc(out_read, 1)
                assert links[0] == LINKS

        @block.tensor
        def _(pe):
            def project(out, hi, lo, m, count, chunks=range(CK)):
                for k in chunks:
                    for i, (a, w) in enumerate(((hi, w_hi), (lo, w_hi), (hi, w_lo))):
                        ins = nc.tensor.matmul(out, a(k), w[:, m, k, :], start=(k == 0 and i == 0),
                                               stop=(k == CK - 1 and i == 2))
                if k == CK - 1:
                    ins.then_inc(count, 1)

            def bank_free(b, what, t):
                turn = PE_TURNS.index((what, t))
                if turn >= 2:
                    what, t = PE_TURNS[turn - 2]
                    if what == "z":
                        pe.wait_ge(zlo_ok, BT * b + t + 1)
                    else:
                        pe.wait_ge(qkT_read, 2 * (BT * b + t) + (what == "k") + 1)

            def transpose_z(b, t):
                n = BT * b + t
                pe.wait_ge(z_ok, n + 1)
                bank_free(b, "z", t)
                for k in range(CK):
                    ins = nc.tensor.transpose(tb[turn_bank("z", t)][:, k * P:(k + 1) * P], z[:, t % 2, k * P:(k + 1) * P],
                                              ident[:, :])
                ins.then_inc(zT_ok, 1)

            def transpose_qk(b, t):
                n = BT * b + t
                pe.wait_ge(n_ok, n + 1)
                for i, what in enumerate("qk"):
                    bank_free(b, what, t)
                    for g in range(HG):
                        ins = nc.tensor.transpose(
                            tb[turn_bank(what, t)][:, g * P:(g + 1) * P],
                            y[:, t % 2, i * H + g * GH:i * H + (g + 1) * GH, :].rearrange("p h d -> p (h d)"),
                            ident[:, :])
                    ins.then_inc(qkT_ok, 1)

            pe.wait_ge(made_ok, 4)
            with pe.Fori(0, B) as b:
                transpose_z(b, 0)
                for t in range(BT):
                    n = BT * b + t
                    if t + 1 < BT:
                        transpose_z(b, t + 1)
                    pe.wait_ge(zlo_ok, n + 1)
                    for m in range(3):
                        if t == 0:
                            pe.wait_ge(*((lo_q_ok, 1), (w_split, 1), (w_split, 2))[m])
                        if 3 * t + m >= 2:
                            tenant = 3 * t + m - 2
                            if tenant % 3 == 2:
                                pe.wait_ge(v_read, BT * b + tenant // 3 + 1)
                            else:
                                pe.wait_ge(qk_read, 2 * (BT * b + tenant // 3) + tenant % 3 + 1)
                        project(pj[(3 * t + m) % 2][:, :], lambda k: z_hi[:, t % 2, k, :],
                                lambda k: z_lo[:, t % 2, k, :], m, qkv_ok)
                    if t >= 1:
                        transpose_qk(b, t - 1)
                transpose_qk(b, BT - 1)
                pe.wait_ge(qkT_read, 2 * BT * (b + 1))
                pe.wait_ge(v_read, BT * (b + 1))
                for hg in range(HG):
                    for kt in range(BT):
                        for j in range(GH):
                            if kt == 0:
                                pe.wait_ge(kz_ok, (b * HG + hg) * GH + j + 1)
                            if hg or kt:
                                pe.wait_ge(att_ok, ((b * HG + hg) * BT + kt - 1) * GH + j + 1)
                            nc.tensor.matmul(sc[j][:, kt * P:S], kz[:, hg % 2, j, kt * P:(kt + 1) * P],
                                             qT[:, hg, kt * P:S], start=True, stop=True).then_inc(s_ok, 1)
                    num, den = nd[hg % 2]
                    if hg >= 2:
                        pe.wait_ge(o32_ok, HG * b + hg - 1)
                    for kt in range(BT):
                        pe.wait_ge(masked, (b * HG + hg) * BT + kt + 1)
                        for j in range(GH):
                            rows = slice(D * j, D * (j + 1))
                            nc.tensor.matmul(num[rows, kt * P:S], v[:, kt, (hg * GH + j) * D:(hg * GH + j + 1) * D],
                                             att[:, kt, j, kt * P:S], start=(kt == 0), stop=(kt == BT - 1))
                        for j in range(GH):
                            rows = slice(D * j, D * (j + 1))
                            ins = nc.tensor.matmul(den[rows, kt * P:S], ones[:, :],
                                                   att[:, kt, j, kt * P:S], start=(kt == 0), stop=(kt == BT - 1))
                            if j == GH - 1:
                                ins.then_inc(av_ok, 1)
                pe.wait_ge(w_split, 3)

                def output(t, groups):
                    project(pj[t % 2][:, :], lambda k: oT_hi[:, k, t * P:(t + 1) * P],
                            lambda k: oT_lo[:, k, t * P:(t + 1) * P], 3, out_ok, groups)
                pe.wait_ge(olo_ok, HG * (b + 1) - 1)
                for t in range(2):
                    output(t, range(HG - 1))
                pe.wait_ge(olo_ok, HG * (b + 1))
                for t in range(2):
                    output(t, [HG - 1])
                for t in range(2, BT):
                    pe.wait_ge(out_read, BT * b + t - 1)
                    output(t, range(HG))
                pe.wait_ge(out_read, BT * (b + 1))
LOOP_TILES = 4
BLOCK_TILES = 2
BLOCKS = LOOP_TILES // BLOCK_TILES


def there(n, count):
    return not isinstance(n, int) or 0 <= n < count


def at_least(n, first):
    return not isinstance(n, int) or n >= first


def wkv_place(stage):
    return stage[:, KT - 2 * CK:KT, :].rearrange("p (k m) c -> p k (m c)", k=CK)


def normalise_statistics(v_, nc, x_res, stats, mv, ve, chain, ve_ok):
    for t in range(TT):
        nc.vector.bn_stats(stats[:, t, :], x_res[:, t, :]).then_inc(chain, 1)
    v_.wait_ge(chain, TT)
    for t in range(TT):
        nc.vector.bn_aggr(mv[:, t, :], stats[:, t, :]).then_inc(chain, 1)
    v_.wait_ge(chain, 2 * TT)
    nc.vector.tensor_scalar(ve[:, :], mv[:, :, 1], LN_EPS, None, ALU.add).then_inc(ve_ok, 1)


def context_keys_values(nc, ctxT_dram, wkv_in, wq_dram, wq_raw, wq_in, bkv_dram, k_parts, v_raw, v_top,
                        x_res, mv, rstd, minus_half, ident_bf):
    with ExitStack() as ctx:
        def sb(name, shape, dt):
            return ctx.enter_context(nc.sbuf_tensor(name, shape, dt))

        def psum(name, shape, dt):
            return ctx.enter_context(nc.psum_tensor(name, shape, dt))

        def sem(name):
            return ctx.enter_context(nc.semaphore("ck_" + name))

        w_raw = wkv_place(v_raw)
        w_hi = sb("ck_w_hi", [P, CK, 2 * C], F32R)
        w_lo = sb("ck_w_lo", [P, CK, 2 * C], F32R)
        raw = sb("ck_raw", [P, BLOCKS, CK, BLOCK_TILES * P], F32)
        c_hi = sb("ck_c_hi", [P, 2, CK, P], F32R)
        c_lo = sb("ck_c_lo", [P, 2, CK, P], F32R)
        bias = sb("ck_bias", [P, 2 * C], F32)
        kf = sb("ck_kf", [P, H, D], F32)
        kint = sb("ck_kint", [P, 2, H, D], F32)
        kq = sb("ck_kq", [P, H, D], F32)
        rest = sb("ck_rest", [P, 2, H, D], F32)
        step = sb("ck_step", [P, 2, H], F32)
        rstep = sb("ck_rstep", [P, H], F32)
        parts = sb("ck_parts", [P, 2, H, 3, D], BF16)
        turn_top = sb("ck_turn_top", [P, C], F32)
        own_top = sb("ck_own_top", [P, C], F32)
        stats = sb("ck_stats", [P, TT, 6], F32)
        ve = sb("ck_ve", [P, TT], F32)

        kb = [psum(f"ck_kb{i}", [P, C], F32) for i in range(2)]
        vb = [psum(f"ck_vb{i}", [P, C], F32) for i in range(2)]
        tr = [psum(f"ck_tr{i}", [3 * D, H, P], BF16) for i in range(2)]

        w_in = wkv_in
        b_in = sem("b_in")
        raw_in = [sem(f"raw_in{i}") for i in range(BLOCKS)]
        whi_ok = sem("whi_ok")
        wklo_ok = sem("wklo_ok")
        wvlo_ok = sem("wvlo_ok")
        chi_ok = sem("chi_ok")
        clo_ok = sem("clo_ok")
        k_ok = sem("k_ok")
        v_ok = sem("v_ok")
        kf_ok = sem("kf_ok")
        vf_ok = sem("vf_ok")
        kint_ok = sem("kint_ok")
        kq_ok = sem("kq_ok")
        hi_ok = sem("hi_ok")
        rest_ok = sem("rest_ok")
        mid_ok = sem("mid_ok")
        lo_ok = sem("lo_ok")
        tr_ok = sem("tr_ok")
        tr_read = sem("tr_read")
        turn_ok = sem("turn_ok")
        top_ok = sem("top_ok")
        all_top = sem("all_top")
        chain = sem("chain")
        ve_ok = sem("ve_ok")
        rstd_ok = sem("rstd_ok")
        dve = sem("dve")

        block = ctx.enter_context(nc.Block(no_gpsimd_drain=True))
        ctxT = ctxT_dram.rearrange("(k p) n -> p k n", p=P)
        TURNS = KT // LOOP_TILES
        LAG = 4

        def tiles(engine, step_of):
            for t in range(LOOP_TILES):
                step_of(t, t, 0)
            with engine.Fori(1, TURNS) as i:
                for t in range(LOOP_TILES):
                    step_of(t, i * LOOP_TILES + t, i)
            for n in range(KT, KT + LAG):
                step_of(n % LOOP_TILES, n, TURNS)

        def raw_tile(t):
            return raw[:, t // BLOCK_TILES, :, t % BLOCK_TILES * P:(t % BLOCK_TILES + 1) * P]

        @block.sync
        def _(sp):
            def load(g, slot):
                sp.dma_start(raw[:, slot, :, :], ctxT[:, :, bass.ds(g * BLOCK_TILES * P, BLOCK_TILES * P)])\
                  .then_inc(raw_in[slot], 16)

            for slot in range(BLOCKS):
                load(slot, slot)
            sp.dma_start(bias[:, :], bkv_dram.partition_broadcast(P)).then_inc(b_in, 16)
            sp.dma_start(wq_raw, wq_dram.rearrange("(k p) n -> p k n", p=P)).then_inc(wq_in, 16)
            with sp.Fori(1, TURNS) as i:
                for slot in range(BLOCKS):
                    sp.wait_ge(clo_ok, (i - 1) * LOOP_TILES + (slot + 1) * BLOCK_TILES)
                    load(i * BLOCKS + slot, slot)

        @block.gpsimd
        def _(pool):
            def low_context(t, n):
                pool.wait_ge(chi_ok, n + 1)
                nc.gpsimd.tensor_tensor(c_lo[:, t % 2, :, :], raw_tile(t), c_hi[:, t % 2, :, :].bitcast(F32),
                                        ALU.subtract).then_inc(clo_ok, 1)

            low_context(0, 0)
            def step_of(t, n, turn):
                if there(n, KT):
                    if not (isinstance(n, int) and n == 0):
                        low_context(t, n)
                if there(n - 2, KT):
                    u = t % 2
                    pool.wait_ge(kint_ok, n - 1)
                    if at_least(n, 3):
                        pool.wait_ge(rest_ok, n - 2)
                    nc.gpsimd.tensor_tensor(kq[:, :, :], kint[:, u, :, :],
                                            step[:, u, :].unsqueeze(2).broadcast_to([P, H, D]), ALU.mult).then_inc(kq_ok, 1)
                    pool.wait_ge(hi_ok, n - 1)
                    if at_least(n, 4):
                        pool.wait_ge(lo_ok, n - 3)
                    nc.gpsimd.tensor_tensor(rest[:, u, :, :], kq[:, :, :], parts[:, u, :, 0, :],
                                            ALU.subtract).then_inc(rest_ok, 1)
                if isinstance(n, int) and n == LOOP_TILES - 1:
                    pool.wait_ge(ve_ok, 1)
                    nc.gpsimd.tensor_tensor(rstd[:, :], ve[:, :], minus_half[:, 0:TT], ALU.pow).then_inc(rstd_ok, 1)
            tiles(pool, step_of)
            pool.wait_ge(top_ok, TURNS)
            nc.gpsimd.partition_all_reduce(v_top[:, :], own_top[:, :], P, ABSMAX).then_inc(all_top, 1)
            pool.wait_ge(all_top, 1)
            pool.wait_ge(rstd_ok, 1)

        @block.scalar
        def _(act):
            for m in range(2):
                act.wait_ge(w_in[m], 16)
                nc.scalar.copy(w_hi[:, :, m * C:(m + 1) * C], w_raw[:, :, m * C:(m + 1) * C]).then_inc(whi_ok, 1)
                if m == 0:
                    act.wait_ge(raw_in[0], 16)
                    nc.scalar.copy(c_hi[:, 0, :, :], raw_tile(0)).then_inc(chi_ok, 1)

            def step_of(t, n, turn):
                u = t % 2
                if there(n, KT) and not (isinstance(n, int) and n == 0):
                    if t % BLOCK_TILES == 0:
                        act.wait_ge(raw_in[t // BLOCK_TILES], 16 * turn + 16)
                    if at_least(n, 2):
                        act.wait_ge(v_ok, n - 1)
                    nc.scalar.copy(c_hi[:, u, :, :], raw_tile(t)).then_inc(chi_ok, 1)
                if there(n - 4, KT):
                    act.wait_ge(tr_ok, n - 3)
                    nc.scalar.copy(k_parts[0:3 * D, :, bass.ds((n - 4) * P, P)], tr[u][:, :, :]).then_inc(tr_read, 1)
                if there(n - 2, KT):
                    act.wait_ge(kq_ok, n - 1)
                    nc.scalar.copy(parts[:, u, :, 0, :], kq[:, :, :]).then_inc(hi_ok, 1)
                    act.wait_ge(rest_ok, n - 1)
                    nc.scalar.copy(parts[:, u, :, 1, :], rest[:, u, :, :]).then_inc(mid_ok, 1)
            tiles(act, step_of)

        @block.vector
        def _(v_):
            def per_head(x):
                return x.unsqueeze(2).broadcast_to([P, H, D])

            LINKS = 4

            def step_of(t, n, turn):
                u = t % 2
                if there(n, KT):
                    links = [0]

                    def link(ins):
                        links[0] += 1
                        ins.then_inc(dve, 1)
                        v_.wait_ge(dve, n * LINKS + links[0])

                    if at_least(n, 1):
                        v_.wait_ge(kint_ok, n)
                    v_.wait_ge(k_ok, n + 1)
                    nc.vector.tensor_tensor(kf[:, :, :], kb[u][:, :].rearrange("p (h d) -> p h d", h=H),
                                            bias[:, 0:C].rearrange("p (h d) -> p h d", h=H), ALU.add).then_inc(kf_ok, 1)
                    v_.wait_ge(kf_ok, n + 1)
                    link(nc.vector.tensor_reduce(rstep[:, :], kf[:, :, :], AX_X, ALU.max, apply_absolute_value=True))
                    if at_least(n, 2):
                        v_.wait_ge(kq_ok, n - 1)
                    link(nc.vector.tensor_scalar(step[:, u, :], rstep[:, :], 1.0 / QMAX, Q_FLOOR, ALU.mult, ALU.max))
                    link(nc.vector.reciprocal(rstep[:, :], step[:, u, :]))
                    link(nc.vector.tensor_tensor(kf[:, :, :], kf[:, :, :], per_head(rstep[:, :]), ALU.mult))
                    nc.vector.tensor_scalar(kint[:, u, :, :], kf[:, :, :], MAGIC, MAGIC, ALU.add,
                                            ALU.subtract).then_inc(kint_ok, 1)
                    if t == LOOP_TILES - 1 and not isinstance(n, int):
                        v_.wait_ge(top_ok, turn)
                    v_.wait_ge(v_ok, n + 1)
                    nc.vector.tensor_tensor(v_raw[:, bass.ds(n, 1), :].rearrange("p a c -> p (a c)"), vb[u][:, :],
                                            bias[:, C:2 * C], ALU.add).then_inc(vf_ok, 1)
                    assert links[0] == LINKS
                turn_done = there(n, KT) and t == LOOP_TILES - 1
                if turn_done:
                    v_.wait_ge(vf_ok, n + 1)
                if there(n - 1, KT):
                    v_.wait_ge(mid_ok, n)
                    nc.vector.tensor_tensor(parts[:, 1 - u, :, 2, :], rest[:, 1 - u, :, :], parts[:, 1 - u, :, 1, :],
                                            ALU.subtract).then_inc(lo_ok, 1)
                if turn_done:
                    first = isinstance(n, int)
                    nc.vector.tensor_reduce((own_top if first else turn_top)[:, :],
                                            v_raw[:, bass.ds(n - t, LOOP_TILES), :].rearrange("p t c -> p c t"),
                                            AX_X, ALU.max, apply_absolute_value=True)\
                        .then_inc(top_ok if first else turn_ok, 1)
                    if not first:
                        v_.wait_ge(turn_ok, turn)
                        nc.vector.tensor_tensor(own_top[:, :], own_top[:, :], turn_top[:, :], ALU.max).then_inc(top_ok, 1)

            for m, made in enumerate((wklo_ok, wvlo_ok)):
                v_.wait_ge(whi_ok, m + 1)
                cols = slice(m * C, (m + 1) * C)
                nc.vector.tensor_tensor(w_lo[:, :, cols], w_raw[:, :, cols], w_hi[:, :, cols].bitcast(F32),
                                        ALU.subtract).then_inc(made, 1)
            normalise_statistics(v_, nc, x_res, stats, mv, ve, chain, ve_ok)
            v_.wait_ge(b_in, 16)
            tiles(v_, step_of)

        @block.tensor
        def _(pe):
            def step_of(t, n, turn):
                u = t % 2
                if there(n, KT):
                    pe.wait_ge(clo_ok, n + 1)
                    for out, m, read, made, lo_in in ((kb, 0, kf_ok, k_ok, wklo_ok), (vb, 1, vf_ok, v_ok, wvlo_ok)):
                        if at_least(n, 2):
                            pe.wait_ge(read, n - 1)
                        else:
                            pe.wait_ge(lo_in, 1)
                        for k in range(CK):
                            for j, (a, w) in enumerate(((c_hi, w_hi), (c_lo, w_hi), (c_hi, w_lo))):
                                ins = nc.tensor.matmul(out[u][:, :], a[:, u, k, :], w[:, k, m * C:(m + 1) * C],
                                                       start=(k == 0 and j == 0), stop=(k == CK - 1 and j == 2))
                        ins.then_inc(made, 1)
                if there(n - 2, KT):
                    pe.wait_ge(lo_ok, n - 1)
                    if at_least(n, 4):
                        pe.wait_ge(tr_read, n - 3)
                    for h in range(H):
                        ins = nc.tensor.transpose(tr[u][:, h, :], parts[:, u, h, :, :].rearrange("p a d -> p (a d)"),
                                                  ident_bf[:, :])
                    ins.then_inc(tr_ok, 1)
            tiles(pe, step_of)


HALF = KEYS // 2
HKT = KT // 2


def cross_queries(nc, w_raw, w_in, bq_dram, x_res, mv, rstd, q_int, q_step, q_nstep, v_raw, v_int, v_step,
                  ident, ident_bf):
    scale = float(D) ** -0.5
    with ExitStack() as ctx:
        def sb(name, shape, dt):
            return ctx.enter_context(nc.sbuf_tensor(name, shape, dt))

        def psum(name, shape, dt):
            return ctx.enter_context(nc.psum_tensor(name, shape, dt))

        def sem(name):
            return ctx.enter_context(nc.semaphore("cq_" + name))

        w_hi = sb("cq_w_hi", [P, CK, C], F32R)
        w_lo = sb("cq_w_lo", [P, CK, C], F32R)
        bias = sb("cq_bias", [P, C], F32)
        z = sb("cq_z", [P, 2, C], F32)
        z_hi = sb("cq_z_hi", [P, 2, CK, P], F32R)
        z_lo = sb("cq_z_lo", [P, 2, CK, P], F32R)
        qf = sb("cq_qf", [P, H, D], F32)
        step = sb("cq_step", [P, H], F32)
        rstep = sb("cq_rstep", [P, H], F32)
        q1 = sb("cq_q1", [P, 2, H, D], BF16)
        q3 = sb("cq_q3", [P, 2, H, 3, D], BF16)
        v_rstep = sb("cq_v_rstep", [P, C], F32)
        tz = [psum(f"cq_tz{i}", [P, C], F32) for i in range(2)]
        pq = [psum(f"cq_pq{i}", [P, C], F32) for i in range(2)]
        tq = [psum(f"cq_tq{i}", [3 * D, H, P], BF16) for i in range(2)]

        b_in = sem("b_in")
        whi_ok = sem("whi_ok")
        wlo_ok = sem("wlo_ok")
        z_ok = sem("z_ok")
        zT_ok = sem("zT_ok")
        zhi_ok = sem("zhi_ok")
        zlo_ok = sem("zlo_ok")
        pq_ok = sem("pq_ok")
        qf_ok = sem("qf_ok")
        q1_ok = sem("q1_ok")
        q3_ok = sem("q3_ok")
        tq_ok = sem("tq_ok")
        tq_read = sem("tq_read")
        v_rstep_ok = sem("v_rstep_ok")
        v_scaled = sem("v_scaled")
        dve = sem("dve")
        block = ctx.enter_context(nc.Block(no_gpsimd_drain=True))
        LAG = 3
        halves = (slice(0, CK // 2), slice(CK // 2, CK))
        V_TILES = KT // TT

        def tiles(engine, step_of):
            for n in range(4):
                step_of(n % 2, n)
            with engine.Fori(2, TT // 2) as i:
                for t in range(2):
                    step_of(t, 2 * i + t)
            for n in range(TT, TT + LAG):
                step_of(n % 2, n)

        @block.sync
        def _(sp):
            sp.dma_start(bias[:, :], bq_dram.partition_broadcast(P)).then_inc(b_in, 16)

        @block.gpsimd
        def _(pool):
            pool.wait_ge(v_rstep_ok, 1)

            def step_of(t, n):
                if there(n, TT):
                    v = v_raw[:, bass.ds(V_TILES * n, V_TILES), :]
                    nc.gpsimd.tensor_tensor(v, v, v_rstep[:, :].unsqueeze(1).broadcast_to([P, V_TILES, C]),
                                            ALU.mult).then_inc(v_scaled, 1)
            tiles(pool, step_of)

        @block.scalar
        def _(act):
            act.wait_ge(w_in, 16)
            for m in range(2):
                nc.scalar.copy(w_hi[:, halves[m], :], w_raw[:, halves[m], :]).then_inc(whi_ok, 1)

            def step_of(t, n):
                if there(n, TT):
                    act.wait_ge(zT_ok, n + 1)
                    if at_least(n, 2):
                        act.wait_ge(pq_ok, n - 1)
                    nc.scalar.copy(z_hi[:, t, :, :], row_halves(tz[t][:, :], CK)).then_inc(zhi_ok, 1)
                if there(n - 2, TT):
                    act.wait_ge(q1_ok, n - 1)
                    nc.scalar.copy(q3[:, t, :, :, :],
                                   q1[:, t, :, :].unsqueeze(2).broadcast_to([P, H, 3, D])).then_inc(q3_ok, 1)
                if there(n - 3, TT):
                    act.wait_ge(tq_ok, n - 2)
                    nc.scalar.copy(q_int[0:3 * D, bass.ds(n - 3, 1), :, :].rearrange("p a h n -> p (a h) n"),
                                   tq[1 - t][:, :, :]).then_inc(tq_read, 1)
            tiles(act, step_of)

        @block.vector
        def _(v_):
            def per_head(x):
                return x[:, :].unsqueeze(2).broadcast_to([P, H, D])

            LINKS = 4

            def norm(t, n):
                if at_least(n, 2):
                    v_.wait_ge(zT_ok, n - 1)
                nc.vector.tensor_scalar(z[:, t, :], x_res[:, n, :], mv[:, n, 0:1], rstd[:, bass.ds(n, 1)],
                                        ALU.subtract, ALU.mult).then_inc(z_ok, 1)

            def quantise(t, n):
                links = [0]

                def link(ins):
                    links[0] += 1
                    ins.then_inc(dve, 1)
                    v_.wait_ge(dve, 1 + n * LINKS + links[0])

                v_.wait_ge(pq_ok, n + 1)
                nc.vector.tensor_tensor(qf[:, :, :], pq[t][:, :].rearrange("p (h d) -> p h d", h=H),
                                        bias[:, :].rearrange("p (h d) -> p h d", h=H), ALU.add).then_inc(qf_ok, 1)
                v_.wait_ge(qf_ok, n + 1)
                link(nc.vector.tensor_reduce(rstep[:, :], qf[:, :, :], AX_X, ALU.max, apply_absolute_value=True))
                link(nc.vector.tensor_scalar(step[:, :], rstep[:, :], 1.0 / QMAX, Q_FLOOR / scale, ALU.mult, ALU.max))
                nc.vector.tensor_scalar(q_step[:, n, :], step[:, :], scale, None, ALU.mult)
                nc.vector.tensor_scalar(q_nstep[:, n, :], step[:, :], -scale, None, ALU.mult)
                link(nc.vector.reciprocal(rstep[:, :], step[:, :]))
                link(nc.vector.tensor_tensor(qf[:, :, :], qf[:, :, :], per_head(rstep), ALU.mult))
                if at_least(n, 2):
                    v_.wait_ge(q3_ok, n - 1)
                nc.vector.tensor_scalar(q1[:, t, :, :], qf[:, :, :], MAGIC, MAGIC, ALU.add,
                                        ALU.subtract).then_inc(q1_ok, 1)
                v_.wait_ge(q1_ok, n + 1)
                assert links[0] == LINKS

            def step_of(t, n):
                if there(n, TT):
                    norm(t, n)
                if there(n - 2, TT):
                    quantise(t, n - 2)
                    v_.wait_ge(v_scaled, n - 1)
                    nc.vector.tensor_scalar(v_int[:, bass.ds(V_TILES * (n - 2), V_TILES), :],
                                            v_raw[:, bass.ds(V_TILES * (n - 2), V_TILES), :], MAGIC, MAGIC,
                                            ALU.add, ALU.subtract)
                first = isinstance(n, int) and n == 0
                if first:
                    for m in range(2):
                        v_.wait_ge(whi_ok, m + 1)
                        nc.vector.tensor_tensor(w_lo[:, halves[m], :], w_raw[:, halves[m], :],
                                                w_hi[:, halves[m], :].bitcast(F32), ALU.subtract).then_inc(wlo_ok, 1)
                if there(n, TT):
                    v_.wait_ge(zhi_ok, n + 1)
                    nc.vector.tensor_tensor(z_lo[:, t, :, :], row_halves(tz[t][:, :], CK), z_hi[:, t, :, :].bitcast(F32),
                                            ALU.subtract).then_inc(zlo_ok, 1)
                if first:
                    nc.vector.tensor_scalar(v_step[:, :], v_step[:, :], 1.0 / QMAX, Q_FLOOR, ALU.mult,
                                            ALU.max).then_inc(dve, 1)
                    v_.wait_ge(dve, 1)
                    nc.vector.reciprocal(v_rstep[:, :], v_step[:, :]).then_inc(v_rstep_ok, 1)

            v_.wait_ge(b_in, 16)
            tiles(v_, step_of)

        @block.tensor
        def _(pe):
            def step_of(t, n):
                if there(n, TT):
                    pe.wait_ge(z_ok, n + 1)
                    if at_least(n, 2):
                        pe.wait_ge(zlo_ok, n - 1)
                    for k in range(CK):
                        ins = nc.tensor.transpose(tz[t][:, k * P:(k + 1) * P], z[:, t, k * P:(k + 1) * P], ident[:, :])
                    ins.then_inc(zT_ok, 1)
                if there(n - 3, TT):
                    pe.wait_ge(q3_ok, n - 2)
                    if at_least(n, 5):
                        pe.wait_ge(tq_read, n - 4)
                    for h in range(H):
                        ins = nc.tensor.transpose(tq[1 - t][:, h, :], q3[:, 1 - t, h, :, :].rearrange("p a d -> p (a d)"),
                                                  ident_bf[:, :])
                    ins.then_inc(tq_ok, 1)
                if there(n - 1, TT):
                    pe.wait_ge(zlo_ok, n)
                    if at_least(n, 3):
                        pe.wait_ge(qf_ok, n - 2)
                    for k in range(CK):
                        if isinstance(n, int) and n == 1 and k % (CK // 2) == 0:
                            pe.wait_ge(wlo_ok, k // (CK // 2) + 1)
                        for j, (a, w) in enumerate(((z_hi, w_hi), (z_lo, w_hi), (z_hi, w_lo))):
                            ins = nc.tensor.matmul(pq[1 - t][:, :], a[:, 1 - t, k, :], w[:, k, :],
                                                   start=(k == 0 and j == 0), stop=(k == CK - 1 and j == 2))
                    ins.then_inc(pq_ok, 1)
            tiles(pe, step_of)


def cross_scores(nc, k_parts, v_int, q_int, q_step, q_nstep, o_raw, z_sum, wp_dram, bp_dram, wp, ident16):
    with ExitStack() as ctx:
        def sb(name, shape, dt):
            return ctx.enter_context(nc.sbuf_tensor(name, shape, dt))

        def psum(name, shape, dt):
            return ctx.enter_context(nc.psum_tensor(name, shape, dt))

        def sem(name):
            return ctx.enter_context(nc.semaphore("cs_" + name))

        p_int = sb("cs_p_int", [P, 2, KEYS], I16)
        pT = sb("cs_pT", [P, 2, KT, P], BF16)
        top = sb("cs_top", [P, 2, 3], F32)
        top1 = sb("cs_top1", [P, 2], F32)
        step_now = sb("cs_step_now", [P, H], F32)
        nstep_now = sb("cs_nstep_now", [P, H], F32)
        z_now = sb("cs_z_now", [P, H, 2], F32)
        bias = sb("cs_bias", [P, 2], F32)
        s_a = [psum(f"cs_s_a{i}", [P, HALF], F32) for i in range(2)]
        s_b = psum("cs_s_b", [P, HALF], F32)
        tp = psum("cs_tp", [P, HKT, P], F16)
        out = psum("cs_out0", [P, C], F32)

        sa_ok = sem("sa_ok")
        sb_ok = sem("sb_ok")
        bias_ok = sem("bias_ok")
        ea_ok = sem("ea_ok")
        eb_ok = sem("eb_ok")
        ta_ok = sem("ta_ok")
        tb_ok = sem("tb_ok")
        ra_ok = sem("ra_ok")
        rb_ok = sem("rb_ok")
        av_ok = sem("av_ok")
        out_read = sem("out_read")
        max_ok = sem("max_ok")
        top_ok = sem("top_ok")
        act_tile = sem("act_tile")
        dve_tile = sem("dve_tile")
        w_in = sem("w_in")
        whi_ok = sem("whi_ok")
        wlo_ok = sem("wlo_ok")
        block = ctx.enter_context(nc.Block(no_gpsimd_drain=True))
        UNITS = TT * H

        def units(engine, step):
            for h in range(H - 1):
                step(0, h, h)
            with engine.Fori(0, TT - 1) as t:
                step(t, H - 1, t * H + H - 1)
                for h in range(H - 1):
                    step(t + 1, h, t * H + H + h)
            step(TT - 1, H - 1, UNITS - 1)
            for n in range(UNITS, UNITS + 2):
                step(TT, n - UNITS, n)

        def exists(n):
            return not isinstance(n, int) or 0 <= n < UNITS

        w_raw, w_hi, w_lo, bias_p = wp

        @block.sync
        def _(sp):
            sp.dma_start(w_raw, wp_dram.rearrange("(k p) n -> p k n", p=P)).then_inc(w_in, 16)
            sp.dma_start(bias_p[:, :], bp_dram.partition_broadcast(P)).then_inc(w_in, 16)

        @block.gpsimd
        def _(pool):
            pool.wait_ge(w_in, 32)
            nc.gpsimd.tensor_copy(w_hi[:, :, :], w_raw).then_inc(whi_ok, 1)
            pool.wait_ge(whi_ok, 1)
            nc.gpsimd.tensor_tensor(w_lo[:, :, :], w_raw, w_hi[:, :, :].bitcast(F32), ALU.subtract).then_inc(wlo_ok, 1)
            pool.wait_ge(wlo_ok, 1)

        @block.scalar
        def _(act):
            def keep_sums(t, n):
                act.wait_ge(ea_ok, n)
                nc.scalar.copy(z_sum[:, t, :, :], z_now[:, :, :]).then_inc(act_tile, 1)
                act.wait_ge(act_tile, 2 * t + 2)

            def step(t, h, n):
                if not exists(n):
                    return
                u = h % 2
                if h == 0:
                    if at_least(n, H):
                        keep_sums(t - 1, n)
                    nc.scalar.copy(step_now[:, :], q_step[:, t, :]).then_inc(act_tile, 1)
                    act.wait_ge(act_tile, 2 * t + 1)
                for half, s, made, used in ((1, s_b, eb_ok, tb_ok), (0, s_a[u], ea_ok, ta_ok)):
                    if half:
                        act.wait_ge(bias_ok, n + 1)
                    if at_least(n, 2):
                        act.wait_ge(used, n - 1)
                    nc.scalar.activation(p_int[:, u, half * HALF:(half + 1) * HALF], s[:, :], ACT.Exp,
                                         bias=bias[:, u:u + 1], scale=step_now[:, h:h + 1],
                                         accum_out=z_now[:, h, half:half + 1]).then_inc(made, 1)
                act.wait_ge(tb_ok, n + 1)
                if at_least(n, 2):
                    act.wait_ge(av_ok, n - 1)
                nc.scalar.copy(pT[:, u, HKT:KT, :], tp[:, :, :].bitcast(I16)).then_inc(rb_ok, 1)
            units(act, step)
            keep_sums(TT - 1, UNITS)

        @block.vector
        def _(v_):
            def max_a(u, n):
                v_.wait_ge(sa_ok, n + 1)
                nc.vector.tensor_reduce(top[:, u, 0:1], s_a[u][:, :], AX_X, ALU.max).then_inc(max_ok, 1)

            def step(t, h, n):
                u = h % 2
                if exists(n):
                    if h == 0:
                        if at_least(n, H):
                            v_.wait_ge(bias_ok, n)
                        nc.vector.tensor_copy(nstep_now[:, :], q_nstep[:, t, :]).then_inc(dve_tile, 1)
                        v_.wait_ge(dve_tile, t + 1)
                    for c in range(2):
                        v_.wait_ge(sb_ok, 2 * n + c + 1)
                        nc.vector.tensor_reduce(top[:, u, 1 + c:2 + c], s_b[:, c * 512:(c + 1) * 512], AX_X,
                                                ALU.max).then_inc(max_ok, 1)
                    v_.wait_ge(max_ok, 3 * n + 3)
                    nc.vector.tensor_reduce(top1[:, u:u + 1], top[:, u, :], AX_X, ALU.max).then_inc(top_ok, 1)
                    v_.wait_ge(top_ok, n + 1)
                    if at_least(n, 2):
                        v_.wait_ge(ea_ok, n - 1)
                    nc.vector.tensor_scalar(bias[:, u:u + 1], top1[:, u:u + 1], nstep_now[:, h:h + 1], LN_PMAX,
                                            ALU.mult, ALU.add).then_inc(bias_ok, 1)
                if exists(n + 1):
                    max_a(1 - u, n + 1)
                if at_least(n, 1) and exists(n - 1):
                    v_.wait_ge(ta_ok, n)
                    if at_least(n, 3):
                        v_.wait_ge(av_ok, n - 2)
                    nc.vector.tensor_copy(pT[:, 1 - u, 0:HKT, :], tp[:, :, :].bitcast(I16)).then_inc(ra_ok, 1)
                if h == 1 and at_least(n, H):
                    v_.wait_ge(av_ok, n - 1)
                    nc.vector.tensor_copy(o_raw[:, t - 1, :], out[:, :]).then_inc(out_read, 1)

            max_a(0, 0)
            units(v_, step)

        @block.tensor
        def _(pe):
            def scores(t, h, s, half, made, each_bank=False):
                for c in range(2):
                    keys = half * HALF + c * 512
                    ins = nc.tensor.matmul(s[:, c * 512:(c + 1) * 512], q_int[0:3 * D, t, h, :],
                                           k_parts[0:3 * D, h, keys:keys + 512], start=True, stop=True)
                    if each_bank or c == 1:
                        ins.then_inc(made, 1)

            def transposes(u, half, made):
                for k in range(HKT):
                    key = (half * HKT + k) * P
                    ins = nc.tensor.transpose(tp[:, k, :], p_int[:, u, key:key + P].bitcast(F16), ident16[:, :])
                ins.then_inc(made, 1)

            def step(t, h, n):
                u = h % 2
                before = at_least(n, 1) and exists(n - 1)
                if exists(n):
                    if at_least(n, 1):
                        pe.wait_ge(eb_ok, n)
                    scores(t, h, s_b, 1, sb_ok, each_bank=True)
                if before:
                    pe.wait_ge(eb_ok, n)
                    if at_least(n, 2):
                        pe.wait_ge(ra_ok, n - 1)
                    transposes(1 - u, 1, tb_ok)
                if exists(n + 1):
                    if at_least(n, 1):
                        pe.wait_ge(ea_ok, n)
                    scores(t + (h + 1) // H, (h + 1) % H, s_a[1 - u], 0, sa_ok)
                if at_least(n, 2):
                    head = (h - 2) % H
                    pe.wait_ge(ra_ok, n - 1)
                    pe.wait_ge(rb_ok, n - 1)
                    if head == 0 and at_least(n, H):
                        pe.wait_ge(out_read, t)
                    for k in range(KT):
                        ins = nc.tensor.matmul(out[:, head * D:(head + 1) * D], pT[:, u, k, :],
                                               v_int[:, k, head * D:(head + 1) * D], start=(k == 0), stop=(k == KT - 1))
                    ins.then_inc(av_ok, 1)
                if before:
                    pe.wait_ge(ea_ok, n)
                    pe.wait_ge(rb_ok, n)
                    transposes(1 - u, 0, ta_ok)

            scores(0, 0, s_a[0], 0, sa_ok)
            units(pe, step)


def cross_output(nc, x_res, mv, rstd, o_raw, z_sum, v_step, w_hi, w_lo, bias, ident, minus_half):
    with ExitStack() as ctx:
        def sb(name, shape, dt):
            return ctx.enter_context(nc.sbuf_tensor(name, shape, dt))

        def psum(name, shape, dt):
            return ctx.enter_context(nc.psum_tensor(name, shape, dt))

        def sem(name):
            return ctx.enter_context(nc.semaphore("co_" + name))

        p_step = sb("co_p_step", [P, TT, H], F32)
        stats = sb("co_stats", [P, TT, 6], F32)
        ve = sb("co_ve", [P, TT], F32)
        o = sb("co_o", [P, 2, H, D], F32)
        o_hi = sb("co_o_hi", [P, 2, CK, P], F32R)
        o_lo = sb("co_o_lo", [P, 2, CK, P], F32R)
        to = [psum(f"co_to{i}", [P, C], F32) for i in range(2)]
        po = [psum(f"co_po{i}", [P, C], F32) for i in range(2)]
        o1_ok = sem("o1_ok")
        o_ok = sem("o_ok")
        oT_ok = sem("oT_ok")
        ohi_ok = sem("ohi_ok")
        olo_ok = sem("olo_ok")
        xb_ok = sem("xb_ok")
        y_ok = sem("y_ok")
        y_read = sem("y_read")
        stats_ok = sem("stats_ok")
        ve_ok = sem("ve_ok")
        rstd_ok = sem("rstd_ok")
        dve = sem("dve")
        block = ctx.enter_context(nc.Block(no_gpsimd_drain=True))

        def tiles(step_of):
            for n in range(TT + 2):
                step_of(n, n % 2)

        @block.scalar
        def _(act):
            def step_of(n, t):
                if n < TT:
                    act.wait_ge(oT_ok, n + 1)
                    if n >= 2:
                        act.wait_ge(y_ok, n - 1)
                    nc.scalar.copy(o_hi[:, t, :, :], row_halves(to[t][:, :], CK)).then_inc(ohi_ok, 1)
            tiles(step_of)

        @block.gpsimd
        def _(pool):
            def step_of(n, t):
                if n < TT:
                    pool.wait_ge(o1_ok, n + 1)
                    flat = o[:, t, :, :].rearrange("p h d -> p (h d)")
                    nc.gpsimd.tensor_tensor(flat, flat, v_step[:, :], ALU.mult).then_inc(o_ok, 1)
                    nc.gpsimd.tensor_tensor(x_res[:, n, :], x_res[:, n, :], bias[:, :], ALU.add).then_inc(xb_ok, 1)
            tiles(step_of)
            pool.wait_ge(ve_ok, 1)
            nc.gpsimd.tensor_tensor(rstd[:, :], ve[:, :], minus_half[:, 0:TT], ALU.pow).then_inc(rstd_ok, 1)
            pool.wait_ge(rstd_ok, 1)

        @block.vector
        def _(v_):
            nc.vector.tensor_reduce(p_step[:, :, :], z_sum[:, :, :, :], AX_X, ALU.add).then_inc(dve, 1)
            v_.wait_ge(dve, 1)
            nc.vector.reciprocal(p_step[:, :, :], p_step[:, :, :]).then_inc(dve, 1)
            v_.wait_ge(dve, 2)
            nc.vector.tensor_scalar(p_step[:, :, :], p_step[:, :, :], Q_FLOOR, None, ALU.max).then_inc(dve, 1)
            v_.wait_ge(dve, 3)

            def scale(n):
                if n >= 2:
                    v_.wait_ge(oT_ok, n - 1)
                nc.vector.tensor_tensor(o[:, n % 2, :, :], o_raw[:, n, :].rearrange("p (h d) -> p h d", h=H),
                                        p_step[:, n, :].unsqueeze(2).broadcast_to([P, H, D]), ALU.mult).then_inc(o1_ok, 1)

            def step_of(n, t):
                if n + 1 < TT:
                    scale(n + 1)
                if n < TT:
                    v_.wait_ge(ohi_ok, n + 1)
                    nc.vector.tensor_tensor(o_lo[:, t, :, :], row_halves(to[t][:, :], CK), o_hi[:, t, :, :].bitcast(F32),
                                            ALU.subtract).then_inc(olo_ok, 1)
                if n >= 2:
                    v_.wait_ge(y_ok, n - 1)
                    v_.wait_ge(xb_ok, n - 1)
                    nc.vector.tensor_tensor(x_res[:, n - 2, :], x_res[:, n - 2, :], po[t][:, :], ALU.add).then_inc(y_read, 1)
                    v_.wait_ge(y_read, n - 1)
                    nc.vector.bn_stats(stats[:, n - 2, :], x_res[:, n - 2, :]).then_inc(stats_ok, 1)
                    v_.wait_ge(stats_ok, n - 1)
                    nc.vector.bn_aggr(mv[:, n - 2, :], stats[:, n - 2, :]).then_inc(dve, 1)
            scale(0)
            tiles(step_of)
            v_.wait_ge(dve, 3 + TT)
            nc.vector.tensor_scalar(ve[:, :], mv[:, :, 1], LN_EPS, None, ALU.add).then_inc(ve_ok, 1)

        @block.tensor
        def _(pe):
            def step_of(n, t):
                if n < TT:
                    pe.wait_ge(o_ok, n + 1)
                    if n >= 2:
                        pe.wait_ge(olo_ok, n - 1)
                    for k in range(CK):
                        ins = nc.tensor.transpose(to[t][:, k * P:(k + 1) * P],
                                                  o[:, t, k * GH:(k + 1) * GH, :].rearrange("p h d -> p (h d)"), ident[:, :])
                    ins.then_inc(oT_ok, 1)
                if 1 <= n <= TT:
                    pe.wait_ge(olo_ok, n)
                    if n >= 3:
                        pe.wait_ge(y_read, n - 2)
                    for k in range(CK):
                        for j, (a, w) in enumerate(((o_hi, w_hi), (o_lo, w_hi), (o_hi, w_lo))):
                            ins = nc.tensor.matmul(po[1 - t][:, :], a[:, 1 - t, k, :], w[:, k, :],
                                                   start=(k == 0 and j == 0), stop=(k == CK - 1 and j == 2))
                    ins.then_inc(y_ok, 1)
            tiles(step_of)


def cross_attention(nc, wq, bq, ctxT, wkv_in, bkv, wp, bp, v_raw, x_res, mv, rstd, ident, minus_half, ident16, ident_bf):
    with ExitStack() as ctx:
        def sb(name, shape, dt):
            return ctx.enter_context(nc.sbuf_tensor(name, shape, dt))

        k_parts = sb("k_parts", [3 * D, H, KEYS], BF16)
        v_step = sb("v_step", [P, C], F32)
        v_int = sb("v_int", [P, KT, C], BF16)
        wq_raw = v_int[:, :, :].rearrange("p t c -> p (t c)")[:, 0:2 * CK * C].bitcast(F32)\
            .rearrange("p (k c) -> p k c", k=CK)
        wq_in = ctx.enter_context(nc.semaphore("wq_in"))
        context_keys_values(nc, ctxT, wkv_in, wq, wq_raw, wq_in, bkv, k_parts, v_raw, v_step, x_res, mv, rstd,
                            minus_half, ident_bf)
        q_step = sb("q_step", [P, TT, H], F32)
        q_nstep = sb("q_nstep", [P, TT, H], F32)
        q_int = sb("q_int", [3 * D, TT, H, P], BF16)
        cross_queries(nc, wq_raw, wq_in, bq, x_res, mv, rstd, q_int, q_step, q_nstep, v_raw, v_int, v_step,
                      ident, ident_bf)
        o_raw = v_raw[:, 0:TT, :]
        w_raw = v_raw[:, TT:TT + CK, :]
        w_hi = sb("wp_hi", [P, CK, C], F32R)
        w_lo = sb("wp_lo", [P, CK, C], F32R)
        bias = sb("bias_p", [P, C], F32)
        z_sum = sb("z_sum", [P, TT, H, 2], F32)
        cross_scores(nc, k_parts, v_int, q_int, q_step, q_nstep, o_raw, z_sum, wp, bp, (w_raw, w_hi, w_lo, bias), ident16)
        cross_output(nc, x_res, mv, rstd, o_raw, z_sum, v_step, w_hi, w_lo, bias, ident, minus_half)


E_N, I_W = 8, 352
ROUTED = E_N * I_W // P
SHARED_W = 2 * I_W
SHARED = -(-SHARED_W // P)
CHUNKS = SHARED + ROUTED
GROUP = 2
PAIR = 2 * GROUP
TURNS_F = CHUNKS // PAIR
HALF_T = TOKENS // 2
LO_ROW = 32


def feed_forward(nc, gate_dram, rank_dram, w_dram, sel_dram, out_dram, x_res, mv, rstd, ident):
    with ExitStack() as ctx:
        def sb(name, shape, dt):
            return ctx.enter_context(nc.sbuf_tensor(name, shape, dt))

        def psum(name, shape, dt):
            return ctx.enter_context(nc.psum_tensor(name, shape, dt))

        def sem(name):
            return ctx.enter_context(nc.semaphore("ff_" + name))

        zT_hi = sb("zT_hi", [P, CK, TOKENS], F32R)
        zT_lo = sb("zT_lo", [P, CK, TOKENS], F32R)
        comb = sb("comb", [2 * LO_ROW, TOKENS], F32R)
        g_raw = sb("ff_g_raw", [P, CK, E_N], F32)
        g_hi = sb("ff_g_hi", [P, CK, E_N], F32R)
        g_lo = sb("ff_g_lo", [P, CK, E_N], F32R)
        rank = sb("ff_rank", [P, TT, E_N], F32)
        z = sb("ff_z", [P, 2, C], F32)
        lgT = sb("ff_lgT", [E_N, TOKENS], F32)
        lg = sb("ff_lg", [P, TT, E_N], F32)
        prob = sb("ff_prob", [P, TT, E_N], F32)
        left = sb("ff_left", [P, TT, E_N], F32)
        hot = sb("ff_hot", [P, TT, E_N], F32)
        w = sb("ff_w", [P, TT, E_N], F32)
        one = sb("ff_one", [P, TT], F32)
        raw = sb("ff_raw", [P, PAIR, 3 * C], F32)
        up_hi = sb("ff_up_hi", [P, 2, 2, CK, P], F32R)
        up_lo = sb("ff_up_lo", [P, 2, 2, CK, P], F32R)
        dn_hi = sb("ff_dn_hi", [P, PAIR, C], F32R)
        dn_lo = sb("ff_dn_lo", [P, PAIR, C], F32R)
        h_hi = sb("ff_h_hi", [P, PAIR, TOKENS], F32R)
        h_lo = sb("ff_h_lo", [P, PAIR, TOKENS], F32R)
        act_s = sb("ff_s", [P, 2, HALF_T], F32)
        g = sb("ff_g", [P, 2, HALF_T], F32)
        sel_raw = sb("ff_sel_raw", [2 * LO_ROW, ROUTED * P], F32)
        sel = sb("ff_sel", [2 * LO_ROW, 2, P], F32R)
        h1 = [psum(f"ff_h1{i}", [P, HALF_T], F32) for i in range(2)]
        h2 = [psum(f"ff_h2{i}", [P, HALF_T], F32) for i in range(2)]
        pc = [psum(f"ff_pc{i}", [P, HALF_T], F32) for i in range(2)]
        py = [psum(f"ff_py{i}", [P, C], F32) for i in range(2)]

        tz = py
        pl = pc[0][:, 0:TT * E_N].rearrange("p (t e) -> p t e", t=TT)

        small_in = sem("small_in")
        ghi_ok = sem("ghi_ok")
        glo_ok = sem("glo_ok")
        z_ok = sem("z_ok")
        zT_ok = sem("zT_ok")
        zhi_ok = sem("zhi_ok")
        zlo_ok = sem("zlo_ok")
        lgT_ok = sem("lgT_ok")
        lgT_read = sem("lgT_read")
        lg_ok = sem("lg_ok")
        sub_ok = sem("sub_ok")
        exp_ok = sem("exp_ok")
        w_ok = sem("w_ok")
        tc_ok = sem("tc_ok")
        chi_ok = sem("chi_ok")
        zero_ok = sem("zero_ok")
        clo_ok = sem("clo_ok")
        dve = sem("dve")
        w_in = [sem(f"w_in{i}") for i in range(PAIR)]
        uhi_ok = sem("uhi_ok")
        ulo_ok = sem("ulo_ok")
        dhi_ok = sem("dhi_ok")
        dlo_ok = sem("dlo_ok")
        h1_ok = sem("h1_ok")
        h2_ok = sem("h2_ok")
        s_ok = sem("s_ok")
        g1_ok = sem("g1_ok")
        g_ok = sem("g_ok")
        hhi_ok = sem("hhi_ok")
        hlo_ok = sem("hlo_ok")
        y_ok = sem("y_ok")
        y_read = sem("y_read")
        stored = sem("stored")
        block = ctx.enter_context(nc.Block(no_gpsimd_drain=True))
        assert CHUNKS % PAIR == 0 and PAIR < SHARED <= 2 * PAIR

        def turns(engine, turn):
            turn(0, PAIR)
            turn(1, SHARED - PAIR)
            with engine.Fori(2, TURNS_F - 1) as p:
                turn(p, 0)
            turn(TURNS_F - 1, 0)

        def before(p, j, n):
            return not (isinstance(p, int) and PAIR * p + j < n)

        def last(p, j):
            return isinstance(p, int) and PAIR * p + j == CHUNKS - 1

        def has_weights(p, j):
            return not (isinstance(p, int) and PAIR * p + j < SHARED)

        @block.sync
        def _(sp):
            def turn(p, first_routed):
                for j in range(PAIR):
                    if before(p, j, PAIR):
                        sp.wait_ge(dlo_ok, PAIR * p + j + 1 - PAIR)
                    sp.dma_start(raw[:, j, :], w_dram[bass.ds(PAIR * p + j, 1), :, :].rearrange("a p n -> p (a n)"))\
                      .then_inc(w_in[j], 16)
                    if isinstance(p, int) and PAIR * p + j == 0:
                        sp.dma_start(g_raw[:, :, :], gate_dram.rearrange("(k p) e -> p k e", p=P)).then_inc(small_in, 16)
                        sp.dma_start(rank[:, :, :].rearrange("p t e -> p (t e)"),
                                     rank_dram.partition_broadcast(P)).then_inc(small_in, 16)
                        sp.dma_start(sel_raw[:, :], sel_dram).then_inc(small_in, 16)
            turns(sp, turn)
            for t in range(0, TT, 2):
                sp.wait_ge(y_read, TT * (2 * TURNS_F - 1) + t + 2)
                sp.dma_start(out_dram.rearrange("(t p) c -> p t c", p=P)[:, t:t + 2, :],
                             x_res[:, t:t + 2, :]).then_inc(stored, 16)
            sp.wait_ge(stored, 16 * (TT // 2))

        @block.scalar
        def _(act):
            def split_up(p, j):
                act.wait_ge(w_in[j], 16 * (p + 1))
                if before(p, j, 2):
                    act.wait_ge(h2_ok, 2 * (PAIR * p + j) - 2)
                if has_weights(p, j):
                    nc.scalar.copy(sel[:, j % 2, :], sel_raw[:, bass.ds((PAIR * p + j - SHARED) * P, P)])
                nc.scalar.copy(up_hi[:, j % 2, :, :, :].rearrange("p a k n -> p (a k n)"),
                               raw[:, j, 0:2 * C]).then_inc(uhi_ok, 1)

            def turn(p, first_routed):
                for j in range(PAIR):
                    c = PAIR * p + j
                    if isinstance(p, int) and c == 1:
                        for b in range(2):
                            act.wait_ge(lgT_ok, b + 1)
                            nc.scalar.copy(lgT[:, b * HALF_T:(b + 1) * HALF_T], pc[b][0:E_N, :]).then_inc(lgT_read, 1)
                    if isinstance(p, int) and c == 2:
                        act.wait_ge(sub_ok, 1)
                        nc.scalar.activation(lg[:, :, :], lg[:, :, :], ACT.Exp).then_inc(exp_ok, 1)
                    if isinstance(p, int) and c == SHARED - 1:
                        act.wait_ge(tc_ok, 1)
                        for b in range(2):
                            nc.scalar.copy(comb[0:E_N, b * HALF_T:(b + 1) * HALF_T], pc[b][0:E_N, :]).then_inc(chi_ok, 1)
                    if j + 1 < PAIR:
                        split_up(p, j + 1)
                    elif not last(p, j):
                        split_up(p + 1, 0)
                    for b in range(2):
                        act.wait_ge(h1_ok, 2 * c + b + 1)
                        nc.scalar.activation(act_s[:, b, :], h1[b][:, :], ACT.Silu).then_inc(s_ok, 1)
                        act.wait_ge(g_ok, 2 * c + b + 1)
                        if before(p, j, PAIR) and b == 0 and j % GROUP == 0:
                            act.wait_ge(y_ok, TT * (2 * p + j // GROUP - 1))
                        nc.scalar.copy(h_hi[:, j, b * HALF_T:(b + 1) * HALF_T], g[:, b, :]).then_inc(hhi_ok, 1)
                    nc.scalar.copy(dn_hi[:, j, :], raw[:, j, 2 * C:3 * C]).then_inc(dhi_ok, 1)

            for t in range(TT):
                act.wait_ge(zT_ok, t + 1)
                nc.scalar.copy(zT_hi[:, :, t * P:(t + 1) * P], row_halves(tz[t % 2][:, :], CK)).then_inc(zhi_ok, 1)
                if t == TT // 2:
                    split_up(0, 0)
            act.wait_ge(small_in, 48)
            nc.scalar.copy(g_hi[:, :, :], g_raw[:, :, :]).then_inc(ghi_ok, 1)
            turns(act, turn)

        @block.gpsimd
        def _(pool):
            def split_up(p, j):
                pool.wait_ge(uhi_ok, PAIR * p + j + 1)
                nc.gpsimd.tensor_tensor(up_lo[:, j % 2, :, :, :].rearrange("p a k n -> p (a k n)"), raw[:, j, 0:2 * C],
                                        up_hi[:, j % 2, :, :, :].rearrange("p a k n -> p (a k n)").bitcast(F32),
                                        ALU.subtract).then_inc(ulo_ok, 1)

            def turn(p, first_routed):
                for j in range(PAIR):
                    c = PAIR * p + j
                    if j + 1 < PAIR:
                        split_up(p, j + 1)
                    elif not last(p, j):
                        split_up(p + 1, 0)
                    for b in range(2):
                        pool.wait_ge(hhi_ok, 2 * c + b + 1)
                        nc.gpsimd.tensor_tensor(h_lo[:, j, b * HALF_T:(b + 1) * HALF_T], g[:, b, :],
                                                h_hi[:, j, b * HALF_T:(b + 1) * HALF_T].bitcast(F32),
                                                ALU.subtract).then_inc(hlo_ok, 1)
                    pool.wait_ge(dhi_ok, c + 1)
                    nc.gpsimd.tensor_tensor(dn_lo[:, j, :], raw[:, j, 2 * C:3 * C], dn_hi[:, j, :].bitcast(F32),
                                            ALU.subtract).then_inc(dlo_ok, 1)

            nc.gpsimd.memset(comb[:, :].bitcast(F32), 0.0).then_inc(zero_ok, 1)
            split_up(0, 0)
            turns(pool, turn)

        @block.vector
        def _(v_):
            links = [0]

            def link(ins):
                links[0] += 1
                ins.then_inc(dve, 1)
                v_.wait_ge(dve, links[0])


            def norm(t):
                if t >= 2:
                    v_.wait_ge(zT_ok, t - 1)
                nc.vector.tensor_scalar(z[:, t % 2, :], x_res[:, t, :], mv[:, t, 0:1], rstd[:, t:t + 1],
                                        ALU.subtract, ALU.mult).then_inc(z_ok, 1)
            norm(0)
            for t in range(TT):
                if t + 1 < TT:
                    norm(t + 1)
                v_.wait_ge(zhi_ok, t + 1)
                nc.vector.tensor_tensor(zT_lo[:, :, t * P:(t + 1) * P], row_halves(tz[t % 2][:, :], CK),
                                        zT_hi[:, :, t * P:(t + 1) * P].bitcast(F32), ALU.subtract).then_inc(zlo_ok, 1)

            def across(x):
                return x[:, :].unsqueeze(2).broadcast_to([P, TT, E_N])

            def route(stage):
                if stage == 0:
                    v_.wait_ge(lg_ok, 1)
                    link(nc.vector.tensor_reduce(one[:, :], pl[:, :, :], AX_X, ALU.max))
                    nc.vector.tensor_tensor(lg[:, :, :], pl[:, :, :], across(one), ALU.subtract).then_inc(sub_ok, 1)
                if stage == 1:
                    v_.wait_ge(exp_ok, 1)
                    link(nc.vector.tensor_reduce(one[:, :], lg[:, :, :], AX_X, ALU.add))
                    link(nc.vector.reciprocal(one[:, :], one[:, :]))
                    link(nc.vector.tensor_tensor(prob[:, :, :], lg[:, :, :], across(one), ALU.mult))
                    link(nc.vector.tensor_copy(left[:, :, :], prob[:, :, :]))
                    v_.wait_ge(small_in, 48)
                if stage in (2, 3):
                    link(nc.vector.tensor_reduce(one[:, :], left[:, :, :], AX_X, ALU.max))
                    link(nc.vector.tensor_tensor(hot[:, :, :], left[:, :, :], across(one), ALU.is_equal))
                    link(nc.vector.tensor_tensor(hot[:, :, :], hot[:, :, :], rank[:, :, :], ALU.mult))
                    link(nc.vector.tensor_reduce(one[:, :], hot[:, :, :], AX_X, ALU.max))
                    link(nc.vector.tensor_tensor(hot[:, :, :], hot[:, :, :], across(one), ALU.is_equal))
                    link(nc.vector.scalar_tensor_tensor(out=left[:, :, :], in0=hot[:, :, :], scalar=-2.0,
                                                        in1=left[:, :, :], op0=ALU.mult, op1=ALU.add))
                if stage == 3:
                    link(nc.vector.tensor_scalar(hot[:, :, :], left[:, :, :], -0.5, None, ALU.is_lt))
                    nc.vector.tensor_tensor(w[:, :, :], hot[:, :, :], prob[:, :, :], ALU.mult).then_inc(w_ok, 1)

            def low_weights():
                v_.wait_ge(chi_ok, 2)
                for b in range(2):
                    cols = slice(b * HALF_T, (b + 1) * HALF_T)
                    nc.vector.tensor_tensor(comb[LO_ROW:LO_ROW + E_N, cols], pc[b][0:E_N, :],
                                            comb[0:E_N, cols].bitcast(F32), ALU.subtract).then_inc(clo_ok, 1)

            def add_y(group):
                for t in range(TT):
                    v_.wait_ge(y_ok, TT * group + t + 1)
                    nc.vector.tensor_tensor(x_res[:, t, :], x_res[:, t, :], py[t % 2][:, :], ALU.add).then_inc(y_read, 1)

            def turn(p, first_routed):
                for j in range(PAIR):
                    c = PAIR * p + j
                    if isinstance(p, int) and c == SHARED - 1:
                        low_weights()
                    for b in range(2):
                        v_.wait_ge(s_ok, 2 * c + b + 1)
                        v_.wait_ge(h2_ok, 2 * c + b + 1)
                        if before(p, j, 1):
                            v_.wait_ge(hlo_ok, 2 * c + b - 1)
                        ins = nc.vector.tensor_tensor(g[:, b, :], act_s[:, b, :], h2[b][:, :], ALU.mult)
                        if j >= first_routed:
                            ins.then_inc(g1_ok, 1)
                            v_.wait_ge(g1_ok, 2 * (c - SHARED) + b + 1)
                            ins = nc.vector.tensor_tensor(g[:, b, :], g[:, b, :], pc[b][:, :], ALU.mult)
                        ins.then_inc(g_ok, 1)
                    if isinstance(p, int) and p == 0:
                        for stage in ((), (0,), (1, 2), (3,))[j]:
                            route(stage)
                    if j == GROUP - 1 and before(p, j, PAIR):
                        add_y(2 * p - 1)
                    if j == PAIR - 1:
                        add_y(2 * p)
            v_.wait_ge(ghi_ok, 1)
            nc.vector.tensor_tensor(g_lo[:, :, :], g_raw[:, :, :], g_hi[:, :, :].bitcast(F32),
                                    ALU.subtract).then_inc(glo_ok, 1)
            turns(v_, turn)
            add_y(2 * TURNS_F - 1)

        @block.tensor
        def _(pe):
            def gate():
                pe.wait_ge(glo_ok, 1)
                for b in range(2):
                    for k in range(CK):
                        for i, (g, zz) in enumerate(((g_hi, zT_hi), (g_lo, zT_hi), (g_hi, zT_lo))):
                            ins = nc.tensor.matmul(pc[b][0:E_N, :], g[:, k, :], zz[:, k, b * HALF_T:(b + 1) * HALF_T],
                                                   start=(k == 0 and i == 0), stop=(k == CK - 1 and i == 2))
                    ins.then_inc(lgT_ok, 1)

            def turn_logits():
                pe.wait_ge(lgT_read, 2)
                for t in range(TT):
                    ins = nc.tensor.transpose(pl[:, t, :], lgT[:, t * P:(t + 1) * P], ident[0:E_N, 0:E_N])
                ins.then_inc(lg_ok, 1)

            for t in range(TT):
                pe.wait_ge(z_ok, t + 1)
                if t >= 2:
                    pe.wait_ge(zlo_ok, t - 1)
                for k in range(CK):
                    ins = nc.tensor.transpose(tz[t % 2][:, k * P:(k + 1) * P], z[:, t % 2, k * P:(k + 1) * P], ident[:, :])
                ins.then_inc(zT_ok, 1)

            def hidden(p, j, routed):
                c = PAIR * p + j
                pe.wait_ge(ulo_ok, c + 1)
                for b in range(2):
                    if isinstance(p, int) and c == 0:
                        pe.wait_ge(zlo_ok, (b + 1) * TT // 2)
                    if before(p, j, 1):
                        pe.wait_ge(g_ok, 2 * c + b - 1)
                    cols = slice(b * HALF_T, (b + 1) * HALF_T)
                    for m, (out, made) in enumerate(((h1, h1_ok), (h2, h2_ok))):
                        if m and routed:
                            nc.tensor.matmul(pc[b][:, :], sel[:, j % 2, :], comb[:, cols], start=True, stop=True)
                        for k in range(CK):
                            for i, (w, zz) in enumerate(((up_hi, zT_hi), (up_lo, zT_hi), (up_hi, zT_lo))):
                                ins = nc.tensor.matmul(out[b][:, :], w[:, j % 2, m, k, :], zz[:, k, cols],
                                                       start=(k == 0 and i == 0), stop=(k == CK - 1 and i == 2))
                        ins.then_inc(made, 1)

            def down(group, u):
                pe.wait_ge(hlo_ok, 2 * GROUP * (group + 1))
                pe.wait_ge(dlo_ok, GROUP * (group + 1))
                for t in range(TT):
                    if not (isinstance(group, int) and group == 0 and t < 2):
                        pe.wait_ge(y_read, TT * group + t - 1)
                    for q in range(GROUP):
                        j = u * GROUP + q
                        tile = slice(t * P, (t + 1) * P)
                        for i, (hh, w) in enumerate(((h_hi, dn_hi), (h_lo, dn_hi), (h_hi, dn_lo))):
                            ins = nc.tensor.matmul(py[t % 2][:, :], hh[:, j, tile], w[:, j, :],
                                                   start=(q == 0 and i == 0), stop=(q == GROUP - 1 and i == 2))
                    ins.then_inc(y_ok, 1)

            def turn_weights():
                pe.wait_ge(w_ok, 1)
                for t in range(TT):
                    ins = nc.tensor.transpose(pc[t // (TT // 2)][0:E_N, t % (TT // 2) * P:(t % (TT // 2) + 1) * P],
                                              w[:, t, :], ident[:, :])
                ins.then_inc(tc_ok, 1)

            def turn(p, first_routed):
                for j in range(PAIR):
                    if isinstance(p, int) and PAIR * p + j == SHARED:
                        pe.wait_ge(clo_ok, 2)
                        pe.wait_ge(zero_ok, 1)
                    hidden(p, j, j >= first_routed)
                    if isinstance(p, int) and p == 0:
                        if j == 0:
                            gate()
                        if j == 1:
                            turn_logits()
                    if isinstance(p, int) and PAIR * p + j == SHARED - 2:
                        turn_weights()
                    if j == GROUP - 1 and before(p, j, PAIR):
                        down(2 * p - 1, 1)
                    if j == PAIR - 1:
                        down(2 * p, 0)
            turns(pe, turn)
            down(2 * TURNS_F - 1, 1)


def decoder_layer(nc, x, ctxT, wq, wk, wv, wo, gamma, beta, cwq, cbq, cwkv, cbkv, cwp, cbp,
                  gate, rank, weights, sel, out):
    with ExitStack() as ctx:
        x_res, (ident, mask, minus_half, ident16, ident_bf) = constants(nc, ctx)
        mv = ctx.enter_context(nc.sbuf_tensor("mv", [P, TT, 2], F32))
        rstd = ctx.enter_context(nc.sbuf_tensor("rstd", [P, TT], F32))
        wkv_in = [ctx.enter_context(nc.semaphore(f"wkv_in{m}")) for m in range(2)]
        with nc.sbuf_tensor("stage", [P, KT, C], F32) as stage:
            self_attention(nc, x, (wq, wk, wv, wo), gamma, beta, cwkv, wkv_in, stage, x_res, ident, mask, minus_half)
            cross_attention(nc, cwq, cbq, ctxT, wkv_in, cbkv, cwp, cbp, stage, x_res, mv, rstd,
                            ident, minus_half, ident16, ident_bf)
        feed_forward(nc, gate, rank, weights, sel, out, x_res, mv, rstd, ident)


def _arrays(inputs):
    import numpy as np

    def f(name):
        return np.asarray(inputs[name])

    a = {
        "x": f("x").reshape(TOKENS, C),
        "ctxT": f("ctx_2048").reshape(KEYS, C).T,
        "wq": f("L0_attn_Wq").T, "wk": f("L0_attn_Wk").T, "wv": f("L0_attn_Wv").T, "wo": f("L0_attn_Wo").T,
        "gamma": np.tile(f("L0_attn_gamma"), H)[None], "beta": np.tile(f("L0_attn_beta"), H)[None],
        "cwq": f("L0_xattn_Wq"), "cbq": f("L0_xattn_bq")[None],
        "cwkv": f("L0_xattn_Wkv"), "cbkv": f("L0_xattn_bkv")[None],
        "cwp": f("L0_xattn_Wp"), "cbp": f("L0_xattn_bp")[None],
        "gate": f("L0_ffn_gate_w").T,
        "rank": np.tile(np.arange(E_N, 0, -1, dtype=np.float32), TT)[None],
    }
    pad = np.zeros((SHARED * P - SHARED_W, C), np.float32)

    def rows(routed, shared):
        return np.concatenate([shared, pad, routed]).reshape(CHUNKS, P, C)

    up = [rows(f(f"L0_ffn_{r}").reshape(-1, C), f(f"L0_ffn_{s}")).reshape(CHUNKS, P, CK, P).transpose(0, 3, 2, 1)
          .reshape(CHUNKS, P, C) for r, s in (("w1", "sw1"), ("w2", "sw2"))]
    down = rows(f("L0_ffn_w3").transpose(0, 2, 1).reshape(-1, C), f("L0_ffn_sw3").T)
    a["weights"] = np.concatenate([*up, down], axis=2)
    one_hot = (np.arange(ROUTED * P)[None] // I_W == np.arange(E_N)[:, None]).astype(np.float32)
    a["sel"] = np.zeros((2 * LO_ROW, ROUTED * P), np.float32)
    a["sel"][0:E_N] = one_hot
    a["sel"][LO_ROW:LO_ROW + E_N] = one_hot
    return {n: np.ascontiguousarray(v) for n, v in a.items()}


def kernel(**inputs):
    import numpy as _np
    import concourse.bacc as _bacc
    from concourse.bass_utils import run_bass_kernel_spmd as _run

    nc = _bacc.Bacc("TRN2", target_bir_lowering=False, num_devices=1)
    arrays, args = {}, []
    for name, a in _arrays(inputs).items():
        arrays[f"in_{name}_dram"] = a
        args.append(nc.dram_tensor(f"in_{name}_dram", a.shape, mybir.dt.from_np(a.dtype), kind="ExternalInput").ap())
    args.append(nc.dram_tensor("out_dram", (TOKENS, C), F32, kind="ExternalOutput").ap())
    decoder_layer(nc, *args)
    r = _run(nc, [arrays], core_ids=[0])
    return r.results[0]["out_dram"].reshape(B, S, C)
```
